# Optimizing a Trainium2 kernel written in Bass

```python
import numpy as np
import jax
import jax.numpy as jnp

def _softmax(x, axis=-1):
    return jax.nn.softmax(x, axis=axis)

def _gelu(x):
    return jax.nn.gelu(x, approximate=True)

def _silu(x):
    return jax.nn.silu(x)

def _sigmoid(x):
    return jax.nn.sigmoid(x)

def _layernorm(x, axis=-1, eps=1e-05):
    m = jnp.mean(x, axis=axis, keepdims=True)
    v = jnp.var(x, axis=axis, keepdims=True)
    return (x - m) / jnp.sqrt(v + eps)

def _scatter_add(tgt, idx, src, axis=0):
    return tgt.at[idx].add(src)

def _segment_sum(src, seg, n):
    return jax.ops.segment_sum(src, seg, n)
kernel_name = 'mk_cond_seq_d2_seqx_r4_1e7ce3'

def setup_inputs(seed: int=0):
    np.random.seed(seed)
    _w = jnp.asarray

    def _rec_inputs():
        import jax
        import jax.numpy as jnp
        _rk = jax.random.key(seed)
        x = 1.648e-05 + 1 * jax.random.normal(jax.random.fold_in(_rk, 1), (8, 256, 256), jnp.float32)
        _lenS = 256 - jax.random.randint(jax.random.fold_in(_rk, 7), (8,), 0, max(1, 256 // 4) + 1, jnp.int32)
        _lenS2 = 256 - jax.random.randint(jax.random.fold_in(_rk, 8), (8,), 0, max(1, 256 // 4) + 1, jnp.int32)
        cond_1024 = 0.00191187 + 0.999416 * jax.random.normal(jax.random.fold_in(_rk, 11), (8, 256), jnp.float32)
        _validS = jnp.arange(256)[None, :] < _lenS[:, None]
        _validS2 = jnp.arange(256)[None, :] < _lenS2[:, None]
        _causal = jnp.tril(jnp.ones((256, 256), dtype=bool))
        mask_BxSxSx11_ik0 = jnp.where(jnp.ones((8, 256, 256, 11), dtype=bool), 0, 1).astype(jnp.int32)
        return (x, cond_1024, mask_BxSxSx11_ik0)
    x, cond_1024, mask_BxSxSx11_ik0 = _rec_inputs()

    def _L0_cond_setup():
        import jax, jax.numpy as jnp
        import numpy as np
        NONGT = 20
        H = 16
        NEG = -9000000000000000.0

        def _gat_attention(self_feat, cond_adj, label_bias, Wq, bq, Wk, bk, Wout, bout):
            B, N, F = self_feat.shape
            ng = min(NONGT, N)
            dh = F // H
            kv = self_feat[:, :ng]
            qh = (self_feat @ Wq.T + bq).reshape(B, N, H, dh)
            kh = (kv @ Wk.T + bk).reshape(B, ng, H, dh)
            aff = jnp.einsum('bnhd,bmhd->bnhm', qh, kh) * (1.0 / np.sqrt(dh))
            mask = cond_adj[:, :, None, :] > 0
            aff = jnp.where(mask, aff, NEG) + label_bias[:, :, None, :]
            w = jax.nn.softmax(aff, axis=-1)
            out_t = jnp.einsum('bnhm,bmf->bnhf', w, kv)
            out = jnp.einsum('bnhf,hgf->bnhg', out_t, Wout) + bout.reshape(H, F // H)
            return out.reshape(B, N, F)

        def _forward(v, q, adj, W_self, b_self, w_bias, b_bias, Wq, bq, Wk, bk, Wout, bout):
            adj_f = adj.astype(jnp.float32)
            exp_v = v
            row_zero = exp_v.sum(-1) == 0
            q_exp = jnp.where(row_zero[..., None], 0.0, q[:, None, :])
            vcq = jnp.concatenate([exp_v, q_exp], axis=-1)
            self_feat = vcq @ W_self.T + b_self
            output = self_feat
            for d in range(2):
                A = adj_f if d == 0 else jnp.swapaxes(adj_f, 1, 2)
                A = A[:, :, :NONGT, :]
                cond = A.sum(-1)
                vb = A @ w_bias + b_bias
                output = output + _gat_attention(self_feat, cond, vb, Wq[d], bq[d], Wk[d], bk[d], Wout[d], bout[d])
            rel = jax.nn.relu(output)
            return exp_v + rel
        key = jax.random.key(seed)
        ks = jax.random.split(key, 8)
        B, N, L, F, Q = (64, 36, 11, 256, 256)
        IN = F + Q
        s = 0.02
        return {'v': jax.random.normal(ks[0], (B, N, F), jnp.float32), 'q': jax.random.normal(ks[1], (B, Q), jnp.float32), 'adj': jax.random.randint(ks[2], (B, N, N, L), 0, 2, jnp.int32), 'W_self': jax.random.normal(ks[3], (F, IN), jnp.float32) * s, 'b_self': jnp.zeros((F,), jnp.float32), 'w_bias': jax.random.normal(ks[4], (L,), jnp.float32) * s, 'b_bias': jnp.zeros((), jnp.float32), 'Wq': jax.random.normal(ks[5], (2, F, F), jnp.float32) * s, 'bq': jnp.zeros((2, F), jnp.float32), 'Wk': jax.random.normal(ks[6], (2, F, F), jnp.float32) * s, 'bk': jnp.zeros((2, F), jnp.float32), 'Wout': jax.random.normal(ks[7], (2, H, F // H, F), jnp.float32) * s, 'bout': jnp.zeros((2, F), jnp.float32)}
    _L0_cond_all = _L0_cond_setup()
    _L0_cond_in = {k: v for k, v in _L0_cond_all.items() if k in ('W_self', 'b_self', 'w_bias', 'b_bias', 'Wq', 'bq', 'Wk', 'bk', 'Wout', 'bout')}
    del _L0_cond_all

    def _L1_cond_setup():
        import jax, jax.numpy as jnp
        import numpy as np
        B, L, D, P = (8, 512, 256, 64)

        def _ln(x):
            m = x.mean(-1, keepdims=True)
            v = x.var(-1, keepdims=True)
            return (x - m) * jax.lax.rsqrt(v + 1e-05)

        def _s5(u, Lam_re, Lam_im, B_re, B_im, C_re, C_im, D_diag, log_step):
            Lam = Lam_re + 1j * Lam_im
            dt = jnp.exp(log_step)
            Lam_bar = jnp.exp(Lam * dt)
            Bc = B_re + 1j * B_im
            B_bar = ((Lam_bar - 1.0) / Lam)[:, None] * Bc
            Bu = jnp.einsum('bld,pd->blp', u.astype(B_bar.dtype), B_bar)
            A = jnp.broadcast_to(Lam_bar, Bu.shape)

            def binop(e1, e2):
                a1, b1 = e1
                a2, b2 = e2
                return (a1 * a2, a2 * b1 + b2)
            _, xs = jax.lax.associative_scan(binop, (A, Bu), axis=1)
            Cc = C_re + 1j * C_im
            return 2.0 * jnp.einsum('blp,dp->bld', xs, Cc).real + D_diag * u
        key = jax.random.key(seed)
        ks = jax.random.split(key, 16)
        inp = {'y': jax.random.normal(ks[0], (B, L, D), jnp.float32), 't': jax.random.normal(ks[1], (B, D), jnp.float32), 'Wm': jax.random.normal(ks[2], (D, 6 * D), jnp.float32) * 0.02, 'bm': jax.random.normal(ks[3], (6 * D,), jnp.float32) * 0.02, 'Lam_re': -0.5 * jnp.ones((P,), jnp.float32), 'Lam_im': jnp.pi * jnp.arange(P, dtype=jnp.float32), 'B_re': jax.random.normal(ks[4], (P, D), jnp.float32) / np.sqrt(D), 'B_im': jax.random.normal(ks[5], (P, D), jnp.float32) / np.sqrt(D), 'C_re': jax.random.normal(ks[6], (D, P), jnp.float32) / np.sqrt(P), 'C_im': jax.random.normal(ks[7], (D, P), jnp.float32) / np.sqrt(P), 'D_diag': jax.random.normal(ks[8], (D,), jnp.float32), 'log_step': jax.random.uniform(ks[9], (P,), jnp.float32, np.log(0.001), np.log(0.1)), 'Wc': jax.random.normal(ks[10], (D, 2 * D), jnp.float32) * 0.02, 'bc': jax.random.normal(ks[11], (2 * D,), jnp.float32) * 0.02, 'W1': jax.random.normal(ks[12], (D, 4 * D), jnp.float32) / np.sqrt(D), 'b1': jnp.zeros((4 * D,), jnp.float32), 'W2': jax.random.normal(ks[13], (4 * D, D), jnp.float32) / np.sqrt(4 * D) * 0.1, 'b2': jnp.zeros((D,), jnp.float32)}
        return inp
    _L1_cond_all = _L1_cond_setup()
    _L1_cond_in = {k: v for k, v in _L1_cond_all.items() if k in ('Wm', 'bm', 'Lam_re', 'Lam_im', 'B_re', 'B_im', 'C_re', 'C_im', 'D_diag', 'log_step', 'Wc', 'bc', 'W1', 'b1', 'W2', 'b2')}
    del _L1_cond_all
    return {'x': x, 'cond_1024': cond_1024, 'mask_BxSxSx11_ik0': mask_BxSxSx11_ik0, 'L0_cond_W_self': _L0_cond_in['W_self'], 'L0_cond_b_self': _L0_cond_in['b_self'], 'L0_cond_w_bias': _L0_cond_in['w_bias'], 'L0_cond_b_bias': _L0_cond_in['b_bias'], 'L0_cond_Wq': _L0_cond_in['Wq'], 'L0_cond_bq': _L0_cond_in['bq'], 'L0_cond_Wk': _L0_cond_in['Wk'], 'L0_cond_bk': _L0_cond_in['bk'], 'L0_cond_Wout': _L0_cond_in['Wout'], 'L0_cond_bout': _L0_cond_in['bout'], 'L1_cond_Wm': _L1_cond_in['Wm'], 'L1_cond_bm': _L1_cond_in['bm'], 'L1_cond_Lam_re': _L1_cond_in['Lam_re'], 'L1_cond_Lam_im': _L1_cond_in['Lam_im'], 'L1_cond_B_re': _L1_cond_in['B_re'], 'L1_cond_B_im': _L1_cond_in['B_im'], 'L1_cond_C_re': _L1_cond_in['C_re'], 'L1_cond_C_im': _L1_cond_in['C_im'], 'L1_cond_D_diag': _L1_cond_in['D_diag'], 'L1_cond_log_step': _L1_cond_in['log_step'], 'L1_cond_Wc': _L1_cond_in['Wc'], 'L1_cond_bc': _L1_cond_in['bc'], 'L1_cond_W1': _L1_cond_in['W1'], 'L1_cond_b1': _L1_cond_in['b1'], 'L1_cond_W2': _L1_cond_in['W2'], 'L1_cond_b2': _L1_cond_in['b2']}

def reference(x, cond_1024, mask_BxSxSx11_ik0, L0_cond_W_self, L0_cond_b_self, L0_cond_w_bias, L0_cond_b_bias, L0_cond_Wq, L0_cond_bq, L0_cond_Wk, L0_cond_bk, L0_cond_Wout, L0_cond_bout, L1_cond_Wm, L1_cond_bm, L1_cond_Lam_re, L1_cond_Lam_im, L1_cond_B_re, L1_cond_B_im, L1_cond_C_re, L1_cond_C_im, L1_cond_D_diag, L1_cond_log_step, L1_cond_Wc, L1_cond_bc, L1_cond_W1, L1_cond_b1, L1_cond_W2, L1_cond_b2):
    import jax
    import jax.numpy as jnp

    def _L0_cond_ref(v, q, adj, W_self, b_self, w_bias, b_bias, Wq, bq, Wk, bk, Wout, bout):
        import jax, jax.numpy as jnp
        import numpy as np
        NONGT = 20
        H = 16
        NEG = -9000000000000000.0

        def _gat_attention(self_feat, cond_adj, label_bias, Wq, bq, Wk, bk, Wout, bout):
            B, N, F = self_feat.shape
            ng = min(NONGT, N)
            dh = F // H
            kv = self_feat[:, :ng]
            qh = (self_feat @ Wq.T + bq).reshape(B, N, H, dh)
            kh = (kv @ Wk.T + bk).reshape(B, ng, H, dh)
            aff = jnp.einsum('bnhd,bmhd->bnhm', qh, kh) * (1.0 / np.sqrt(dh))
            mask = cond_adj[:, :, None, :] > 0
            aff = jnp.where(mask, aff, NEG) + label_bias[:, :, None, :]
            w = jax.nn.softmax(aff, axis=-1)
            out_t = jnp.einsum('bnhm,bmf->bnhf', w, kv)
            out = jnp.einsum('bnhf,hgf->bnhg', out_t, Wout) + bout.reshape(H, F // H)
            return out.reshape(B, N, F)

        def _forward(v, q, adj, W_self, b_self, w_bias, b_bias, Wq, bq, Wk, bk, Wout, bout):
            adj_f = adj.astype(jnp.float32)
            exp_v = v
            row_zero = exp_v.sum(-1) == 0
            q_exp = jnp.where(row_zero[..., None], 0.0, q[:, None, :])
            vcq = jnp.concatenate([exp_v, q_exp], axis=-1)
            self_feat = vcq @ W_self.T + b_self
            output = self_feat
            for d in range(2):
                A = adj_f if d == 0 else jnp.swapaxes(adj_f, 1, 2)
                A = A[:, :, :NONGT, :]
                cond = A.sum(-1)
                vb = A @ w_bias + b_bias
                output = output + _gat_attention(self_feat, cond, vb, Wq[d], bq[d], Wk[d], bk[d], Wout[d], bout[d])
            rel = jax.nn.relu(output)
            return exp_v + rel
        return _forward(v, q, adj, W_self, b_self, w_bias, b_bias, Wq, bq, Wk, bk, Wout, bout)

    def _L1_cond_ref(y, t, Wm, bm, Lam_re, Lam_im, B_re, B_im, C_re, C_im, D_diag, log_step, Wc, bc, W1, b1, W2, b2):
        import jax, jax.numpy as jnp
        import numpy as np
        B, L, D, P = (8, 512, 256, 64)

        def _ln(x):
            m = x.mean(-1, keepdims=True)
            v = x.var(-1, keepdims=True)
            return (x - m) * jax.lax.rsqrt(v + 1e-05)

        def _s5(u, Lam_re, Lam_im, B_re, B_im, C_re, C_im, D_diag, log_step):
            Lam = Lam_re + 1j * Lam_im
            dt = jnp.exp(log_step)
            Lam_bar = jnp.exp(Lam * dt)
            Bc = B_re + 1j * B_im
            B_bar = ((Lam_bar - 1.0) / Lam)[:, None] * Bc
            Bu = jnp.einsum('bld,pd->blp', u.astype(B_bar.dtype), B_bar)
            A = jnp.broadcast_to(Lam_bar, Bu.shape)

            def binop(e1, e2):
                a1, b1 = e1
                a2, b2 = e2
                return (a1 * a2, a2 * b1 + b2)
            _, xs = jax.lax.associative_scan(binop, (A, Bu), axis=1)
            Cc = C_re + 1j * C_im
            return 2.0 * jnp.einsum('blp,dp->bld', xs, Cc).real + D_diag * u
        mod = t @ Wm + bm
        shift_a, scale_a, gate_a, shift_ff, scale_ff, gate_ff = jnp.split(mod, 6, axis=-1)
        y_mod = _ln(y) * (1 + scale_a[:, None]) + shift_a[:, None]
        a_y = _s5(y_mod, Lam_re, Lam_im, B_re, B_im, C_re, C_im, D_diag, log_step)
        y = y + gate_a[:, None] * a_y
        cond = t @ Wc + bc
        scale_c, shift_c = jnp.split(cond, 2, axis=-1)
        y_norm = _ln(y) * (1 + scale_c[:, None]) + shift_c[:, None]
        y_mod = y_norm * (1 + scale_ff[:, None]) + shift_ff[:, None]
        h = jax.nn.gelu(y_mod @ W1 + b1)
        ff_y = h @ W2 + b2
        return y + gate_ff[:, None] * ff_y
    x = _L0_cond_ref(x, cond_1024, mask_BxSxSx11_ik0, L0_cond_W_self, L0_cond_b_self, L0_cond_w_bias, L0_cond_b_bias, L0_cond_Wq, L0_cond_bq, L0_cond_Wk, L0_cond_bk, L0_cond_Wout, L0_cond_bout)
    x = _L1_cond_ref(x, cond_1024, L1_cond_Wm, L1_cond_bm, L1_cond_Lam_re, L1_cond_Lam_im, L1_cond_B_re, L1_cond_B_im, L1_cond_C_re, L1_cond_C_im, L1_cond_D_diag, L1_cond_log_step, L1_cond_Wc, L1_cond_bc, L1_cond_W1, L1_cond_b1, L1_cond_W2, L1_cond_b2)
    return x

_drawn_inputs = setup_inputs


def setup_inputs(seed=0):
    import zlib

    import numpy as np

    out = dict(_drawn_inputs(seed))
    spreads = {'L0_cond_b_self': (0.0, 0.1),
     'L0_cond_bq': (0.0, 0.1),
     'L0_cond_bk': (0.0, 0.1),
     'L0_cond_bout': (0.0, 0.1),
     'L1_cond_Lam_re': (-0.5, 0.6),
     'L1_cond_b1': (0.0, 2.0),
     'L1_cond_b2': (0.0, 0.288)}
    factors = {'L1_cond_bm': 2.915, 'L1_cond_Wc': 6.326, 'L1_cond_bc': 32.78, 'L1_cond_W1': 2.818}
    for name, (base, spread) in spreads.items():
        noise = np.random.default_rng([zlib.crc32(name.encode()), seed]).standard_normal(out[name].shape)
        drawn = base * np.exp(spread * noise) if base else spread * noise
        out[name] = jnp.asarray(drawn.astype(out[name].dtype))
    for name, factor in factors.items():
        out[name] = (out[name] * factor).astype(out[name].dtype)
    return out
```

```python
from contextlib import ExitStack

import numpy as np

import concourse.bass as bass
from concourse import mybir

F32 = mybir.dt.float32
F32R = mybir.dt.float32r
I32 = mybir.dt.int32
ALU = mybir.AluOpType
ACT = mybir.ActivationFunctionType
AX_X = mybir.AxisListType.X

P = 128
B = 8
N = 256
F = 256
KT = F // P
NT = N // P
D = 2
H = 16
G = F // H
M = 20
L = 11
HM = H * M
HB = P // G
CH = 6
CR = CH * M
CHUNK_HEAD = (0, 6, 10)
CHUNK_COLS = ((0, 96), (96, 192), (192, 256))
NC = len(CHUNK_HEAD)
KV = B * M
GB = 4
GR = GB * M
S = 64
FF = 4 * F
FT = FF // P
NEG = -9000000000000000.0
EPS = 1e-5
ROUND = 12582912.0
TWO_PI = 6.283185307179586
LOG2E = 1.4426950408889634
LN2_H = 0.693359375
LN2_L = -2.12194440054690581e-4
PI2_H = 6.28125
PI2_M = 1.93500518798828125e-3
PI2_L = 3.0199159819567e-7
SIN_SCALE = 6.2831845

C_ID = 0
C_REP = C_ID + P
C_VMASK = C_REP + D * HM
C_KMASK = C_VMASK + F
C_BSEL = C_KMASK + HB
C_KVSEL = C_BSEL + B
C_GSEL = C_KVSEL + KV
C_TIME = C_GSEL + GB * CR
C_SIGN = C_TIME + N
C_ROW = C_SIGN + 1
C_ONE = C_ROW + P
C_BIASROW = C_ONE + P
C_END = C_BIASROW + 1


def constants():
    c = np.zeros((P, C_END), np.float32)
    c[:, C_ID:C_ID + P] = np.eye(P)
    rep = c[:, C_REP:C_REP + D * HM].reshape(P, D, H, M)
    for d in range(D):
        for m in range(M):
            rep[64 * d + m, d, :, m] = 1
            rep[64 * d + M + m, d, :, m] = 1
    for n, (lo, hi) in enumerate(CHUNK_COLS):
        for r in range(CR):
            h = CHUNK_HEAD[n] + r // M
            a, b = max(lo, h * G), min(hi, (h + 1) * G)
            if a < b:
                c[r, C_VMASK + a:C_VMASK + b] = 1
    for p in range(P):
        c[p, C_KMASK + p // G] = 0.25
    for b in range(B):
        for r in (b, 32 + b):
            c[r, C_BSEL + b] = 1
            c[r, C_KVSEL + b * M:C_KVSEL + (b + 1) * M] = 1
    gsel = c[:, C_GSEL:C_GSEL + GB * CR].reshape(P, GB, CH, M)
    for b in range(GB):
        for m in range(M):
            gsel[b * M + m, b, :, m] = 1
    c[:, C_TIME:C_TIME + N] = np.arange(N)
    c[:S, C_SIGN] = -1
    c[S:, C_SIGN] = 1
    c[0, C_ROW + 64] = c[0, C_ROW + 96] = 1
    c[:, C_ONE:C_ONE + P] = 1
    c[64, C_BIASROW] = c[96, C_BIASROW] = 1
    return c


def build(nc, dram):
    ctx = ExitStack()
    with ctx:
        def sb(name, shape, dt=F32):
            return ctx.enter_context(nc.sbuf_tensor(name, shape, dt))

        def sem(name):
            return ctx.enter_context(nc.semaphore(name))

        def f32(ap):
            return ap.bitcast(F32)

        const = sb("const", [P, C_END])
        ident = const[:, C_ID:C_ID + P]
        ident_r = sb("ident_r", [P, P], F32R)
        rep_r = sb("rep_r", [P, D, HM], F32R)
        gsel_r = sb("gsel_r", [P, GB, CR], F32R)
        ones_r = sb("ones_r", [P, P], F32R)
        stage = sb("stage", [P, 4, KT * D * F])
        wk, wq, wout = (stage[:, k].rearrange("p (k n) -> p k n", k=KT) for k in range(3))
        wself, wselfq = (stage[:, 3, k * KT * F:(k + 1) * KT * F].rearrange("p (k n) -> p k n", k=KT)
                         for k in range(2))
        w1 = stage[:, 0:2].rearrange("p a (b n) -> p (a b) n", n=FF)
        w2 = stage[:, 2:4].rearrange("p a (b n) -> p (a b) n", n=F)
        wself_h, wself_l = sb("wself_h", [P, KT, F], F32R), sb("wself_l", [P, KT, F], F32R)
        wq_h, wq_l = sb("wq_h", [P, KT, D * F], F32R), sb("wq_l", [P, KT, D * F], F32R)
        gl_h, gl_l = sb("gl_h", [P, FT, N], F32R), sb("gl_l", [P, FT, N], F32R)
        wk_h, wk_l, wout_h, wout_l = (g[:, k * FT // 2:(k + 1) * FT // 2].rearrange("p (k a) n -> p k (a n)", k=KT)
                                      for g in (gl_h, gl_l) for k in range(2))
        w1_h, w1_l = sb("w1_h", [P, KT, FF], F32R), sb("w1_l", [P, KT, FF], F32R)
        w2_h, w2_l = sb("w2_h", [P, FT, F], F32R), sb("w2_l", [P, FT, F], F32R)
        NMOD = 8 * KT
        late = sb("late", [P, KT * NMOD * P])
        wmod = late[:, :].rearrange("p (k n) -> p k n", k=KT)
        gl = late[:, 0:FT * N].rearrange("p (k n) -> p k n", n=N)
        aT, cz, y2, ffT = (late[:, (FT + 2 * k) * N:(FT + 2 * k + 2) * N].rearrange("p (k n) -> p k n", n=N)
                           for k in range(4))
        condT = sb("condT", [P, KT, P])
        rows = sb("rows", [1, F + D * F])
        bq = sb("bq", [P, D * KT])
        bk = sb("bk", [P, D * KT])
        bmod = sb("bmod", [P, NMOD])
        b12 = sb("b12", [P, FT + 2 * KT])
        wbias = sb("wbias", [P, L])
        bbias = sb("bbias", [P, 1])
        xkv = sb("xkv", [P, KT, KV])
        xkv_h, xkv_l = sb("xkv_h", [P, KT, KV], F32R), sb("xkv_l", [P, KT, KV], F32R)
        nzkv = sb("nzkv", [P, KV], F32R)
        qw = sb("qw", [P, F], F32R)
        skv_h, skv_l = sb("skv_h", [P, KT, KV], F32R), sb("skv_l", [P, KT, KV], F32R)
        kh = sb("kh", [P, D * KT, KV])
        vo_h, vo_l = (w2_l[:, k * FT // 2:(k + 1) * FT // 2].rearrange("p (g a) n -> p g (a n)", g=B // GB)
                      for k in range(2))
        vo_all = sb("vo_all", [P, B, D * F])
        lam = sb("lam", [P, 3])
        sc = sb("sc", [P, 40])
        sci = sb("sci", [P, 1], I32)
        bri = sb("bri", [P, 2, F])
        bw = sb("bw", [P, 2, F])
        bt = sb("bt", [P, 3, F])
        bwT = sb("bwT", [P, KT, 2, P])
        cri = sb("cri", [P, 2, F])
        cw = sb("cw", [P, 2, F])
        rot = sb("rot", [P, 2, N])
        mod = sb("mod", [P, NMOD, B])
        par_a = sb("par_a", [P, B, 8])
        par_f = sb("par_f", [P, B, 8])
        pt = sb("pt", [P, 4, KT, B])
        xT = sb("xT", [P, KT, N])
        x = sb("x", [P, NT, F])
        adj = sb("adj", [P, NT * D * M, L], I32)
        x_h, x_l = sb("x_h", [P, KT, N], F32R), sb("x_l", [P, KT, N], F32R)
        nz = sb("nz", [P, N], F32R)
        sf_h, sf_l = sb("sf_h", [P, KT, N], F32R), sb("sf_l", [P, KT, N], F32R)
        qT = sb("qT", [P, D, KT, N])
        count = sb("count", [P, NT * D * M])
        weighed = sb("weighed", [P, NT * D * M, L])
        vbias = sb("vbias", [P, NT * D * M])
        masked = sb("masked", [P, NT * D * M])
        addv = sb("addv", [P, NT, D, M])
        addn = sb("addn", [P, NT, D, 64])
        addT = sb("addT", [P, NT, P], F32R)
        kbd = sb("kbd", [P, D * KT, HB, M])
        vbd = sb("vbd", [P, D, F])
        smax = sb("smax", [P, NT, D * H])
        soft = sb("soft", [P, NT, D * H, M])
        ssum = sb("ssum", [P, NT, D * H])
        srec = sb("srec", [P, NT, D * H])
        pT = sb("pT", [P, NT, D, NC * P])
        tb = pT[:, :, :, :].rearrange("p t d (a n) -> p (t d a) n", n=P).rearrange("p (a b) n -> p a (b n)", b=2)
        y = sb("y", [P, NT, F])
        cur_a = sb("cur_a", [P, 8])
        cur_f = sb("cur_f", [P, 8])
        st = sb("st", [P, 2, NT, 6])
        mv = sb("mv", [P, 2, NT, 2])
        rstd = sb("rstd", [P, 2, NT])
        veps = sb("veps", [P, 2, NT])
        half, eps = sb("half", [P, NT]), sb("eps", [P, NT])
        mrs = sb("mrs", [P, 2, NT])
        ln = sb("ln", [P, 2, NT, F])
        uT = sb("uT", [P, KT, N])
        gdu = sb("gdu", [P, KT, N])
        bu = sb("bu", [P, 2, N])
        zin = sb("zin", [P, N])
        z = sb("z", [P, N])
        mt = sb("mt", [P, KT, N])
        m_h, m_l = sb("m_h", [P, KT, N], F32R), sb("m_l", [P, KT, N], F32R)
        res = sb("res", [P, NT, F])

        ps = ctx.enter_context(nc.psum_tensor("ps", [P, 8, 512], F32))
        ROWS, FEAT, SCORE, PROB, B6, B7 = 0, 1, 2, 4, 6, 7

        def bank(n, *dims):
            size = int(np.prod(dims))
            return ps[:, n, 0:size] if len(dims) == 1 else ps[:, n, 0:size].rearrange(
                "p (a b) -> p a b", a=dims[0])

        s_const, s_wselfq, s_rows, s_small, s_lam, s_bri, s_cri, s_wmod = (sem(n) for n in (
            "const_loaded", "wselfq_loaded", "rows_loaded", "small_loaded", "lam_loaded", "b_loaded",
            "c_loaded", "wmod_loaded"))
        s_cond = sem("cond_loaded")
        split_order = ("wself", "xkv", "wk", "wq", "wout", "w1", "w2")
        loaded = {n: sem(n + "_loaded") for n in split_order}
        high = sem("high_parts")
        low, low_mlp = sem("low_parts"), sem("low_parts_mlp")
        at = {n: k + 1 for k, n in enumerate(split_order)}
        parts = {"wself": (wself, wself_h, wself_l), "xkv": (xkv, xkv_h, xkv_l), "wk": (wk, wk_h, wk_l),
                 "wq": (wq, wq_h, wq_l), "wout": (wout, wout_h, wout_l), "w1": (w1, w1_h, w1_l),
                 "w2": (w2, w2_h, w2_l)}
        cleared, consts_r, cond_ready, qw_ready, kv_sums, nzkv_ready = (sem(n) for n in (
            "cleared", "consts_rounded", "cond_part_ready", "qw_ready", "kv_sums", "nzkv_ready"))
        skv_ready, skv_hs, skv_ls, kh_ready, kh_copied = (sem(n) for n in (
            "skv_ready", "skv_h_ready", "skv_l_ready", "kh_ready", "kh_copied"))
        vo_ready, vo_hs, vo_ls, vo_spread, vo_masked = (sem(n) for n in (
            "vo_ready", "vo_h_ready", "vo_l_ready", "vo_spread", "vo_masked"))
        mod_ready, mod_copied, params_step = sem("mod_ready"), sem("mod_copied"), sem("params_ready")
        s5_step, turns, rot_ready, bw_ready, cw_ready, bwt_ready, bwt_copied = (sem(n) for n in (
            "s5_step", "turns_ready", "rot_ready", "bw_ready", "cw_ready", "bwt_ready", "bwt_copied"))

        s_xT, s_x, s_adj, s_out = (sem(n) for n in ("xT_loaded", "x_loaded", "adj_loaded", "out_stored"))
        x_high, x_low = sem("x_high"), sem("x_low")
        row_sums, nz_ready, feat_ready, feat_h, feat_l = (sem(n) for n in (
            "row_sums", "nz_ready", "feat_ready", "feat_h_ready", "feat_l_ready"))
        q_ready, q_copied = sem("q_ready"), sem("q_copied")
        label_floats = sem("label_floats")
        counted, label_weighed, label_sums, label_add, add_ready, addt_ready, addt_copied = (sem(n) for n in (
            "counted", "label_weighed", "label_sums", "label_add", "add_ready", "addt_ready", "addt_copied"))
        kbd_ready, vbd_ready = sem("kbd_ready"), sem("vbd_ready")
        scored, maxed, shifted_s, exped, summed, inverted, probs_ready = (sem(n) for n in (
            "scored", "maxed", "shifted_ready", "exped", "summed", "inverted", "probs_ready"))
        pt_ready, pt_copied, attended, y_ready = (sem(n) for n in (
            "pt_ready", "pt_copied", "attended", "y_ready"))
        cur_a_s, cur_f_s = sem("cur_a_ready"), sem("cur_f_ready")
        stats_s, mv_s, veps_s, rstd_s, mrs_s, ln_s, lnt_ready = ([sem(f"{n}_{k}") for k in range(2)] for n in (
            "stats_ready", "mean_var_ready", "var_eps_ready", "rstd_ready", "mean_rstd_ready", "ln_ready",
            "lnt_ready"))
        u_ready, gdu_ready, bu_ready, bu_turned, zin_s, z_s, cz_s, c_ready, a_ready, at_ready = (sem(n) for n in (
            "u_ready", "gdu_ready", "bu_ready", "bu_turned", "scan_input", "scanned", "z_turned",
            "c_ready", "a_ready", "at_ready"))
        y2_ready, m_ready, m_hs, m_ls, h_ready, gelu_s, gl_hs, gl_ls = (sem(n) for n in (
            "y2_ready", "m_ready", "m_h_ready", "m_l_ready", "h_ready", "gelu_done", "gelu_h_ready",
            "gelu_l_ready"))
        ff_ready, ff_copied, fft_ready, res_ready = (sem(n) for n in (
            "ff_ready", "ff_copied", "fft_ready", "res_ready"))

        block = ctx.enter_context(nc.Block())

        GIVEN = 1

        def waited(eng, signal, value):
            if not (isinstance(value, int) and value <= 0):
                eng.wait_ge(signal, value)

        def stepper(eng, chain):
            count = {}

            def step(ins, signal=chain):
                count[signal.name] = count.get(signal.name, 0) + 1
                ins.then_inc(signal, 1)
                eng.wait_ge(signal, count[signal.name])
            return step

        @block.sync
        def _(sp):
            def load_xT(u):
                waited(sp, x_low, u)
                sp.dma_start(xT[:], dram["xT"][bass.ds(u, 1)].rearrange("b p k n -> (b p) k n")).then_inc(s_xT, 16)

            def load_adj(u):
                waited(sp, counted, u)
                waited(sp, label_floats, u)
                sp.dma_start(adj[:], dram["adj"][bass.ds(u, 1)].rearrange("b p t l -> (b p) t l")).then_inc(s_adj, 16)

            def load_x(u):
                waited(sp, y_ready, u)
                sp.dma_start(x[:], dram["x"][bass.ds(u, 1)].rearrange("b (t p) f -> p (b t) f", p=P)).then_inc(s_x, 16)

            def store(u):
                sp.wait_ge(res_ready, GIVEN + u + 1)
                sp.dma_start(dram["out"][bass.ds(u, 1)].rearrange("b (t p) f -> p (b t) f", p=P), res[:]).then_inc(s_out, 16)

            for signal, turn in ((a_ready, KT), (ff_copied, KT), (ff_ready, 1), (res_ready, 1), (s_out, 16)):
                sp.sem_inc(signal, GIVEN * turn)
            for name in ("wself", "xkv", "wk"):
                sp.dma_start(parts[name][0][:], dram[name]).then_inc(loaded[name], 16)
            load_xT(0)
            sp.dma_start(const[:], dram["const"]).then_inc(s_const, 16)
            for name in ("wq", "wout"):
                sp.dma_start(parts[name][0][:], dram[name]).then_inc(loaded[name], 16)
            load_adj(0)
            load_x(0)
            sp.dma_start(wmod[:], dram["wmod"]).then_inc(s_wmod, 16)
            for name, before in (("w1", "wq"), ("w2", "wout")):
                sp.wait_ge(low, at[before])
                if name == "w2":
                    sp.wait_ge(cond_ready, 1)
                sp.dma_start(parts[name][0][:], dram[name]).then_inc(loaded[name], 16)
            with sp.Fori(0, B - 1) as i:
                load_xT(i + 1)
                load_adj(i + 1)
                load_x(i + 1)
                store(i)
            store(B - 1)
            sp.wait_ge(s_out, 16 * (GIVEN + B))

        @block.gpsimd
        def _(pool):
            step = stepper(pool, s5_step)

            def exp_steps(out, v, t):
                n, r, q, w = (sc[:, t + k:t + k + 1] for k in range(4))
                step(pool.tensor_scalar(q, v, -87.0, 88.0, ALU.max, ALU.min))
                step(pool.tensor_scalar(n, q, LOG2E, ROUND, ALU.mult, ALU.add))
                step(pool.tensor_scalar(n, n, ROUND, None, ALU.subtract))
                step(pool.tensor_scalar(w, n, LN2_H, None, ALU.mult))
                step(pool.tensor_tensor(r, q, w, ALU.subtract))
                step(pool.tensor_scalar(w, n, LN2_L, None, ALU.mult))
                step(pool.tensor_tensor(r, r, w, ALU.subtract))
                step(pool.tensor_scalar(q, r, 1.0 / 5040, 1.0 / 720, ALU.mult, ALU.add))
                for c in (1.0 / 120, 1.0 / 24, 1.0 / 6, 0.5, 1.0, 1.0):
                    step(pool.tensor_scalar(q, q, r, c, ALU.mult, ALU.add))
                step(pool.tensor_scalar(sci[:], n, 127.0, 8388608.0, ALU.add, ALU.mult))
                step(pool.tensor_tensor(out, q, sci[:].bitcast(F32), ALU.mult))

            def x_parts(u):
                pool.wait_ge(x_high, u + 1)
                pool.tensor_tensor(x_l[:], xT[:], f32(x_h[:]), ALU.subtract).then_inc(x_low, 1)

            def label_weights(u):
                pool.wait_ge(label_floats, u + 1)
                pool.tensor_tensor(weighed[:], weighed[:], wbias[:].unsqueeze(1).broadcast_to([P, NT * D * M, L]),
                                   ALU.mult).then_inc(label_weighed, 1)

            def key_blocks(u):
                waited(pool, scored, NT * u)
                keys = kh[:, :, bass.ds(u * M, M)]
                pool.tensor_tensor(kbd[:], keys.unsqueeze(2).broadcast_to([P, D * KT, HB, M]),
                                   const[:, C_KMASK:C_KMASK + HB].unsqueeze(1).unsqueeze(3)
                                   .broadcast_to([P, D * KT, HB, M]), ALU.mult).then_inc(kbd_ready, 1)

            def value_blocks(u):
                waited(pool, attended, u)
                pool.tensor_copy(vbd[0:CR, :, :].rearrange("p d f -> p (d f)"),
                                 vo_all[0:CR, bass.ds(u, 1), :].rearrange("p b f -> p (b f)")).then_inc(vbd_ready, 1)

            def probabilities(u, t):
                pool.wait_ge(inverted, NT * u + t + 1)
                pool.tensor_tensor(soft[:, t], soft[:, t], srec[:, t].unsqueeze(2).broadcast_to([P, D * H, M]),
                                   ALU.mult).then_inc(probs_ready, 1)

            def rstd_of(u, k):
                pool.wait_ge(mv_s[k], NT * u + NT)
                pool.tensor_tensor(veps[:, k], mv[:, k, :, 1], eps[:], ALU.add).then_inc(veps_s[k], 1)
                pool.wait_ge(veps_s[k], u + 1)
                pool.tensor_tensor(rstd[:, k], veps[:, k], half[:], ALU.pow).then_inc(rstd_s[k], 1)
                pool.wait_ge(rstd_s[k], u + 1)
                pool.tensor_tensor(mrs[:, k], mv[:, k, :, 0], rstd[:, k], ALU.mult).then_inc(mrs_s[k], 1)

            def take_params(u):
                pool.wait_ge(a_ready, KT * (GIVEN + u))
                pool.tensor_copy(cur_a[:], par_a[:, bass.ds(u, 1), :].rearrange("p b k -> p (b k)")).then_inc(cur_a_s, 1)
                pool.wait_ge(ff_copied, KT * (GIVEN + u))
                pool.tensor_copy(cur_f[:], par_f[:, bass.ds(u, 1), :].rearrange("p b k -> p (b k)")).then_inc(cur_f_s, 1)

            def skip_term(u):
                pool.wait_ge(u_ready, KT * u + KT)
                pool.tensor_tensor(gdu[:], uT[:], cur_a[:, 6:6 + KT].unsqueeze(2).broadcast_to([P, KT, N]), ALU.mult)\
                    .then_inc(gdu_ready, 1)

            def both(ua, ub):
                take_params(ub)
                if ua is not None:
                    x_parts(ua)
                skip_term(ub)
                if ua is not None:
                    label_weights(ua)
                    key_blocks(ua)
                    value_blocks(ua)
                rstd_of(ub, 1)
                if ua is not None:
                    probabilities(ua, 0)
                    probabilities(ua, 1)
                if ua is not None:
                    rstd_of(ua, 0)

            step(pool.memset(condT[:], 0.0), cleared)
            step(pool.memset(addn[:], 0.0), cleared)
            step(pool.memset(half[:], -0.5), cleared)
            step(pool.memset(eps[:], EPS), cleared)
            x_parts(0)

            v = lambda k: sc[:, k:k + 1]
            lr, li, ls = lam[:, 0:1], lam[:, 1:2], lam[:, 2:3]
            dt, a, th, n, r, w = v(0), v(1), v(2), v(3), v(4), v(5)
            sign = const[:, C_SIGN:C_SIGN + 1]
            pool.wait_ge(s_lam, 32)
            exp_steps(dt, ls, 10)
            step(pool.tensor_tensor(a, lr, dt, ALU.mult))
            exp_steps(a, a, 10)
            step(pool.tensor_tensor(th, li, dt, ALU.mult))
            step(pool.tensor_scalar(n, th, 1.0 / TWO_PI, ROUND, ALU.mult, ALU.add))
            step(pool.tensor_scalar(n, n, ROUND, None, ALU.subtract))
            for part in (PI2_H, PI2_M, PI2_L):
                step(pool.tensor_scalar(w, n, part, None, ALU.mult))
                step(pool.tensor_tensor(th, th, w, ALU.subtract))
            fh, fl = v(6), v(7)
            step(pool.tensor_scalar(r, th, 1.0 / TWO_PI, None, ALU.mult))
            step(pool.tensor_scalar(fh, r, 4096.0, ROUND, ALU.mult, ALU.add))
            step(pool.tensor_scalar(fh, fh, ROUND, 1.0 / 4096, ALU.subtract, ALU.mult))
            step(pool.tensor_tensor(fl, r, fh, ALU.subtract))
            pool.wait_ge(s_const, 16)
            time = const[:, C_TIME:C_TIME + N]
            T = lambda k: tb[:, k, :]
            step(pool.tensor_scalar(T(0), time, fh, None, ALU.mult))
            step(pool.tensor_scalar(T(1), T(0), ROUND, ROUND, ALU.add, ALU.subtract))
            step(pool.tensor_tensor(T(0), T(0), T(1), ALU.subtract))
            step(pool.tensor_scalar(T(2), time, fl, None, ALU.mult))
            step(pool.tensor_tensor(T(0), T(0), T(2), ALU.add))
            step(pool.tensor_scalar(T(3), T(0), 0.25, None, ALU.add))
            step(pool.tensor_scalar(T(1), T(0), ROUND, ROUND, ALU.add, ALU.subtract))
            step(pool.tensor_scalar(T(2), T(3), ROUND, ROUND, ALU.add, ALU.subtract))
            step(pool.tensor_tensor(T(4), T(3), T(2), ALU.subtract), turns)
            step(pool.tensor_tensor(T(5), T(0), T(1), ALU.subtract), turns)
            pool.wait_ge(kh_copied, D * KT)
            key_blocks(0)
            pool.wait_ge(s_small, 16 * 6)
            label_weights(0)
            pool.wait_ge(rot_ready, 2)
            cs, sn = rot[:, 0, 1:2], rot[:, 1, 1:2]
            nr, ni, den, kr, ki, e = v(20), v(21), v(22), v(23), v(24), v(25)
            kis, krs, c2 = v(26), v(27), v(28)
            step(pool.tensor_tensor(nr, a, cs, ALU.mult))
            step(pool.tensor_scalar(nr, nr, 1.0, None, ALU.subtract))
            step(pool.tensor_tensor(ni, a, sn, ALU.mult))
            step(pool.tensor_tensor(den, lr, lr, ALU.mult))
            step(pool.tensor_tensor(e, li, li, ALU.mult))
            step(pool.tensor_tensor(den, den, e, ALU.add))
            step(pool.tensor_tensor(kr, nr, lr, ALU.mult))
            step(pool.tensor_tensor(e, ni, li, ALU.mult))
            step(pool.tensor_tensor(kr, kr, e, ALU.add))
            step(pool.tensor_tensor(ki, ni, lr, ALU.mult))
            step(pool.tensor_tensor(e, nr, li, ALU.mult))
            step(pool.tensor_tensor(ki, ki, e, ALU.subtract))
            step(pool.memset(c2, -1.0))
            step(pool.tensor_tensor(den, den, c2, ALU.pow))
            step(pool.tensor_tensor(kr, kr, den, ALU.mult))
            step(pool.tensor_tensor(ki, ki, den, ALU.mult))
            step(pool.tensor_tensor(kis, ki, sign, ALU.mult))
            step(pool.tensor_tensor(krs, kr, sign, ALU.mult))
            step(pool.tensor_scalar(krs, krs, -1.0, None, ALU.mult))
            pool.wait_ge(s_bri, 64)
            step(pool.tensor_scalar(bt[:, 0], bri[:, 0], kr, None, ALU.mult))
            step(pool.tensor_scalar(bt[:, 1], bri[:, 1], kis, None, ALU.mult))
            step(pool.tensor_tensor(bw[:, 0], bt[:, 0], bt[:, 1], ALU.add), bw_ready)
            step(pool.tensor_scalar(bt[:, 2], bri[:, 0], ki, None, ALU.mult))
            step(pool.tensor_scalar(bt[:, 1], bri[:, 1], krs, None, ALU.mult))
            step(pool.tensor_tensor(bw[:, 1], bt[:, 2], bt[:, 1], ALU.add), bw_ready)
            pool.wait_ge(s_cri, 64)
            step(pool.tensor_scalar(cw[:, 0], cri[:, 0], sign, -2.0, ALU.mult, ALU.mult), cw_ready)
            step(pool.tensor_scalar(cw[:, 1], cri[:, 1], -2.0, None, ALU.mult), cw_ready)
            pool.wait_ge(vo_masked, B)
            value_blocks(0)
            probabilities(0, 0)
            probabilities(0, 1)
            rstd_of(0, 0)
            for name in ("w1", "w2"):
                whole, part_h, part_l = parts[name]
                pool.wait_ge(high, at[name])
                pool.tensor_tensor(part_l[:], whole[:], f32(part_h[:]), ALU.subtract).then_inc(low_mlp, 1)
            pool.wait_ge(params_step, 11)
            with pool.Fori(0, B - 1) as i:
                both(i + 1, i)
            both(None, B - 1)

        @block.scalar
        def _(act):
            def tokens_high(u):
                act.wait_ge(s_xT, 16 * u + 16)
                waited(act, feat_ready, u)
                act.activation(x_h[:], xT[:], ACT.Copy).then_inc(x_high, 1)

            def label_float(u):
                act.wait_ge(s_adj, 16 * u + 16)
                waited(act, label_sums, u)
                act.activation(weighed[:], adj[:], ACT.Copy).then_inc(label_floats, 1)

            def features_high(u):
                act.wait_ge(feat_ready, u + 1)
                act.activation(sf_h[:], bank(FEAT, KT, N), ACT.Copy).then_inc(feat_h, 1)

            def queries(u, d):
                act.wait_ge(q_ready, D * u + d + 1)
                for k in range(KT):
                    act.activation(qT[:, d, k], bank(ROWS + d, KT, N)[:, k], ACT.Identity,
                                   bias=bq[:, d * KT + k:d * KT + k + 1]).then_inc(q_copied, 1)

            def additive(u):
                act.wait_ge(addt_ready, u + 1)
                act.activation(addT[:], bank(PROB, NT, P), ACT.Copy).then_inc(addt_copied, 1)

            def exponentials(u, t):
                act.wait_ge(shifted_s, NT * u + t + 1)
                act.activation(soft[:, t], soft[:, t], ACT.Exp).then_inc(exped, 1)

            def transposed(u, t):
                act.wait_ge(pt_ready, NT * u + t + 1)
                act.activation(pT[0:CR, t], ps[0:CR, PROB:PROB + D, 0:NC * P], ACT.Copy).then_inc(pt_copied, 1)

            def s5_input(u):
                act.wait_ge(lnt_ready[0], u + 1)
                act.wait_ge(cur_a_s, u + 1)
                for k in range(KT):
                    act.activation(uT[:, k], bank(B6, KT, N)[:, k], ACT.Identity, bias=cur_a[:, 2 + k:3 + k],
                                   scale=cur_a[:, k:k + 1]).then_inc(u_ready, 1)

            def mlp_input(u):
                act.wait_ge(lnt_ready[1], u + 1)
                act.wait_ge(cur_f_s, u + 1)
                for k in range(KT):
                    act.activation(mt[:, k], bank(B6, KT, N)[:, k], ACT.Identity, bias=cur_f[:, 2 + k:3 + k],
                                   scale=cur_f[:, k:k + 1]).then_inc(m_ready, 1)

            def gelus(u, q):
                act.wait_ge(h_ready, FT // 2 * u + q + 1)
                act.wait_ge(ff_ready, GIVEN + u)
                for k in (2 * q, 2 * q + 1):
                    act.activation(gl[:, k], bank(B7 if q % 2 == 0 else B6, 2, N)[:, k % 2], ACT.Gelu_apprx_tanh,
                                   bias=b12[:, k:k + 1]).then_inc(gelu_s, 1)
                act.wait_ge(gelu_s, FT * u + 2 * q + 2)
                act.activation(gl_h[:, 2 * q:2 * q + 2], gl[:, 2 * q:2 * q + 2], ACT.Copy).then_inc(gl_hs, 1)

            def mlp_output(u):
                act.wait_ge(ff_ready, GIVEN + u + 1)
                for k in range(KT):
                    act.activation(ffT[:, k], bank(B7, KT, N)[:, k], ACT.Identity, bias=cur_f[:, 6 + k:7 + k],
                                   scale=cur_f[:, 4 + k:5 + k]).then_inc(ff_copied, 1)

            def both(ua, ub):
                if ua is not None:
                    tokens_high(ua)
                s5_input(ub)
                if ua is not None:
                    features_high(ua)
                    label_float(ua)
                    queries(ua, 0)
                    queries(ua, 1)
                    additive(ua)
                    exponentials(ua, 0)
                    exponentials(ua, 1)
                    transposed(ua, 0)
                mlp_input(ub)
                if ua is not None:
                    transposed(ua, 1)
                for q in range(FT // 2):
                    gelus(ub, q)
                mlp_output(ub)

            def high_part(name):
                whole, part_h, _ = parts[name]
                act.wait_ge(loaded[name], 16)
                act.activation(part_h[:], whole[:], ACT.Copy).then_inc(high, 1)

            act.dma_start(wselfq[:], dram["wselfq"]).then_inc(s_wselfq, 16)
            act.wait_ge(cleared, 1)
            act.dma_start(condT[:, :, 0:B], dram["condT"]).then_inc(s_cond, 16)
            act.dma_start(condT[:, :, 32:32 + B], dram["condT"]).then_inc(s_cond, 16)
            act.dma_start(rows[:], dram["rows"]).then_inc(s_rows, 16)
            for h in range(2):
                act.dma_start(lam[h * S:(h + 1) * S, :], dram["lam"]).then_inc(s_lam, 16)
            act.dma_start(bk[:], dram["bk"]).then_inc(s_small, 16)
            act.dma_start(bq[:], dram["bq"]).then_inc(s_small, 16)
            act.dma_start(wbias[:], dram["wbias"].broadcast_to([P, L])).then_inc(s_small, 16)
            act.dma_start(bbias[:], dram["bbias"].broadcast_to([P, 1])).then_inc(s_small, 16)
            act.dma_start(bmod[:], dram["bmod"]).then_inc(s_small, 16)
            act.dma_start(b12[:], dram["b12"]).then_inc(s_small, 16)
            high_part("wself")
            high_part("xkv")
            high_part("wk")
            tokens_high(0)
            for h in range(2):
                act.dma_start(bri[h * S:(h + 1) * S, 0, :], dram["b_ri"][h]).then_inc(s_bri, 16)
                act.dma_start(bri[h * S:(h + 1) * S, 1, :], dram["b_ri"][1 - h]).then_inc(s_bri, 16)
                act.dma_start(cri[h * S:(h + 1) * S, 0, :], dram["c_ri"][h]).then_inc(s_cri, 16)
                act.dma_start(cri[h * S:(h + 1) * S, 1, :], dram["c_ri"][1 - h]).then_inc(s_cri, 16)
            act.wait_ge(skv_ready, 1)
            act.activation(skv_h[:], bank(SCORE, KT, KV), ACT.Copy).then_inc(skv_hs, 1)
            high_part("wq")
            act.wait_ge(s_small, 16 * 6)
            for d in range(D):
                act.wait_ge(kh_ready, d + 1)
                for k in range(KT):
                    act.activation(kh[:, d * KT + k], bank(SCORE + 1 + d, KT, KV)[:, k], ACT.Identity,
                                   bias=bk[:, d * KT + k:d * KT + k + 1]).then_inc(kh_copied, 1)
            high_part("wout")
            features_high(0)
            label_float(0)
            queries(0, 0)
            queries(0, 1)
            for g in range(B // GB):
                act.wait_ge(vo_ready, g + 1)
                act.activation(vo_h[0:GR, g], ps[0:GR, (5, 2)[g], :], ACT.Copy).then_inc(vo_hs, 1)
            additive(0)
            act.wait_ge(turns, 2)
            for k in range(2):
                act.activation(rot[:, k], tb[:, 4 + k, :], ACT.Sin, scale=SIN_SCALE).then_inc(rot_ready, 1)
            exponentials(0, 0)
            exponentials(0, 1)
            act.wait_ge(bwt_ready, 1)
            act.activation(bwT[:].rearrange("p k s q -> p (k s q)"), ps[:, 7, :], ACT.Copy).then_inc(bwt_copied, 1)
            transposed(0, 0)
            transposed(0, 1)
            high_part("w1")
            high_part("w2")
            with act.Fori(0, B - 1) as i:
                both(i + 1, i)
            both(None, B - 1)

        @block.tensor
        def _(pe):
            def three(out, wh, wl, xh, xl, first, last):
                pe.matmul(out, wh, xh, start=first, stop=False, skip_group_check=True)
                pe.matmul(out, wh, xl, start=False, stop=False, skip_group_check=True)
                return pe.matmul(out, wl, xh, start=False, stop=last, skip_group_check=True)

            def rowsums(u):
                pe.wait_ge(x_high, u + 1)
                pe.wait_ge(x_low, u + 1)
                waited(pe, q_copied, D * KT * u)
                for k in range(KT):
                    for part in (x_h, x_l):
                        last = pe.matmul(bank(ROWS, N), ones_r[:], part[:, k], start=k == 0 and part is x_h,
                                         stop=k == KT - 1 and part is x_l)
                last.then_inc(row_sums, 1)

            def features(u):
                waited(pe, y_ready, u)
                for f in range(KT):
                    out, cols = bank(FEAT, KT, N)[:, f], slice(f * P, (f + 1) * P)
                    for k in range(KT):
                        three(out, wself_h[:, k, cols], wself_l[:, k, cols], x_h[:, k], x_l[:, k], k == 0, False)
                    if f == 0:
                        pe.wait_ge(nz_ready, u + 1)
                    last = pe.matmul(out, qw[:, cols], nz[:], start=False, stop=True, skip_group_check=True)
                last.then_inc(feat_ready, 1)

            def queries(u, d):
                if d == 0:
                    pe.wait_ge(feat_h, u + 1)
                    pe.wait_ge(feat_l, u + 1)
                for f in range(KT):
                    cols = slice(d * F + f * P, d * F + (f + 1) * P)
                    for k in range(KT):
                        last = three(bank(ROWS + d, KT, N)[:, f], wq_h[:, k, cols], wq_l[:, k, cols],
                                     sf_h[:, k], sf_l[:, k], k == 0, k == KT - 1)
                last.then_inc(q_ready, 1)

            def additive(u):
                pe.wait_ge(add_ready, 2 * u + 2)
                waited(pe, pt_copied, NT * u)
                for t in range(NT):
                    last = pe.transpose(bank(PROB, NT, P)[:, t], addn[:, t].rearrange("p d m -> p (d m)"), ident)
                last.then_inc(addt_ready, 1)

            def scores(u, t):
                if t == 0:
                    pe.wait_ge(kbd_ready, u + 1)
                    pe.wait_ge(q_copied, D * KT * (u + 1))
                    pe.wait_ge(addt_copied, u + 1)
                waited(pe, shifted_s, NT * u + t)
                rows_t = slice(t * P, (t + 1) * P)
                for d in range(D):
                    out = ps[:, SCORE + d, 0:HM]
                    pe.matmul(out, addT[:, t], rep_r[:, d], start=True, stop=False, skip_group_check=True)
                    for k in range(KT):
                        last = pe.matmul(out[:, k * HB * M:(k + 1) * HB * M], qT[:, d, k, rows_t],
                                         kbd[:, d * KT + k].rearrange("p h m -> p (h m)"), start=False,
                                         stop=k == KT - 1, skip_group_check=True)
                last.then_inc(scored, 1)

            def prob_transposes(u, t):
                pe.wait_ge(probs_ready, NT * u + t + 1)
                waited(pe, pt_copied, NT * u + t)
                for d in range(D):
                    rows_of = soft[:, t, d * H:(d + 1) * H].rearrange("p h m -> p (h m)")
                    for c, h in enumerate(CHUNK_HEAD):
                        last = pe.transpose(ps[0:CR, PROB + d, c * P:(c + 1) * P],
                                            rows_of[:, h * M:h * M + CR], ident)
                last.then_inc(pt_ready, 1)

            def own_features(u):
                for t in range(NT):
                    rows_t = slice(t * P, (t + 1) * P)
                    for k in range(KT):
                        out = ps[:, FEAT, t * F + k * P:t * F + (k + 1) * P]
                        pe.matmul(out, sf_h[:, k, rows_t], ident_r[:], start=t == 0 and k == 0, stop=False,
                                  skip_group_check=True)
                        pe.matmul(out, sf_l[:, k, rows_t], ident_r[:], start=False, stop=False,
                                  skip_group_check=True)

            def attend(u, t):
                if t == 0:
                    pe.wait_ge(vbd_ready, u + 1)
                pe.wait_ge(pt_copied, NT * u + t + 1)
                for d in range(D):
                    for c, (lo, hi) in enumerate(CHUNK_COLS):
                        last = pe.matmul(ps[:, FEAT, t * F + lo:t * F + hi], pT[0:CR, t, d, c * P:(c + 1) * P],
                                         vbd[0:CR, d, lo:hi], start=False,
                                         stop=t == NT - 1 and d == D - 1 and c == NC - 1, skip_group_check=True)
                if t == NT - 1:
                    last.then_inc(attended, 1)

            def ln_transposes(u, n):
                pe.wait_ge(ln_s[n], NT * u + NT)
                if n == 0:
                    pe.wait_ge(res_ready, GIVEN + u)
                for t in range(NT):
                    for k in range(KT):
                        last = pe.transpose(bank(B6, KT, N)[:, k, t * P:(t + 1) * P],
                                            ln[:, n, t, k * P:(k + 1) * P], ident)
                last.then_inc(lnt_ready[n], 1)

            def s5_in(u):
                pe.wait_ge(u_ready, KT * u + KT)
                for s in range(2):
                    for k in range(KT):
                        last = pe.matmul(bank(B7, 2, N)[:, s], bwT[:, k, s], uT[:, k], start=k == 0,
                                         stop=k == KT - 1)
                last.then_inc(bu_ready, 1)

            def s5_out(u):
                pe.wait_ge(cz_s, u + 1)
                for f in range(KT):
                    for s in range(2):
                        last = pe.matmul(bank(B6, KT, N)[:, f], cw[:, s, f * P:(f + 1) * P], cz[:, s],
                                         start=s == 0, stop=s == 1)
                last.then_inc(c_ready, 1)

            def s5_transposes(u):
                pe.wait_ge(a_ready, KT * (GIVEN + u + 1))
                for t in range(NT):
                    for k in range(KT):
                        last = pe.transpose(bank(B7, NT, F)[:, t, k * P:(k + 1) * P],
                                            aT[:, k, t * P:(t + 1) * P], ident)
                last.then_inc(at_ready, 1)

            def mlp_up(u, q):
                if q == 0:
                    pe.wait_ge(m_hs, u + 1)
                    pe.wait_ge(m_ls, u + 1)
                if q >= 2:
                    pe.wait_ge(gelu_s, FT * u + 2 * q - 2)
                for j in range(2):
                    cols = slice((2 * q + j) * P, (2 * q + j + 1) * P)
                    for k in range(KT):
                        last = three(bank(B7 if q % 2 == 0 else B6, 2, N)[:, j], w1_h[:, k, cols],
                                     w1_l[:, k, cols], m_h[:, k], m_l[:, k], k == 0, k == KT - 1)
                last.then_inc(h_ready, 1)

            def mlp_down(u):
                for k in range(FT):
                    if k == 0:
                        pe.wait_ge(gelu_s, FT * u + FT - 2)
                    if k % 2 == 0:
                        pe.wait_ge(gl_hs, FT // 2 * u + k // 2 + 1)
                        pe.wait_ge(gl_ls, FT // 2 * u + k // 2 + 1)
                    for f in range(KT):
                        cols = slice(f * P, (f + 1) * P)
                        last = three(bank(B7, KT, N)[:, f], w2_h[:, k, cols], w2_l[:, k, cols], gl_h[:, k],
                                     gl_l[:, k], k == 0 and f == 0, k == FT - 1 and f == KT - 1)
                last.then_inc(ff_ready, 1)

            def mlp_transposes(u):
                pe.wait_ge(ff_copied, KT * (GIVEN + u + 1))
                pe.wait_ge(gelu_s, FT * u + FT)
                for t in range(NT):
                    for k in range(KT):
                        last = pe.transpose(bank(B6, NT, F)[:, t, k * P:(k + 1) * P],
                                            ffT[:, k, t * P:(t + 1) * P], ident)
                last.then_inc(fft_ready, 1)

            def both(ua, ub):
                ln_transposes(ub, 0)
                if ua is not None:
                    rowsums(ua)
                    features(ua)
                s5_in(ub)
                if ua is not None:
                    queries(ua, 0)
                    queries(ua, 1)
                    additive(ua)
                    scores(ua, 0)
                s5_out(ub)
                if ua is not None:
                    own_features(ua)
                    scores(ua, 1)
                s5_transposes(ub)
                if ua is not None:
                    prob_transposes(ua, 0)
                ln_transposes(ub, 1)
                if ua is not None:
                    prob_transposes(ua, 1)
                    attend(ua, 0)
                mlp_up(ub, 0)
                mlp_up(ub, 1)
                if ua is not None:
                    attend(ua, 1)
                mlp_up(ub, 2)
                mlp_up(ub, 3)
                mlp_down(ub)
                mlp_transposes(ub)

            pe.wait_ge(cleared, 4)
            pe.wait_ge(s_cond, 32)
            pe.wait_ge(s_wselfq, 16)
            for k in range(KT):
                pe.matmul(bank(B6, F), condT[:, k], wselfq[:, k], start=k == 0, stop=False)
            pe.wait_ge(s_rows, 16)
            pe.wait_ge(s_const, 16)
            pe.matmul(bank(B6, F), const[0:1, C_ROW:C_ROW + P], rows[:, 0:F], start=False, stop=True)\
                .then_inc(cond_ready, 1)
            pe.wait_ge(consts_r, 4)
            pe.wait_ge(high, at["xkv"])
            pe.wait_ge(low, at["xkv"])
            for k in range(KT):
                for part in (xkv_h, xkv_l):
                    last = pe.matmul(bank(B7, KV), ones_r[:], part[:, k], start=k == 0 and part is xkv_h,
                                     stop=k == KT - 1 and part is xkv_l)
            last.then_inc(kv_sums, 1)
            for f in range(KT):
                out, cols = bank(SCORE, KT, KV)[:, f], slice(f * P, (f + 1) * P)
                for k in range(KT):
                    three(out, wself_h[:, k, cols], wself_l[:, k, cols], xkv_h[:, k], xkv_l[:, k], k == 0, False)
                if f == 0:
                    pe.wait_ge(qw_ready, 3)
                    pe.wait_ge(nzkv_ready, 4)
                last = pe.matmul(out, qw[:, cols], nzkv[:], start=False, stop=True, skip_group_check=True)
            last.then_inc(skv_ready, 1)
            rowsums(0)
            features(0)
            pe.wait_ge(high, at["wk"])
            pe.wait_ge(low, at["wk"])
            pe.wait_ge(skv_hs, 1)
            pe.wait_ge(skv_ls, 1)
            for d in range(D):
                for f in range(KT):
                    cols = slice(d * F + f * P, d * F + (f + 1) * P)
                    for k in range(KT):
                        last = three(bank(SCORE + 1 + d, KT, KV)[:, f], wk_h[:, k, cols], wk_l[:, k, cols],
                                     skv_h[:, k], skv_l[:, k], k == 0, k == KT - 1)
                last.then_inc(kh_ready, 1)
            pe.wait_ge(high, at["wq"])
            pe.wait_ge(low, at["wq"])
            queries(0, 0)
            queries(0, 1)
            pe.wait_ge(high, at["wout"])
            pe.wait_ge(low, at["wout"])
            for g in range(B // GB):
                out, keys = ps[0:GR, (5, 2)[g], :], slice(g * GR, (g + 1) * GR)
                for k in range(KT):
                    three(out, skv_h[:, k, keys], skv_l[:, k, keys], wout_h[:, k], wout_l[:, k], k == 0, False)
                pe.matmul(out, const[0:1, C_ONE:C_ONE + GR], rows[:, F:F + D * F], start=False, stop=True,
                          skip_group_check=True).then_inc(vo_ready, 1)
            additive(0)
            for b in range(B):
                if b == 0:
                    pe.wait_ge(qw_ready, 3)
                    pe.wait_ge(nzkv_ready, 4)
                pe.wait_ge(vo_hs, b // GB + 1)
                pe.wait_ge(vo_ls, b // GB + 1)
                if b >= 2:
                    pe.wait_ge(vo_masked, b - 1)
                out = ps[0:CR, (B6, B7)[b % 2], :]
                pe.matmul(out, gsel_r[0:GR, b % GB], vo_h[0:GR, b // GB], start=True, stop=False)
                pe.matmul(out, gsel_r[0:GR, b % GB], vo_l[0:GR, b // GB], start=False, stop=True)\
                    .then_inc(vo_spread, 1)
            pe.wait_ge(kh_copied, D * KT)
            scores(0, 0)
            own_features(0)
            scores(0, 1)
            pe.wait_ge(bw_ready, 2)
            pe.wait_ge(vo_masked, B)
            for k in range(KT):
                for s in range(2):
                    last = pe.transpose(ps[:, B7, (2 * k + s) * P:(2 * k + s + 1) * P], bw[:, s, k * P:(k + 1) * P],
                                        ident)
            last.then_inc(bwt_ready, 1)
            prob_transposes(0, 0)
            prob_transposes(0, 1)
            attend(0, 0)
            attend(0, 1)
            pe.wait_ge(s_wmod, 16)
            for j in range(NMOD):
                for k in range(KT):
                    last = pe.matmul(bank(B6, NMOD, B)[:, j], wmod[:, k, j * P:(j + 1) * P], condT[:, k, 0:B],
                                     start=k == 0, stop=k == KT - 1)
            last.then_inc(mod_ready, 1)
            pe.wait_ge(mod_copied, 1)
            pe.wait_ge(bwt_copied, 1)
            pe.wait_ge(cw_ready, 2)
            pe.wait_ge(high, at["w2"])
            pe.wait_ge(low_mlp, 2)
            with pe.Fori(0, B - 1) as i:
                both(i + 1, i)
            both(None, B - 1)

        @block.vector
        def _(dve):
            def nonzero(u):
                dve.wait_ge(row_sums, u + 1)
                dve.tensor_scalar(nz[0:64], ps[0:64, ROWS, 0:N], 0.0, const[0:64, bass.ds(u + C_BSEL, 1)],
                                  ALU.not_equal, ALU.mult).then_inc(nz_ready, 1)

            def features_low(u):
                dve.wait_ge(feat_h, u + 1)
                dve.tensor_tensor(sf_l[:], bank(FEAT, KT, N), f32(sf_h[:]), ALU.subtract).then_inc(feat_l, 1)

            def label_counts(u):
                dve.wait_ge(s_adj, 16 * u + 16)
                dve.tensor_reduce(count[:], adj[:], AX_X, ALU.add).then_inc(counted, 1)

            def label_biases(u):
                dve.wait_ge(counted, u + 1)
                dve.tensor_scalar(masked[:], count[:], 0.0, NEG, ALU.is_le, ALU.mult).then_inc(label_add, 1)
                dve.wait_ge(label_weighed, u + 1)
                dve.tensor_reduce(vbias[:], weighed[:], AX_X, ALU.add).then_inc(label_sums, 1)
                dve.wait_ge(label_sums, u + 1)
                dve.wait_ge(label_add, 2 * u + 1)
                dve.scalar_tensor_tensor(out=addv[:].rearrange("p t d m -> p (t d m)"), in0=vbias[:],
                                         scalar=bbias[:], in1=masked[:], op0=ALU.add, op1=ALU.add)\
                    .then_inc(label_add, 1)
                dve.wait_ge(label_add, 2 * u + 2)
                waited(dve, addt_ready, u)
                dve.tensor_copy(addn[:, :, :, 0:M].bitcast(F32R), addv[:]).then_inc(add_ready, 1)
                dve.wait_ge(add_ready, 2 * u + 1)
                dve.tensor_tensor(addn[:, :, :, M:2 * M].bitcast(F32R), addv[:], addn[:, :, :, 0:M],
                                  ALU.subtract).then_inc(add_ready, 1)

            def shift(u, t):
                dve.wait_ge(scored, NT * u + t + 1)
                s = ps[:, SCORE:SCORE + D, 0:HM].rearrange("p d (h m) -> p d h m", m=M)
                dve.tensor_reduce(smax[:, t].rearrange("p (d h) -> p d h", d=D), s, AX_X, ALU.max).then_inc(maxed, 1)
                dve.wait_ge(maxed, NT * u + t + 1)
                dve.tensor_tensor(soft[:, t].rearrange("p (d h) m -> p d h m", d=D), s,
                                  smax[:, t].rearrange("p (d h) -> p d h", d=D).unsqueeze(3)
                                  .broadcast_to([P, D, H, M]), ALU.subtract).then_inc(shifted_s, 1)

            def sums(u, t):
                dve.wait_ge(exped, NT * u + t + 1)
                dve.tensor_reduce(ssum[:, t], soft[:, t], AX_X, ALU.add).then_inc(summed, 1)
                dve.wait_ge(summed, NT * u + t + 1)
                dve.reciprocal(srec[:, t], ssum[:, t]).then_inc(inverted, 1)

            def residual(u):
                dve.wait_ge(attended, u + 1)
                dve.wait_ge(s_x, 16 * u + 16)
                dve.scalar_tensor_tensor(out=y[:], in0=bank(FEAT, NT, F), scalar=0.0, in1=x[:], op0=ALU.max,
                                         op1=ALU.add).then_inc(y_ready, 1)

            def statistics(u, n):
                v = (y, y2)[n]
                dve.wait_ge((y_ready, y2_ready)[n], u + 1)
                for t in range(NT):
                    dve.bn_stats(st[:, n, t], v[:, t]).then_inc(stats_s[n], 1)

            def aggregate(u, n, op):
                dve.wait_ge(stats_s[n], NT * u + NT)
                op()
                for t in range(NT):
                    dve.bn_aggr(mv[:, n, t], st[:, n, t]).then_inc(mv_s[n], 1)

            def normalize(u, n):
                v = (y, y2)[n]
                dve.wait_ge(mrs_s[n], u + 1)
                for t in range(NT):
                    dve.tensor_scalar(ln[:, n, t], v[:, t], rstd[:, n, t:t + 1], mrs[:, n, t:t + 1],
                                      ALU.mult, ALU.subtract).then_inc(ln_s[n], 1)

            def scan(u):
                dve.wait_ge(bu_ready, u + 1)
                dve.tensor_tensor(bu[:], bank(B7, 2, N), rot[:], ALU.mult).then_inc(bu_turned, 1)
                dve.wait_ge(bu_turned, u + 1)
                dve.tensor_tensor(zin[:], bu[:, 0], bu[:, 1], ALU.add).then_inc(zin_s, 1)
                dve.wait_ge(zin_s, u + 1)
                dve.tensor_tensor_scan(z[:], sc[:, 1:2].broadcast_to([P, N]), zin[:], 0.0, ALU.mult, ALU.add)\
                    .then_inc(z_s, 1)
                dve.wait_ge(z_s, u + 1)
                dve.tensor_tensor(cz[:], z[:].unsqueeze(1).broadcast_to([P, 2, N]), rot[:], ALU.mult)\
                    .then_inc(cz_s, 1)

            def gated(u):
                dve.wait_ge(c_ready, u + 1)
                dve.wait_ge(gdu_ready, u + 1)
                for k in range(KT):
                    dve.scalar_tensor_tensor(out=aT[:, k], in0=bank(B6, KT, N)[:, k], scalar=cur_a[:, 4 + k:5 + k],
                                             in1=gdu[:, k], op0=ALU.mult, op1=ALU.add).then_inc(a_ready, 1)

            def s5_residual(u):
                dve.wait_ge(at_ready, u + 1)
                dve.tensor_tensor(y2[:], bank(B7, NT, F), y[:], ALU.add).then_inc(y2_ready, 1)

            def mlp_parts(u):
                dve.wait_ge(m_ready, KT * u + KT)
                dve.tensor_copy(m_h[:], mt[:]).then_inc(m_hs, 1)
                dve.wait_ge(m_hs, u + 1)
                dve.tensor_tensor(m_l[:], mt[:], f32(m_h[:]), ALU.subtract).then_inc(m_ls, 1)

            def gelu_low(u, q):
                dve.wait_ge(gl_hs, FT // 2 * u + q + 1)
                two = slice(2 * q, 2 * q + 2)
                dve.tensor_tensor(gl_l[:, two], gl[:, two], f32(gl_h[:, two]), ALU.subtract).then_inc(gl_ls, 1)

            def result(u):
                dve.wait_ge(fft_ready, u + 1)
                dve.wait_ge(s_out, 16 * (GIVEN + u))
                dve.tensor_tensor(res[:], bank(B6, NT, F), y2[:], ALU.add).then_inc(res_ready, 1)

            def both(ua, ub):
                if ua is not None:
                    label_counts(ua)
                    nonzero(ua)
                    features_low(ua)
                scan(ub)
                if ua is not None:
                    label_biases(ua)
                    shift(ua, 0)
                gated(ub)
                if ua is not None:
                    shift(ua, 1)
                    sums(ua, 0)
                s5_residual(ub)
                statistics(ub, 1)
                aggregate(ub, 1, lambda: None if ua is None else sums(ua, 1))
                normalize(ub, 1)
                mlp_parts(ub)
                gelu_low(ub, 0)
                if ua is not None:
                    residual(ua)
                    statistics(ua, 0)
                    aggregate(ua, 0, lambda: gelu_low(ub, 1))
                else:
                    gelu_low(ub, 1)
                gelu_low(ub, 2)
                if ua is not None:
                    normalize(ua, 0)
                gelu_low(ub, 3)
                result(ub)

            def low_part(name):
                whole, part_h, part_l = parts[name]
                dve.wait_ge(high, at[name])
                dve.tensor_tensor(part_l[:], whole[:], f32(part_h[:]), ALU.subtract).then_inc(low, 1)

            step = stepper(dve, params_step)
            low_part("wself")
            low_part("xkv")
            dve.wait_ge(s_const, 16)
            dve.tensor_copy(ones_r[:], const[:, C_ONE:C_ONE + P]).then_inc(consts_r, 1)
            dve.tensor_copy(ident_r[:], ident).then_inc(consts_r, 1)
            dve.tensor_copy(rep_r[:].rearrange("p d k -> p (d k)"), const[:, C_REP:C_REP + D * HM]).then_inc(consts_r, 1)
            dve.tensor_copy(gsel_r[:].rearrange("p b k -> p (b k)"), const[:, C_GSEL:C_GSEL + GB * CR])\
                .then_inc(consts_r, 1)
            dve.wait_ge(cond_ready, 1)
            dve.tensor_copy(qw[:], bank(B6, F)).then_inc(qw_ready, 1)
            dve.wait_ge(qw_ready, 1)
            for r in (32, 96):
                dve.tensor_tensor(qw[r:r + 32], ps[r:r + 32, B6, 0:F], f32(qw[r:r + 32]), ALU.subtract)\
                    .then_inc(qw_ready, 1)
            bias_rows = const[64:P, C_BIASROW:C_BIASROW + 1]
            dve.tensor_copy(nz[64:P], bias_rows.broadcast_to([64, N])).then_inc(nzkv_ready, 1)
            dve.tensor_copy(nzkv[64:P], bias_rows.broadcast_to([64, KV])).then_inc(nzkv_ready, 1)
            dve.memset(f32(nz[0:64]), 0.0).then_inc(nzkv_ready, 1)
            dve.wait_ge(nzkv_ready, 3)
            dve.wait_ge(kv_sums, 1)
            dve.scalar_tensor_tensor(out=nzkv[0:64], in0=ps[0:64, B7, 0:KV], scalar=0.0,
                                     in1=const[0:64, C_KVSEL:C_KVSEL + KV], op0=ALU.not_equal, op1=ALU.mult)\
                .then_inc(nzkv_ready, 1)
            low_part("wk")
            nonzero(0)
            dve.wait_ge(skv_hs, 1)
            dve.tensor_tensor(skv_l[:], bank(SCORE, KT, KV), f32(skv_h[:]), ALU.subtract).then_inc(skv_ls, 1)
            low_part("wq")
            features_low(0)
            low_part("wout")
            label_counts(0)
            for g in range(B // GB):
                dve.wait_ge(vo_hs, g + 1)
                dve.tensor_tensor(vo_l[0:GR, g], ps[0:GR, (5, 2)[g], :], f32(vo_h[0:GR, g]), ALU.subtract)\
                    .then_inc(vo_ls, 1)
            dve.wait_ge(s_small, 16 * 6)
            label_biases(0)
            for b in range(B):
                dve.wait_ge(vo_spread, b + 1)
                dve.tensor_tensor(vo_all[0:CR, b].rearrange("p (d f) -> p d f", d=D),
                                  ps[0:CR, (B6, B7)[b % 2], :].rearrange("p (d f) -> p d f", d=D),
                                  const[0:CR, C_VMASK:C_VMASK + F].unsqueeze(1).broadcast_to([CR, D, F]),
                                  ALU.mult).then_inc(vo_masked, 1)
            shift(0, 0)
            sums(0, 0)
            shift(0, 1)
            sums(0, 1)
            residual(0)
            statistics(0, 0)
            aggregate(0, 0, lambda: None)
            normalize(0, 0)
            dve.wait_ge(mod_ready, 1)
            dve.tensor_tensor(mod[:], bank(B6, NMOD, B), bmod[:].unsqueeze(2).broadcast_to([P, NMOD, B]),
                              ALU.add).then_inc(mod_copied, 1)
            dve.wait_ge(mod_copied, 1)
            shift_a, scale_a, gate_a, shift_f, scale_f, gate_f, scale_c, shift_c = (
                mod[:, KT * j:KT * j + KT] for j in range(8))
            pa = [par_a[:, :, KT * j:KT * j + KT].rearrange("p b k -> p k b") for j in range(4)]
            pf = [par_f[:, :, KT * j:KT * j + KT].rearrange("p b k -> p k b") for j in range(4)]
            per_feature = lambda j: b12[:, j:j + KT].unsqueeze(2).broadcast_to([P, KT, B])
            step(dve.tensor_scalar(pa[0], scale_a, 1.0, None, ALU.add))
            step(dve.tensor_copy(pa[1], shift_a))
            step(dve.tensor_copy(pa[2], gate_a))
            step(dve.tensor_tensor(pa[3], gate_a, per_feature(FT + KT), ALU.mult))
            step(dve.tensor_scalar(pt[:, 0], scale_f, 1.0, None, ALU.add))
            step(dve.tensor_scalar(pt[:, 1], scale_c, 1.0, None, ALU.add))
            step(dve.tensor_tensor(pf[0], pt[:, 0], pt[:, 1], ALU.mult))
            step(dve.tensor_tensor(pt[:, 2], shift_c, pt[:, 0], ALU.mult))
            step(dve.tensor_tensor(pf[1], pt[:, 2], shift_f, ALU.add))
            step(dve.tensor_copy(pf[2], gate_f))
            step(dve.tensor_tensor(pf[3], gate_f, per_feature(FT), ALU.mult))
            with dve.Fori(0, B - 1) as i:
                both(i + 1, i)
            both(None, B - 1)


def kernel(x, cond_1024, mask_BxSxSx11_ik0, L0_cond_W_self, L0_cond_b_self, L0_cond_w_bias, L0_cond_b_bias,
           L0_cond_Wq, L0_cond_bq, L0_cond_Wk, L0_cond_bk, L0_cond_Wout, L0_cond_bout, L1_cond_Wm, L1_cond_bm,
           L1_cond_Lam_re, L1_cond_Lam_im, L1_cond_B_re, L1_cond_B_im, L1_cond_C_re, L1_cond_C_im,
           L1_cond_D_diag, L1_cond_log_step, L1_cond_Wc, L1_cond_bc, L1_cond_W1, L1_cond_b1, L1_cond_W2,
           L1_cond_b2):
    import concourse.bacc as bacc
    from concourse.bass_utils import run_bass_kernel_spmd

    def on_rows(a):
        a = np.asarray(a)
        return np.ascontiguousarray(a.reshape(a.shape[0] // P, P, -1).transpose(1, 0, 2))

    def columns(*vectors):
        return np.ascontiguousarray(np.concatenate([np.asarray(v).reshape(-1) for v in vectors]).reshape(-1, P).T)

    x = np.asarray(x)
    w_self = np.asarray(L0_cond_W_self)
    adj = np.asarray(mask_BxSxSx11_ik0)
    pairs = np.stack([adj[:, :, :M], adj[:, :M].transpose(0, 2, 1, 3)], axis=2)
    pairs = pairs.reshape(B, NT, P, D * M, L).transpose(0, 2, 1, 3, 4).reshape(B, P, NT * D * M, L)
    arrays = {
        "const": constants(),
        "x": x,
        "xT": np.ascontiguousarray(x.reshape(B, N, KT, P).transpose(0, 3, 2, 1)),
        "xkv": on_rows(x[:, :M].reshape(KV, F).T),
        "adj": np.ascontiguousarray(pairs),
        "wself": on_rows(w_self[:, :F].T),
        "wselfq": on_rows(w_self[:, F:].T),
        "condT": on_rows(np.asarray(cond_1024).T),
        "rows": np.concatenate([np.asarray(L0_cond_b_self), np.asarray(L0_cond_bout).reshape(-1)])[None],
        "wbias": np.asarray(L0_cond_w_bias)[None],
        "bbias": np.asarray(L0_cond_b_bias).reshape(1, 1),
        "wq": on_rows(np.asarray(L0_cond_Wq).reshape(D * F, F).T),
        "wk": on_rows(np.asarray(L0_cond_Wk).reshape(D * F, F).T),
        "bq": columns(L0_cond_bq),
        "bk": columns(L0_cond_bk),
        "wout": on_rows(np.asarray(L0_cond_Wout).reshape(D * F, F).T),
        "wmod": on_rows(np.concatenate([np.asarray(L1_cond_Wm), np.asarray(L1_cond_Wc)], axis=1)),
        "bmod": columns(L1_cond_bm, L1_cond_bc),
        "lam": np.stack([np.asarray(v) for v in (L1_cond_Lam_re, L1_cond_Lam_im, L1_cond_log_step)], axis=1),
        "b_ri": np.stack([np.asarray(L1_cond_B_re), np.asarray(L1_cond_B_im)]),
        "c_ri": np.stack([np.asarray(L1_cond_C_re).T, np.asarray(L1_cond_C_im).T]),
        "w1": on_rows(L1_cond_W1),
        "w2": on_rows(L1_cond_W2),
        "b12": columns(L1_cond_b1, L1_cond_b2, L1_cond_D_diag),
    }
    nc = bacc.Bacc("TRN2", target_bir_lowering=False, num_devices=1, dynamic_dma_scratch_size=1024)
    arrays = {f"in_{n}": np.ascontiguousarray(a) for n, a in arrays.items()}
    dram = {n[3:]: nc.dram_tensor(n, a.shape, mybir.dt.from_np(a.dtype), kind="ExternalInput").ap()
            for n, a in arrays.items()}
    dram["out"] = nc.dram_tensor("out", (B, N, F), F32, kind="ExternalOutput").ap()
    build(nc, dram)
    return run_bass_kernel_spmd(nc, [arrays], core_ids=[0]).results[0]["out"]
```

```python
from contextlib import ExitStack

import numpy as np

import concourse.bass as bass
from concourse import mybir

F32 = mybir.dt.float32
F32R = mybir.dt.float32r
I32 = mybir.dt.int32
ALU = mybir.AluOpType
ACT = mybir.ActivationFunctionType
AX_X = mybir.AxisListType.X

P = 128
B = 8
N = 256
F = 256
KT = F // P
NT = N // P
D = 2
H = 16
G = F // H
M = 20
L = 11
HM = H * M
HB = P // G
CH = 6
CR = CH * M
CHUNK_HEAD = (0, 6, 10)
CHUNK_COLS = ((0, 96), (96, 192), (192, 256))
NC = len(CHUNK_HEAD)
KV = B * M
GB = 4
GR = GB * M
S = 64
FF = 4 * F
FT = FF // P
NEG = -9000000000000000.0
EPS = 1e-5
ROUND = 12582912.0
TWO_PI = 6.283185307179586
LOG2E = 1.4426950408889634
LN2_H = 0.693359375
LN2_L = -2.12194440054690581e-4
PI2_H = 6.28125
PI2_M = 1.93500518798828125e-3
PI2_L = 3.0199159819567e-7
SIN_SCALE = 6.2831845

C_ID = 0
C_REP = C_ID + P
C_VMASK = C_REP + D * HM
C_KMASK = C_VMASK + F
C_BSEL = C_KMASK + HB
C_KVSEL = C_BSEL + B
C_GSEL = C_KVSEL + KV
C_TIME = C_GSEL + GB * CR
C_SIGN = C_TIME + N
C_ROW = C_SIGN + 1
C_ONE = C_ROW + P
C_BIASROW = C_ONE + P
C_END = C_BIASROW + 1


def constants():
    c = np.zeros((P, C_END), np.float32)
    c[:, C_ID:C_ID + P] = np.eye(P)
    rep = c[:, C_REP:C_REP + D * HM].reshape(P, D, H, M)
    for d in range(D):
        for m in range(M):
            rep[64 * d + m, d, :, m] = 1
            rep[64 * d + M + m, d, :, m] = 1
    for n, (lo, hi) in enumerate(CHUNK_COLS):
        for r in range(CR):
            h = CHUNK_HEAD[n] + r // M
            a, b = max(lo, h * G), min(hi, (h + 1) * G)
            if a < b:
                c[r, C_VMASK + a:C_VMASK + b] = 1
    for p in range(P):
        c[p, C_KMASK + p // G] = 0.25
    for b in range(B):
        for r in (b, 32 + b):
            c[r, C_BSEL + b] = 1
            c[r, C_KVSEL + b * M:C_KVSEL + (b + 1) * M] = 1
    gsel = c[:, C_GSEL:C_GSEL + GB * CR].reshape(P, GB, CH, M)
    for b in range(GB):
        for m in range(M):
            gsel[b * M + m, b, :, m] = 1
    c[:, C_TIME:C_TIME + N] = np.arange(N)
    c[:S, C_SIGN] = -1
    c[S:, C_SIGN] = 1
    c[0, C_ROW + 64] = c[0, C_ROW + 96] = 1
    c[:, C_ONE:C_ONE + P] = 1
    c[64, C_BIASROW] = c[96, C_BIASROW] = 1
    return c


def build(nc, dram):
    ctx = ExitStack()
    with ctx:
        def sb(name, shape, dt=F32):
            return ctx.enter_context(nc.sbuf_tensor(name, shape, dt))

        def sem(name):
            return ctx.enter_context(nc.semaphore(name))

        def f32(ap):
            return ap.bitcast(F32)

        const = sb("const", [P, C_END])
        ident = const[:, C_ID:C_ID + P]
        ident_r = sb("ident_r", [P, P], F32R)
        rep_r = sb("rep_r", [P, D, HM], F32R)
        gsel_r = sb("gsel_r", [P, GB, CR], F32R)
        ones_r = sb("ones_r", [P, P], F32R)
        stage = sb("stage", [P, 4, KT * D * F])
        wk, wq, wout = (stage[:, k].rearrange("p (k n) -> p k n", k=KT) for k in range(3))
        wself, wselfq = (stage[:, 3, k * KT * F:(k + 1) * KT * F].rearrange("p (k n) -> p k n", k=KT)
                         for k in range(2))
        w1 = stage[:, 0:2].rearrange("p a (b n) -> p (a b) n", n=FF)
        w2 = stage[:, 2:4].rearrange("p a (b n) -> p (a b) n", n=F)
        wself_h, wself_l = sb("wself_h", [P, KT, F], F32R), sb("wself_l", [P, KT, F], F32R)
        wq_h, wq_l = sb("wq_h", [P, KT, D * F], F32R), sb("wq_l", [P, KT, D * F], F32R)
        gl_h, gl_l = sb("gl_h", [P, FT, N], F32R), sb("gl_l", [P, FT, N], F32R)
        wk_h, wk_l, wout_h, wout_l = (g[:, k * FT // 2:(k + 1) * FT // 2].rearrange("p (k a) n -> p k (a n)", k=KT)
                                      for g in (gl_h, gl_l) for k in range(2))
        w1_h, w1_l = sb("w1_h", [P, KT, FF], F32R), sb("w1_l", [P, KT, FF], F32R)
        w2_h, w2_l = sb("w2_h", [P, FT, F], F32R), sb("w2_l", [P, FT, F], F32R)
        NMOD = 8 * KT
        late = sb("late", [P, KT * NMOD * P])
        wmod = late[:, :].rearrange("p (k n) -> p k n", k=KT)
        gl = late[:, 0:FT * N].rearrange("p (k n) -> p k n", n=N)
        aT, cz, ffT, y2 = (late[:, (FT + 2 * k) * N:(FT + 2 * k + 2) * N].rearrange("p (k n) -> p k n", n=N)
                           for k in range(4))
        condT = sb("condT", [P, KT, P])
        rows = sb("rows", [1, F + D * F])
        bq = sb("bq", [P, D * KT])
        bk = sb("bk", [P, D * KT])
        bmod = sb("bmod", [P, NMOD])
        b12 = sb("b12", [P, FT + 2 * KT])
        wbias = sb("wbias", [P, L])
        bbias = sb("bbias", [P, 1])
        xkv = sb("xkv", [P, KT, KV])
        xkv_h, xkv_l = sb("xkv_h", [P, KT, KV], F32R), sb("xkv_l", [P, KT, KV], F32R)
        nzkv = sb("nzkv", [P, KV], F32R)
        qw = sb("qw", [P, F], F32R)
        skv_h, skv_l = sb("skv_h", [P, KT, KV], F32R), sb("skv_l", [P, KT, KV], F32R)
        kh = sb("kh", [P, D * KT, KV])
        vo_h, vo_l = (w2_l[:, k * FT // 2:(k + 1) * FT // 2].rearrange("p (g a) n -> p g (a n)", g=B // GB)
                      for k in range(2))
        vo_all = sb("vo_all", [P, B, D * F])
        lam = sb("lam", [P, 3])
        sc = sb("sc", [P, 40])
        sci = sb("sci", [P, 1], I32)
        bri = sb("bri", [P, 2, F])
        bw = sb("bw", [P, 2, F])
        bt = sb("bt", [P, 3, F])
        bwT = sb("bwT", [P, KT, 2, P])
        cri = sb("cri", [P, 2, F])
        cw = sb("cw", [P, 2, F])
        rot = sb("rot", [P, 2, N])
        mod = sb("mod", [P, NMOD, B])
        par_a = sb("par_a", [P, B, 8])
        par_f = sb("par_f", [P, B, 8])
        pt = sb("pt", [P, 4, KT, B])
        xT = sb("xT", [P, KT, N])
        x = sb("x", [P, NT, F])
        adj = sb("adj", [P, NT * D * M, L], I32)
        x_h, x_l = sb("x_h", [P, KT, N], F32R), sb("x_l", [P, KT, N], F32R)
        nz = sb("nz", [P, N], F32R)
        sf_h, sf_l = sb("sf_h", [P, KT, N], F32R), sb("sf_l", [P, KT, N], F32R)
        qT = sb("qT", [P, D, KT, N])
        count = sb("count", [P, NT * D * M])
        weighed = sb("weighed", [P, NT * D * M, L])
        vbias = sb("vbias", [P, NT * D * M])
        masked = sb("masked", [P, NT * D * M])
        addv = sb("addv", [P, NT, D, M])
        addn = sb("addn", [P, NT, D, 64])
        addT = sb("addT", [P, NT, P], F32R)
        kbd = sb("kbd", [P, D * KT, HB, M])
        vbd = sb("vbd", [P, D, F])
        smax = sb("smax", [P, NT, D * H])
        soft = sb("soft", [P, NT, D * H, M])
        ssum = sb("ssum", [P, NT, D * H])
        srec = sb("srec", [P, NT, D * H])
        pT = sb("pT", [P, NT, D, NC * P])
        tb = pT[:, :, :, :].rearrange("p t d (a n) -> p (t d a) n", n=P).rearrange("p (a b) n -> p a (b n)", b=2)
        y = sb("y", [P, NT, F])
        cur_a = sb("cur_a", [P, 8])
        cur_f = sb("cur_f", [P, 4])
        cur_g = sb("cur_g", [P, 4])
        st = sb("st", [P, 2, NT, 6])
        mv = sb("mv", [P, 2, NT, 2])
        rstd = sb("rstd", [P, 2, NT])
        veps = sb("veps", [P, 2, NT])
        half, eps = sb("half", [P, NT]), sb("eps", [P, NT])
        mrs = sb("mrs", [P, 2, NT])
        ln = sb("ln", [P, 2, NT, F])
        y2_kept = sb("y2_kept", [P, NT, F])
        uT = sb("uT", [P, KT, N])
        gdu = sb("gdu", [P, KT, N])
        bu = sb("bu", [P, 2, N])
        zin = sb("zin", [P, N])
        z = sb("z", [P, N])
        mt = sb("mt", [P, KT, N])
        m_h, m_l = sb("m_h", [P, KT, N], F32R), sb("m_l", [P, KT, N], F32R)
        res = sb("res", [P, NT, F])

        ps = ctx.enter_context(nc.psum_tensor("ps", [P, 8, 512], F32))
        ROWS, FEAT, SCORE, PROB, B6, B7 = 0, 1, 2, 4, 6, 7

        def bank(n, *dims):
            size = int(np.prod(dims))
            return ps[:, n, 0:size] if len(dims) == 1 else ps[:, n, 0:size].rearrange(
                "p (a b) -> p a b", a=dims[0])

        s_const, s_wselfq, s_rows, s_small, s_lam, s_bri, s_cri, s_wmod = (sem(n) for n in (
            "const_loaded", "wselfq_loaded", "rows_loaded", "small_loaded", "lam_loaded", "b_loaded",
            "c_loaded", "wmod_loaded"))
        s_cond = sem("cond_loaded")
        split_order = ("wself", "xkv", "wk", "wq", "wout", "w1", "w2")
        loaded = {n: sem(n + "_loaded") for n in split_order}
        high = sem("high_parts")
        low, low_mlp = sem("low_parts"), sem("low_parts_mlp")
        at = {n: k + 1 for k, n in enumerate(split_order)}
        parts = {"wself": (wself, wself_h, wself_l), "xkv": (xkv, xkv_h, xkv_l), "wk": (wk, wk_h, wk_l),
                 "wq": (wq, wq_h, wq_l), "wout": (wout, wout_h, wout_l), "w1": (w1, w1_h, w1_l),
                 "w2": (w2, w2_h, w2_l)}
        cleared, consts_r, cond_ready, qw_ready, kv_sums, nzkv_ready = (sem(n) for n in (
            "cleared", "consts_rounded", "cond_part_ready", "qw_ready", "kv_sums", "nzkv_ready"))
        skv_ready, skv_hs, skv_ls, kh_ready, kh_copied = (sem(n) for n in (
            "skv_ready", "skv_h_ready", "skv_l_ready", "kh_ready", "kh_copied"))
        vo_ready, vo_hs, vo_ls, vo_spread, vo_masked = (sem(n) for n in (
            "vo_ready", "vo_h_ready", "vo_l_ready", "vo_spread", "vo_masked"))
        mod_ready, mod_copied, params_step = sem("mod_ready"), sem("mod_copied"), sem("params_ready")
        s5_step, turns, rot_ready, bw_ready, cw_ready, bwt_ready, bwt_copied = (sem(n) for n in (
            "s5_step", "turns_ready", "rot_ready", "bw_ready", "cw_ready", "bwt_ready", "bwt_copied"))

        s_xT, s_x, s_adj, s_out = (sem(n) for n in ("xT_loaded", "x_loaded", "adj_loaded", "out_stored"))
        x_high, x_low = sem("x_high"), sem("x_low")
        row_sums, nz_ready, feat_ready, feat_h, feat_l = (sem(n) for n in (
            "row_sums", "nz_ready", "feat_ready", "feat_h_ready", "feat_l_ready"))
        q_ready, q_copied = sem("q_ready"), sem("q_copied")
        label_floats = sem("label_floats")
        counted, label_weighed, label_sums, label_add, add_ready, addt_ready, addt_copied = (sem(n) for n in (
            "counted", "label_weighed", "label_sums", "label_add", "add_ready", "addt_ready", "addt_copied"))
        kbd_ready, vbd_ready = sem("kbd_ready"), sem("vbd_ready")
        scored, maxed, shifted_s, exped, summed, inverted, probs_ready = (sem(n) for n in (
            "scored", "maxed", "shifted_ready", "exped", "summed", "inverted", "probs_ready"))
        pt_ready, pt_copied, attended, y_ready = (sem(n) for n in (
            "pt_ready", "pt_copied", "attended", "y_ready"))
        cur_a_s, cur_f_s, cur_g_s = sem("cur_a_ready"), sem("cur_f_ready"), sem("cur_g_ready")
        stats_s, mv_s, veps_s, rstd_s, mrs_s, ln_s, lnt_ready = ([sem(f"{n}_{k}") for k in range(2)] for n in (
            "stats_ready", "mean_var_ready", "var_eps_ready", "rstd_ready", "mean_rstd_ready", "ln_ready",
            "lnt_ready"))
        u_ready, gdu_ready, bu_ready, bu_turned, zin_s, z_s, cz_s, c_ready, a_ready, at_ready = (sem(n) for n in (
            "u_ready", "gdu_ready", "bu_ready", "bu_turned", "scan_input", "scanned", "z_turned",
            "c_ready", "a_ready", "at_ready"))
        y2_ready, y2_copied, m_ready, m_hs, m_ls, h_ready, gelu_s, gl_hs, gl_ls = (sem(n) for n in (
            "y2_ready", "y2_copied", "m_ready", "m_h_ready", "m_l_ready", "h_ready", "gelu_done", "gelu_h_ready",
            "gelu_l_ready"))
        ff_ready, ff_copied, fft_ready, res_ready = (sem(n) for n in (
            "ff_ready", "ff_copied", "fft_ready", "res_ready"))

        block = ctx.enter_context(nc.Block())

        GIVEN = 1

        def waited(eng, signal, value):
            if not (isinstance(value, int) and value <= 0):
                eng.wait_ge(signal, value)

        def stepper(eng, chain):
            count = {}

            def step(ins, signal=chain):
                count[signal.name] = count.get(signal.name, 0) + 1
                ins.then_inc(signal, 1)
                eng.wait_ge(signal, count[signal.name])
            return step

        def all_turns(eng, turn):
            turn(2, 1, 0, None)
            with eng.Fori(0, B - 3) as i:
                turn(i + 3, i + 2, i + 1, i)
            turn(None, B - 1, B - 2, B - 3)
            turn(None, None, B - 1, B - 2)
            turn(None, None, None, B - 1)

        @block.sync
        def _(sp):
            def load_xT(u):
                waited(sp, x_low, u)
                sp.dma_start(xT[:], dram["xT"][bass.ds(u, 1)].rearrange("b p k n -> (b p) k n")).then_inc(s_xT, 16)

            def load_adj(u):
                waited(sp, counted, u)
                waited(sp, label_floats, u)
                sp.dma_start(adj[:], dram["adj"][bass.ds(u, 1)].rearrange("b p t l -> (b p) t l")).then_inc(s_adj, 16)

            def load_x(u):
                waited(sp, y_ready, u)
                sp.dma_start(x[:], dram["x"][bass.ds(u, 1)].rearrange("b (t p) f -> p (b t) f", p=P)).then_inc(s_x, 16)

            def store(u):
                sp.wait_ge(res_ready, GIVEN + u + 1)
                sp.dma_start(dram["out"][bass.ds(u, 1)].rearrange("b (t p) f -> p (b t) f", p=P), res[:]).then_inc(s_out, 16)

            for signal, count in ((ff_copied, KT), (ff_ready, KT), (res_ready, 1), (s_out, 16)):
                sp.sem_inc(signal, GIVEN * count)
            for name in ("wself", "xkv", "wk"):
                sp.dma_start(parts[name][0][:], dram[name]).then_inc(loaded[name], 16)
            load_xT(0)
            sp.dma_start(const[:], dram["const"]).then_inc(s_const, 16)
            for name in ("wq", "wout"):
                sp.dma_start(parts[name][0][:], dram[name]).then_inc(loaded[name], 16)
            load_adj(0)
            load_x(0)
            sp.dma_start(wmod[:], dram["wmod"]).then_inc(s_wmod, 16)
            for name, before in (("w1", "wq"), ("w2", "wout")):
                sp.wait_ge(low, at[before])
                if name == "w2":
                    sp.wait_ge(cond_ready, 1)
                sp.dma_start(parts[name][0][:], dram[name]).then_inc(loaded[name], 16)
            load_xT(1)
            load_adj(1)
            for u in (1, 2):
                load_xT(u + 1)
                load_adj(u + 1)
                load_x(u)
            with sp.Fori(0, B - 4) as i:
                load_xT(i + 4)
                load_adj(i + 4)
                load_x(i + 3)
                store(i)
            load_x(B - 1)
            for u in range(B - 4, B):
                store(u)
            sp.wait_ge(s_out, 16 * (GIVEN + B))

        @block.gpsimd
        def _(pool):
            step = stepper(pool, s5_step)

            def exp_steps(out, v, t):
                n, r, q, w = (sc[:, t + k:t + k + 1] for k in range(4))
                step(pool.tensor_scalar(q, v, -87.0, 88.0, ALU.max, ALU.min))
                step(pool.tensor_scalar(n, q, LOG2E, ROUND, ALU.mult, ALU.add))
                step(pool.tensor_scalar(n, n, ROUND, None, ALU.subtract))
                step(pool.tensor_scalar(w, n, LN2_H, None, ALU.mult))
                step(pool.tensor_tensor(r, q, w, ALU.subtract))
                step(pool.tensor_scalar(w, n, LN2_L, None, ALU.mult))
                step(pool.tensor_tensor(r, r, w, ALU.subtract))
                step(pool.tensor_scalar(q, r, 1.0 / 5040, 1.0 / 720, ALU.mult, ALU.add))
                for c in (1.0 / 120, 1.0 / 24, 1.0 / 6, 0.5, 1.0, 1.0):
                    step(pool.tensor_scalar(q, q, r, c, ALU.mult, ALU.add))
                step(pool.tensor_scalar(sci[:], n, 127.0, 8388608.0, ALU.add, ALU.mult))
                step(pool.tensor_tensor(out, q, sci[:].bitcast(F32), ALU.mult))

            def x_parts(u):
                pool.wait_ge(x_high, u + 1)
                pool.tensor_tensor(x_l[:], xT[:], f32(x_h[:]), ALU.subtract).then_inc(x_low, 1)

            def label_weights(u):
                pool.wait_ge(label_floats, u + 1)
                pool.tensor_tensor(weighed[:], weighed[:], wbias[:].unsqueeze(1).broadcast_to([P, NT * D * M, L]),
                                   ALU.mult).then_inc(label_weighed, 1)

            def key_blocks(u):
                waited(pool, scored, NT * u)
                keys = kh[:, :, bass.ds(u * M, M)]
                pool.tensor_tensor(kbd[:], keys.unsqueeze(2).broadcast_to([P, D * KT, HB, M]),
                                   const[:, C_KMASK:C_KMASK + HB].unsqueeze(1).unsqueeze(3)
                                   .broadcast_to([P, D * KT, HB, M]), ALU.mult).then_inc(kbd_ready, 1)

            def value_blocks(u):
                waited(pool, attended, u)
                pool.tensor_copy(vbd[0:CR, :, :].rearrange("p d f -> p (d f)"),
                                 vo_all[0:CR, bass.ds(u, 1), :].rearrange("p b f -> p (b f)")).then_inc(vbd_ready, 1)

            def probabilities(u, t):
                pool.wait_ge(inverted, NT * u + t + 1)
                pool.tensor_tensor(soft[:, t], soft[:, t], srec[:, t].unsqueeze(2).broadcast_to([P, D * H, M]),
                                   ALU.mult).then_inc(probs_ready, 1)

            def rstd_of(u, k):
                pool.wait_ge(mv_s[k], NT * u + NT)
                pool.tensor_tensor(veps[:, k], mv[:, k, :, 1], eps[:], ALU.add).then_inc(veps_s[k], 1)
                pool.wait_ge(veps_s[k], u + 1)
                pool.tensor_tensor(rstd[:, k], veps[:, k], half[:], ALU.pow).then_inc(rstd_s[k], 1)
                pool.wait_ge(rstd_s[k], u + 1)
                pool.tensor_tensor(mrs[:, k], mv[:, k, :, 0], rstd[:, k], ALU.mult).then_inc(mrs_s[k], 1)

            def take_s5_params(u):
                waited(pool, a_ready, KT * u)
                pool.tensor_copy(cur_a[:], par_a[:, bass.ds(u, 1), :].rearrange("p b k -> p (b k)")).then_inc(cur_a_s, 1)

            def take_mlp_params(u):
                waited(pool, m_ready, KT * u)
                pool.tensor_copy(cur_f[:], par_f[:, bass.ds(u, 1), 0:4].rearrange("p b k -> p (b k)")).then_inc(cur_f_s, 1)

            def take_gate(u):
                pool.wait_ge(ff_copied, KT * (GIVEN + u))
                pool.tensor_copy(cur_g[:], par_f[:, bass.ds(u, 1), 4:8].rearrange("p b k -> p (b k)")).then_inc(cur_g_s, 1)

            def skip_term(u):
                pool.wait_ge(u_ready, KT * u + KT)
                pool.tensor_tensor(gdu[:], uT[:], cur_a[:, 6:6 + KT].unsqueeze(2).broadcast_to([P, KT, N]), ALU.mult)\
                    .then_inc(gdu_ready, 1)

            def mlp_low_part(name):
                whole, part_h, part_l = parts[name]
                pool.wait_ge(high, at[name])
                pool.tensor_tensor(part_l[:], whole[:], f32(part_h[:]), ALU.subtract).then_inc(low_mlp, 1)

            def turn(un, ua, ub, uc):
                if ub is not None:
                    take_s5_params(ub)
                    take_mlp_params(ub)
                if uc is not None:
                    take_gate(uc)
                if ua is not None:
                    label_weights(ua)
                    key_blocks(ua)
                if ub is not None:
                    skip_term(ub)
                if ua is not None:
                    value_blocks(ua)
                if uc is None:
                    mlp_low_part("w1")
                if ua is not None:
                    probabilities(ua, 0)
                if un is not None:
                    x_parts(un)
                if ua is not None:
                    probabilities(ua, 1)
                if ub is not None:
                    rstd_of(ub, 1)
                if ua is not None:
                    rstd_of(ua, 0)
                if uc is None:
                    mlp_low_part("w2")

            step(pool.memset(condT[:], 0.0), cleared)
            step(pool.memset(addn[:], 0.0), cleared)
            step(pool.memset(half[:], -0.5), cleared)
            step(pool.memset(eps[:], EPS), cleared)
            x_parts(0)

            v = lambda k: sc[:, k:k + 1]
            lr, li, ls = lam[:, 0:1], lam[:, 1:2], lam[:, 2:3]
            dt, a, th, n, r, w = v(0), v(1), v(2), v(3), v(4), v(5)
            sign = const[:, C_SIGN:C_SIGN + 1]
            pool.wait_ge(s_lam, 32)
            exp_steps(dt, ls, 10)
            step(pool.tensor_tensor(a, lr, dt, ALU.mult))
            exp_steps(a, a, 10)
            step(pool.tensor_tensor(th, li, dt, ALU.mult))
            step(pool.tensor_scalar(n, th, 1.0 / TWO_PI, ROUND, ALU.mult, ALU.add))
            step(pool.tensor_scalar(n, n, ROUND, None, ALU.subtract))
            for part in (PI2_H, PI2_M, PI2_L):
                step(pool.tensor_scalar(w, n, part, None, ALU.mult))
                step(pool.tensor_tensor(th, th, w, ALU.subtract))
            fh, fl = v(6), v(7)
            step(pool.tensor_scalar(r, th, 1.0 / TWO_PI, None, ALU.mult))
            step(pool.tensor_scalar(fh, r, 4096.0, ROUND, ALU.mult, ALU.add))
            step(pool.tensor_scalar(fh, fh, ROUND, 1.0 / 4096, ALU.subtract, ALU.mult))
            step(pool.tensor_tensor(fl, r, fh, ALU.subtract))
            pool.wait_ge(s_const, 16)
            time = const[:, C_TIME:C_TIME + N]
            T = lambda k: tb[:, k, :]
            step(pool.tensor_scalar(T(0), time, fh, None, ALU.mult))
            step(pool.tensor_scalar(T(1), T(0), ROUND, ROUND, ALU.add, ALU.subtract))
            step(pool.tensor_tensor(T(0), T(0), T(1), ALU.subtract))
            step(pool.tensor_scalar(T(2), time, fl, None, ALU.mult))
            step(pool.tensor_tensor(T(0), T(0), T(2), ALU.add))
            step(pool.tensor_scalar(T(3), T(0), 0.25, None, ALU.add))
            step(pool.tensor_scalar(T(1), T(0), ROUND, ROUND, ALU.add, ALU.subtract))
            step(pool.tensor_scalar(T(2), T(3), ROUND, ROUND, ALU.add, ALU.subtract))
            step(pool.tensor_tensor(T(4), T(3), T(2), ALU.subtract), turns)
            step(pool.tensor_tensor(T(5), T(0), T(1), ALU.subtract), turns)
            pool.wait_ge(kh_copied, D * KT)
            key_blocks(0)
            pool.wait_ge(s_small, 16 * 6)
            label_weights(0)
            pool.wait_ge(rot_ready, 2)
            cs, sn = rot[:, 0, 1:2], rot[:, 1, 1:2]
            nr, ni, den, kr, ki, e = v(20), v(21), v(22), v(23), v(24), v(25)
            kis, krs, c2 = v(26), v(27), v(28)
            step(pool.tensor_tensor(nr, a, cs, ALU.mult))
            step(pool.tensor_scalar(nr, nr, 1.0, None, ALU.subtract))
            step(pool.tensor_tensor(ni, a, sn, ALU.mult))
            step(pool.tensor_tensor(den, lr, lr, ALU.mult))
            step(pool.tensor_tensor(e, li, li, ALU.mult))
            step(pool.tensor_tensor(den, den, e, ALU.add))
            step(pool.tensor_tensor(kr, nr, lr, ALU.mult))
            step(pool.tensor_tensor(e, ni, li, ALU.mult))
            step(pool.tensor_tensor(kr, kr, e, ALU.add))
            step(pool.tensor_tensor(ki, ni, lr, ALU.mult))
            step(pool.tensor_tensor(e, nr, li, ALU.mult))
            step(pool.tensor_tensor(ki, ki, e, ALU.subtract))
            step(pool.memset(c2, -1.0))
            step(pool.tensor_tensor(den, den, c2, ALU.pow))
            step(pool.tensor_tensor(kr, kr, den, ALU.mult))
            step(pool.tensor_tensor(ki, ki, den, ALU.mult))
            step(pool.tensor_tensor(kis, ki, sign, ALU.mult))
            step(pool.tensor_tensor(krs, kr, sign, ALU.mult))
            step(pool.tensor_scalar(krs, krs, -1.0, None, ALU.mult))
            pool.wait_ge(s_bri, 64)
            step(pool.tensor_scalar(bt[:, 0], bri[:, 0], kr, None, ALU.mult))
            step(pool.tensor_scalar(bt[:, 1], bri[:, 1], kis, None, ALU.mult))
            step(pool.tensor_tensor(bw[:, 0], bt[:, 0], bt[:, 1], ALU.add), bw_ready)
            step(pool.tensor_scalar(bt[:, 2], bri[:, 0], ki, None, ALU.mult))
            step(pool.tensor_scalar(bt[:, 1], bri[:, 1], krs, None, ALU.mult))
            step(pool.tensor_tensor(bw[:, 1], bt[:, 2], bt[:, 1], ALU.add), bw_ready)
            pool.wait_ge(s_cri, 64)
            step(pool.tensor_scalar(cw[:, 0], cri[:, 0], sign, -2.0, ALU.mult, ALU.mult), cw_ready)
            step(pool.tensor_scalar(cw[:, 1], cri[:, 1], -2.0, None, ALU.mult), cw_ready)
            pool.wait_ge(vo_masked, B)
            value_blocks(0)
            probabilities(0, 0)
            probabilities(0, 1)
            rstd_of(0, 0)
            x_parts(1)
            pool.wait_ge(params_step, 11)
            all_turns(pool, turn)

        @block.scalar
        def _(act):
            def tokens_high(u):
                act.wait_ge(s_xT, 16 * u + 16)
                waited(act, feat_ready, u)
                act.activation(x_h[:], xT[:], ACT.Copy).then_inc(x_high, 1)

            def label_float(u):
                act.wait_ge(s_adj, 16 * u + 16)
                waited(act, label_sums, u)
                act.activation(weighed[:], adj[:], ACT.Copy).then_inc(label_floats, 1)

            def features_high(u):
                act.wait_ge(feat_ready, u + 1)
                act.activation(sf_h[:], bank(FEAT, KT, N), ACT.Copy).then_inc(feat_h, 1)

            def queries(u, d):
                act.wait_ge(q_ready, D * u + d + 1)
                for k in range(KT):
                    act.activation(qT[:, d, k], bank(ROWS + d, KT, N)[:, k], ACT.Identity,
                                   bias=bq[:, d * KT + k:d * KT + k + 1]).then_inc(q_copied, 1)

            def additive(u):
                act.wait_ge(addt_ready, u + 1)
                act.activation(addT[:], bank(PROB + 1, NT, P), ACT.Copy).then_inc(addt_copied, 1)

            def exponentials(u, t):
                act.wait_ge(shifted_s, NT * u + t + 1)
                act.activation(soft[:, t], soft[:, t], ACT.Exp).then_inc(exped, 1)

            def transposed(u, t):
                act.wait_ge(pt_ready, NT * u + t + 1)
                act.activation(pT[0:CR, t], ps[0:CR, PROB:PROB + D, 0:NC * P], ACT.Copy).then_inc(pt_copied, 1)

            def s5_input(u):
                act.wait_ge(lnt_ready[0], u + 1)
                act.wait_ge(cur_a_s, u + 1)
                for k in range(KT):
                    act.activation(uT[:, k], bank(B6, KT, N)[:, k], ACT.Identity, bias=cur_a[:, 2 + k:3 + k],
                                   scale=cur_a[:, k:k + 1]).then_inc(u_ready, 1)

            def mlp_input(u):
                act.wait_ge(lnt_ready[1], u + 1)
                act.wait_ge(cur_f_s, u + 1)
                waited(act, m_ls, u)
                for k in range(KT):
                    act.activation(mt[:, k], bank(B6, KT, N)[:, k], ACT.Identity, bias=cur_f[:, 2 + k:3 + k],
                                   scale=cur_f[:, k:k + 1]).then_inc(m_ready, 1)

            def gelus(u, q):
                act.wait_ge(h_ready, FT // 2 * u + q + 1)
                if q == 0:
                    act.wait_ge(ff_ready, KT * (GIVEN + u))
                for k in (2 * q, 2 * q + 1):
                    act.activation(gl[:, k], bank((PROB, B7)[q % 2], 2, N)[:, k % 2], ACT.Gelu_apprx_tanh,
                                   bias=b12[:, k:k + 1]).then_inc(gelu_s, 1)
                act.wait_ge(gelu_s, FT * u + 2 * q + 2)
                act.activation(gl_h[:, 2 * q:2 * q + 2], gl[:, 2 * q:2 * q + 2], ACT.Copy).then_inc(gl_hs, 1)

            def mlp_output(u):
                act.wait_ge(cur_g_s, u + 1)
                for k in range(KT):
                    act.wait_ge(ff_ready, KT * (GIVEN + u) + k + 1)
                    act.activation(ffT[:, k], ps[:, (B7, SCORE)[k], 0:N], ACT.Identity, bias=cur_g[:, 2 + k:3 + k],
                                   scale=cur_g[:, k:k + 1]).then_inc(ff_copied, 1)

            def keep_y2(u):
                act.wait_ge(y2_ready, u + 1)
                act.wait_ge(res_ready, GIVEN + u)
                act.activation(y2_kept[:], y2[:], ACT.Copy).then_inc(y2_copied, 1)

            def turn(un, ua, ub, uc):
                if uc is not None:
                    gelus(uc, 0)
                if ua is not None:
                    features_high(ua)
                if ub is not None:
                    s5_input(ub)
                if uc is not None:
                    gelus(uc, 1)
                    keep_y2(uc)
                if ua is not None:
                    queries(ua, 0)
                    queries(ua, 1)
                if uc is not None:
                    gelus(uc, 2)
                else:
                    high_part("w1")
                if ua is not None:
                    additive(ua)
                if uc is not None:
                    gelus(uc, 3)
                if ua is not None:
                    exponentials(ua, 0)
                if un is not None:
                    label_float(un)
                    tokens_high(un)
                if ua is not None:
                    exponentials(ua, 1)
                    transposed(ua, 0)
                    transposed(ua, 1)
                if ub is not None:
                    mlp_input(ub)
                if uc is not None:
                    mlp_output(uc)
                else:
                    high_part("w2")

            def high_part(name):
                whole, part_h, _ = parts[name]
                act.wait_ge(loaded[name], 16)
                act.activation(part_h[:], whole[:], ACT.Copy).then_inc(high, 1)

            act.dma_start(wselfq[:], dram["wselfq"]).then_inc(s_wselfq, 16)
            act.wait_ge(cleared, 1)
            act.dma_start(condT[:, :, 0:B], dram["condT"]).then_inc(s_cond, 16)
            act.dma_start(condT[:, :, 32:32 + B], dram["condT"]).then_inc(s_cond, 16)
            act.dma_start(rows[:], dram["rows"]).then_inc(s_rows, 16)
            for h in range(2):
                act.dma_start(lam[h * S:(h + 1) * S, :], dram["lam"]).then_inc(s_lam, 16)
            act.dma_start(bk[:], dram["bk"]).then_inc(s_small, 16)
            act.dma_start(bq[:], dram["bq"]).then_inc(s_small, 16)
            act.dma_start(wbias[:], dram["wbias"].broadcast_to([P, L])).then_inc(s_small, 16)
            act.dma_start(bbias[:], dram["bbias"].broadcast_to([P, 1])).then_inc(s_small, 16)
            act.dma_start(bmod[:], dram["bmod"]).then_inc(s_small, 16)
            act.dma_start(b12[:], dram["b12"]).then_inc(s_small, 16)
            high_part("wself")
            high_part("xkv")
            high_part("wk")
            tokens_high(0)
            for h in range(2):
                act.dma_start(bri[h * S:(h + 1) * S, 0, :], dram["b_ri"][h]).then_inc(s_bri, 16)
                act.dma_start(bri[h * S:(h + 1) * S, 1, :], dram["b_ri"][1 - h]).then_inc(s_bri, 16)
                act.dma_start(cri[h * S:(h + 1) * S, 0, :], dram["c_ri"][h]).then_inc(s_cri, 16)
                act.dma_start(cri[h * S:(h + 1) * S, 1, :], dram["c_ri"][1 - h]).then_inc(s_cri, 16)
            act.wait_ge(skv_ready, 1)
            act.activation(skv_h[:], bank(SCORE, KT, KV), ACT.Copy).then_inc(skv_hs, 1)
            high_part("wq")
            act.wait_ge(s_small, 16 * 6)
            for d in range(D):
                act.wait_ge(kh_ready, d + 1)
                for k in range(KT):
                    act.activation(kh[:, d * KT + k], bank(SCORE + 1 + d, KT, KV)[:, k], ACT.Identity,
                                   bias=bk[:, d * KT + k:d * KT + k + 1]).then_inc(kh_copied, 1)
            high_part("wout")
            features_high(0)
            label_float(0)
            queries(0, 0)
            queries(0, 1)
            for g in range(B // GB):
                act.wait_ge(vo_ready, g + 1)
                act.activation(vo_h[0:GR, g], ps[0:GR, (PROB, SCORE)[g], :], ACT.Copy).then_inc(vo_hs, 1)
            additive(0)
            act.wait_ge(turns, 2)
            for k in range(2):
                act.activation(rot[:, k], tb[:, 4 + k, :], ACT.Sin, scale=SIN_SCALE).then_inc(rot_ready, 1)
            exponentials(0, 0)
            exponentials(0, 1)
            act.wait_ge(bwt_ready, 1)
            act.activation(bwT[:].rearrange("p k s q -> p (k s q)"), ps[:, 7, :], ACT.Copy).then_inc(bwt_copied, 1)
            transposed(0, 0)
            transposed(0, 1)
            tokens_high(1)
            label_float(1)
            all_turns(act, turn)

        @block.tensor
        def _(pe):
            def three(out, wh, wl, xh, xl, first, last):
                pe.matmul(out, wh, xh, start=first, stop=False, skip_group_check=True)
                pe.matmul(out, wh, xl, start=False, stop=False, skip_group_check=True)
                return pe.matmul(out, wl, xh, start=False, stop=last, skip_group_check=True)

            def rowsums(u):
                pe.wait_ge(x_high, u + 1)
                pe.wait_ge(x_low, u + 1)
                waited(pe, q_copied, D * KT * u)
                for k in range(KT):
                    for part in (x_h, x_l):
                        last = pe.matmul(bank(ROWS, N), ones_r[:], part[:, k], start=k == 0 and part is x_h,
                                         stop=k == KT - 1 and part is x_l)
                last.then_inc(row_sums, 1)

            def features(u):
                waited(pe, y_ready, u)
                for f in range(KT):
                    out, cols = bank(FEAT, KT, N)[:, f], slice(f * P, (f + 1) * P)
                    for k in range(KT):
                        three(out, wself_h[:, k, cols], wself_l[:, k, cols], x_h[:, k], x_l[:, k], k == 0, False)
                    if f == 0:
                        pe.wait_ge(nz_ready, u + 1)
                    last = pe.matmul(out, qw[:, cols], nz[:], start=False, stop=True, skip_group_check=True)
                last.then_inc(feat_ready, 1)

            def queries(u, d):
                if d == 0:
                    pe.wait_ge(feat_h, u + 1)
                    pe.wait_ge(feat_l, u + 1)
                for f in range(KT):
                    cols = slice(d * F + f * P, d * F + (f + 1) * P)
                    for k in range(KT):
                        last = three(bank(ROWS + d, KT, N)[:, f], wq_h[:, k, cols], wq_l[:, k, cols],
                                     sf_h[:, k], sf_l[:, k], k == 0, k == KT - 1)
                last.then_inc(q_ready, 1)

            def additive(u):
                pe.wait_ge(add_ready, 2 * u + 2)
                waited(pe, pt_copied, NT * u)
                for t in range(NT):
                    last = pe.transpose(bank(PROB + 1, NT, P)[:, t], addn[:, t].rearrange("p d m -> p (d m)"), ident)
                last.then_inc(addt_ready, 1)

            def scores(u, t):
                if t == 0:
                    pe.wait_ge(kbd_ready, u + 1)
                    pe.wait_ge(q_copied, D * KT * (u + 1))
                    pe.wait_ge(addt_copied, u + 1)
                rows_t = slice(t * P, (t + 1) * P)
                for d in range(D):
                    out = ps[:, (SCORE, ROWS)[t] + d, 0:HM]
                    pe.matmul(out, addT[:, t], rep_r[:, d], start=True, stop=False, skip_group_check=True)
                    for k in range(KT):
                        last = pe.matmul(out[:, k * HB * M:(k + 1) * HB * M], qT[:, d, k, rows_t],
                                         kbd[:, d * KT + k].rearrange("p h m -> p (h m)"), start=False,
                                         stop=k == KT - 1, skip_group_check=True)
                last.then_inc(scored, 1)

            def prob_transposes(u, t):
                pe.wait_ge(probs_ready, NT * u + t + 1)
                waited(pe, pt_copied, NT * u + t)
                if t == 0:
                    waited(pe, gelu_s, FT * (u - 1) - 2)
                for d in range(D):
                    rows_of = soft[:, t, d * H:(d + 1) * H].rearrange("p h m -> p (h m)")
                    for c, h in enumerate(CHUNK_HEAD):
                        last = pe.transpose(ps[0:CR, PROB + d, c * P:(c + 1) * P],
                                            rows_of[:, h * M:h * M + CR], ident)
                last.then_inc(pt_ready, 1)

            def own_features(u):
                pe.wait_ge(shifted_s, NT * u + NT)
                for t in range(NT):
                    rows_t = slice(t * P, (t + 1) * P)
                    for k in range(KT):
                        out = ps[:, FEAT, t * F + k * P:t * F + (k + 1) * P]
                        pe.matmul(out, sf_h[:, k, rows_t], ident_r[:], start=t == 0 and k == 0, stop=False,
                                  skip_group_check=True)
                        pe.matmul(out, sf_l[:, k, rows_t], ident_r[:], start=False, stop=False,
                                  skip_group_check=True)

            def attend(u, t):
                if t == 0:
                    pe.wait_ge(vbd_ready, u + 1)
                pe.wait_ge(pt_copied, NT * u + t + 1)
                for d in range(D):
                    for c, (lo, hi) in enumerate(CHUNK_COLS):
                        last = pe.matmul(ps[:, FEAT, t * F + lo:t * F + hi], pT[0:CR, t, d, c * P:(c + 1) * P],
                                         vbd[0:CR, d, lo:hi], start=False,
                                         stop=t == NT - 1 and d == D - 1 and c == NC - 1, skip_group_check=True)
                if t == NT - 1:
                    last.then_inc(attended, 1)

            def ln_transposes(u, n):
                pe.wait_ge(ln_s[n], NT * u + NT)
                if n == 0:
                    waited(pe, m_ready, KT * u)
                for t in range(NT):
                    for k in range(KT):
                        last = pe.transpose(bank(B6, KT, N)[:, k, t * P:(t + 1) * P],
                                            ln[:, n, t, k * P:(k + 1) * P], ident)
                last.then_inc(lnt_ready[n], 1)

            def s5_in(u):
                pe.wait_ge(u_ready, KT * u + KT)
                for s in range(2):
                    for k in range(KT):
                        last = pe.matmul(bank(B6, 2, N)[:, s], bwT[:, k, s], uT[:, k], start=k == 0,
                                         stop=k == KT - 1)
                last.then_inc(bu_ready, 1)

            def s5_out(u):
                pe.wait_ge(cz_s, u + 1)
                for f in range(KT):
                    for s in range(2):
                        last = pe.matmul(bank(B6, KT, N)[:, f], cw[:, s, f * P:(f + 1) * P], cz[:, s],
                                         start=s == 0, stop=s == 1)
                last.then_inc(c_ready, 1)

            def s5_transposes(u):
                pe.wait_ge(a_ready, KT * (u + 1))
                for t in range(NT):
                    for k in range(KT):
                        last = pe.transpose(bank(B6, NT, F)[:, t, k * P:(k + 1) * P],
                                            aT[:, k, t * P:(t + 1) * P], ident)
                last.then_inc(at_ready, 1)

            def mlp_up(u, q):
                if q == 0:
                    pe.wait_ge(m_hs, u + 1)
                    pe.wait_ge(m_ls, u + 1)
                if q == 1:
                    pe.wait_ge(res_ready, GIVEN + u)
                if q >= 2:
                    pe.wait_ge(gelu_s, FT * u + 2 * q - 2)
                for j in range(2):
                    cols = slice((2 * q + j) * P, (2 * q + j + 1) * P)
                    for k in range(KT):
                        last = three(bank((PROB, B7)[q % 2], 2, N)[:, j], w1_h[:, k, cols],
                                     w1_l[:, k, cols], m_h[:, k], m_l[:, k], k == 0, k == KT - 1)
                last.then_inc(h_ready, 1)

            def mlp_down(u, q, ua):
                if q == 0:
                    pe.wait_ge(gelu_s, FT * u + FT)
                    if ua is not None:
                        pe.wait_ge(shifted_s, NT * ua + 1)
                pe.wait_ge(gl_hs, FT // 2 * u + q + 1)
                pe.wait_ge(gl_ls, FT // 2 * u + q + 1)
                for f in range(KT):
                    cols = slice(f * P, (f + 1) * P)
                    for k in (2 * q, 2 * q + 1):
                        last = three(ps[:, (B7, SCORE)[f], 0:N], w2_h[:, k, cols], w2_l[:, k, cols], gl_h[:, k],
                                     gl_l[:, k], k == 0, k == FT - 1)
                    if q == FT // 2 - 1:
                        last.then_inc(ff_ready, 1)

            def mlp_transposes(u):
                for k in range(KT):
                    pe.wait_ge(ff_copied, KT * (GIVEN + u) + k + 1)
                    for t in range(NT):
                        last = pe.transpose(bank(B7, NT, F)[:, t, k * P:(k + 1) * P],
                                            ffT[:, k, t * P:(t + 1) * P], ident)
                last.then_inc(fft_ready, 1)

            def turn(un, ua, ub, uc):
                if uc is not None:
                    mlp_up(uc, 0)
                if ua is not None:
                    rowsums(ua)
                    features(ua)
                if ub is not None:
                    ln_transposes(ub, 0)
                if uc is not None:
                    mlp_up(uc, 1)
                if ub is not None:
                    s5_in(ub)
                if ua is not None:
                    queries(ua, 0)
                    queries(ua, 1)
                if uc is not None:
                    mlp_up(uc, 2)
                if ua is not None:
                    additive(ua)
                if uc is not None:
                    mlp_up(uc, 3)
                if ua is not None:
                    scores(ua, 0)
                if ub is not None:
                    s5_out(ub)
                if ua is not None:
                    scores(ua, 1)
                if ub is not None:
                    s5_transposes(ub)
                if uc is not None:
                    mlp_down(uc, 0, ua)
                    mlp_down(uc, 1, ua)
                if ua is not None:
                    own_features(ua)
                    prob_transposes(ua, 0)
                if uc is not None:
                    mlp_down(uc, 2, ua)
                if ua is not None:
                    prob_transposes(ua, 1)
                    attend(ua, 0)
                if ub is not None:
                    ln_transposes(ub, 1)
                if ua is not None:
                    attend(ua, 1)
                if uc is not None:
                    mlp_down(uc, 3, ua)
                    mlp_transposes(uc)
                else:
                    pe.wait_ge(high, at["w2"])
                    pe.wait_ge(low_mlp, 2)

            pe.wait_ge(cleared, 4)
            pe.wait_ge(s_cond, 32)
            pe.wait_ge(s_wselfq, 16)
            for k in range(KT):
                pe.matmul(bank(B6, F), condT[:, k], wselfq[:, k], start=k == 0, stop=False)
            pe.wait_ge(s_rows, 16)
            pe.wait_ge(s_const, 16)
            pe.matmul(bank(B6, F), const[0:1, C_ROW:C_ROW + P], rows[:, 0:F], start=False, stop=True)\
                .then_inc(cond_ready, 1)
            pe.wait_ge(consts_r, 4)
            pe.wait_ge(high, at["xkv"])
            pe.wait_ge(low, at["xkv"])
            for k in range(KT):
                for part in (xkv_h, xkv_l):
                    last = pe.matmul(bank(B7, KV), ones_r[:], part[:, k], start=k == 0 and part is xkv_h,
                                     stop=k == KT - 1 and part is xkv_l)
            last.then_inc(kv_sums, 1)
            for f in range(KT):
                out, cols = bank(SCORE, KT, KV)[:, f], slice(f * P, (f + 1) * P)
                for k in range(KT):
                    three(out, wself_h[:, k, cols], wself_l[:, k, cols], xkv_h[:, k], xkv_l[:, k], k == 0, False)
                if f == 0:
                    pe.wait_ge(qw_ready, 3)
                    pe.wait_ge(nzkv_ready, 4)
                last = pe.matmul(out, qw[:, cols], nzkv[:], start=False, stop=True, skip_group_check=True)
            last.then_inc(skv_ready, 1)
            rowsums(0)
            features(0)
            pe.wait_ge(high, at["wk"])
            pe.wait_ge(low, at["wk"])
            pe.wait_ge(skv_hs, 1)
            pe.wait_ge(skv_ls, 1)
            for d in range(D):
                for f in range(KT):
                    cols = slice(d * F + f * P, d * F + (f + 1) * P)
                    for k in range(KT):
                        last = three(bank(SCORE + 1 + d, KT, KV)[:, f], wk_h[:, k, cols], wk_l[:, k, cols],
                                     skv_h[:, k], skv_l[:, k], k == 0, k == KT - 1)
                last.then_inc(kh_ready, 1)
            pe.wait_ge(high, at["wq"])
            pe.wait_ge(low, at["wq"])
            queries(0, 0)
            queries(0, 1)
            pe.wait_ge(high, at["wout"])
            pe.wait_ge(low, at["wout"])
            for g in range(B // GB):
                out, keys = ps[0:GR, (PROB, SCORE)[g], :], slice(g * GR, (g + 1) * GR)
                for k in range(KT):
                    three(out, skv_h[:, k, keys], skv_l[:, k, keys], wout_h[:, k], wout_l[:, k], k == 0, False)
                pe.matmul(out, const[0:1, C_ONE:C_ONE + GR], rows[:, F:F + D * F], start=False, stop=True,
                          skip_group_check=True).then_inc(vo_ready, 1)
            additive(0)
            for b in range(B):
                if b == 0:
                    pe.wait_ge(qw_ready, 3)
                    pe.wait_ge(nzkv_ready, 4)
                pe.wait_ge(vo_hs, b // GB + 1)
                pe.wait_ge(vo_ls, b // GB + 1)
                if b >= 2:
                    pe.wait_ge(vo_masked, b - 1)
                out = ps[0:CR, (B6, B7)[b % 2], :]
                pe.matmul(out, gsel_r[0:GR, b % GB], vo_h[0:GR, b // GB], start=True, stop=False)
                pe.matmul(out, gsel_r[0:GR, b % GB], vo_l[0:GR, b // GB], start=False, stop=True)\
                    .then_inc(vo_spread, 1)
            pe.wait_ge(kh_copied, D * KT)
            scores(0, 0)
            scores(0, 1)
            own_features(0)
            pe.wait_ge(bw_ready, 2)
            pe.wait_ge(vo_masked, B)
            for k in range(KT):
                for s in range(2):
                    last = pe.transpose(ps[:, B7, (2 * k + s) * P:(2 * k + s + 1) * P], bw[:, s, k * P:(k + 1) * P],
                                        ident)
            last.then_inc(bwt_ready, 1)
            prob_transposes(0, 0)
            prob_transposes(0, 1)
            attend(0, 0)
            attend(0, 1)
            pe.wait_ge(s_wmod, 16)
            for j in range(NMOD):
                for k in range(KT):
                    last = pe.matmul(bank(B6, NMOD, B)[:, j], wmod[:, k, j * P:(j + 1) * P], condT[:, k, 0:B],
                                     start=k == 0, stop=k == KT - 1)
            last.then_inc(mod_ready, 1)
            pe.wait_ge(mod_copied, 1)
            pe.wait_ge(bwt_copied, 1)
            pe.wait_ge(cw_ready, 2)
            all_turns(pe, turn)

        @block.vector
        def _(dve):
            def nonzero(u):
                dve.wait_ge(row_sums, u + 1)
                dve.tensor_scalar(nz[0:64], ps[0:64, ROWS, 0:N], 0.0, const[0:64, bass.ds(u + C_BSEL, 1)],
                                  ALU.not_equal, ALU.mult).then_inc(nz_ready, 1)

            def features_low(u):
                dve.wait_ge(feat_h, u + 1)
                dve.tensor_tensor(sf_l[:], bank(FEAT, KT, N), f32(sf_h[:]), ALU.subtract).then_inc(feat_l, 1)

            def label_counts(u):
                dve.wait_ge(s_adj, 16 * u + 16)
                dve.tensor_reduce(count[:], adj[:], AX_X, ALU.add).then_inc(counted, 1)

            def label_biases(u):
                dve.wait_ge(counted, u + 1)
                dve.tensor_scalar(masked[:], count[:], 0.0, NEG, ALU.is_le, ALU.mult).then_inc(label_add, 1)
                dve.wait_ge(label_weighed, u + 1)
                dve.tensor_reduce(vbias[:], weighed[:], AX_X, ALU.add).then_inc(label_sums, 1)
                dve.wait_ge(label_sums, u + 1)
                dve.wait_ge(label_add, 2 * u + 1)
                dve.scalar_tensor_tensor(out=addv[:].rearrange("p t d m -> p (t d m)"), in0=vbias[:],
                                         scalar=bbias[:], in1=masked[:], op0=ALU.add, op1=ALU.add)\
                    .then_inc(label_add, 1)
                dve.wait_ge(label_add, 2 * u + 2)
                waited(dve, addt_ready, u)
                dve.tensor_copy(addn[:, :, :, 0:M].bitcast(F32R), addv[:]).then_inc(add_ready, 1)
                dve.wait_ge(add_ready, 2 * u + 1)
                dve.tensor_tensor(addn[:, :, :, M:2 * M].bitcast(F32R), addv[:], addn[:, :, :, 0:M],
                                  ALU.subtract).then_inc(add_ready, 1)

            def shift(u, t):
                dve.wait_ge(scored, NT * u + t + 1)
                first = (SCORE, ROWS)[t]
                s = ps[:, first:first + D, 0:HM].rearrange("p d (h m) -> p d h m", m=M)
                dve.tensor_reduce(smax[:, t].rearrange("p (d h) -> p d h", d=D), s, AX_X, ALU.max).then_inc(maxed, 1)
                dve.wait_ge(maxed, NT * u + t + 1)
                dve.tensor_tensor(soft[:, t].rearrange("p (d h) m -> p d h m", d=D), s,
                                  smax[:, t].rearrange("p (d h) -> p d h", d=D).unsqueeze(3)
                                  .broadcast_to([P, D, H, M]), ALU.subtract).then_inc(shifted_s, 1)

            def sums(u, t):
                dve.wait_ge(exped, NT * u + t + 1)
                dve.tensor_reduce(ssum[:, t], soft[:, t], AX_X, ALU.add).then_inc(summed, 1)
                dve.wait_ge(summed, NT * u + t + 1)
                dve.reciprocal(srec[:, t], ssum[:, t]).then_inc(inverted, 1)

            def residual(u):
                dve.wait_ge(attended, u + 1)
                dve.wait_ge(s_x, 16 * u + 16)
                dve.scalar_tensor_tensor(out=y[:], in0=bank(FEAT, NT, F), scalar=0.0, in1=x[:], op0=ALU.max,
                                         op1=ALU.add).then_inc(y_ready, 1)

            def statistics(u, n):
                v = (y, y2)[n]
                dve.wait_ge((y_ready, y2_ready)[n], u + 1)
                for t in range(NT):
                    dve.bn_stats(st[:, n, t], v[:, t]).then_inc(stats_s[n], 1)

            def aggregate(u, n, op):
                dve.wait_ge(stats_s[n], NT * u + NT)
                op()
                for t in range(NT):
                    dve.bn_aggr(mv[:, n, t], st[:, n, t]).then_inc(mv_s[n], 1)

            def normalize(u, n):
                v = (y, y2)[n]
                dve.wait_ge(mrs_s[n], u + 1)
                for t in range(NT):
                    dve.tensor_scalar(ln[:, n, t], v[:, t], rstd[:, n, t:t + 1], mrs[:, n, t:t + 1],
                                      ALU.mult, ALU.subtract).then_inc(ln_s[n], 1)

            def scan(u):
                dve.wait_ge(bu_ready, u + 1)
                dve.tensor_tensor(bu[:], bank(B6, 2, N), rot[:], ALU.mult).then_inc(bu_turned, 1)
                dve.wait_ge(bu_turned, u + 1)
                dve.tensor_tensor(zin[:], bu[:, 0], bu[:, 1], ALU.add).then_inc(zin_s, 1)
                dve.wait_ge(zin_s, u + 1)
                dve.tensor_tensor_scan(z[:], sc[:, 1:2].broadcast_to([P, N]), zin[:], 0.0, ALU.mult, ALU.add)\
                    .then_inc(z_s, 1)
                dve.wait_ge(z_s, u + 1)
                dve.tensor_tensor(cz[:], z[:].unsqueeze(1).broadcast_to([P, 2, N]), rot[:], ALU.mult)\
                    .then_inc(cz_s, 1)

            def gated(u):
                dve.wait_ge(c_ready, u + 1)
                dve.wait_ge(gdu_ready, u + 1)
                for k in range(KT):
                    dve.scalar_tensor_tensor(out=aT[:, k], in0=bank(B6, KT, N)[:, k], scalar=cur_a[:, 4 + k:5 + k],
                                             in1=gdu[:, k], op0=ALU.mult, op1=ALU.add).then_inc(a_ready, 1)

            def s5_residual(u):
                dve.wait_ge(at_ready, u + 1)
                waited(dve, y2_copied, u)
                dve.tensor_tensor(y2[:], bank(B6, NT, F), y[:], ALU.add).then_inc(y2_ready, 1)

            def mlp_high(u):
                dve.wait_ge(m_ready, KT * u + KT)
                waited(dve, h_ready, FT // 2 * u)
                dve.tensor_copy(m_h[:], mt[:]).then_inc(m_hs, 1)

            def mlp_low(u):
                dve.wait_ge(m_hs, u + 1)
                dve.tensor_tensor(m_l[:], mt[:], f32(m_h[:]), ALU.subtract).then_inc(m_ls, 1)

            def gelu_low(u, q):
                dve.wait_ge(gl_hs, FT // 2 * u + q + 1)
                two = slice(2 * q, 2 * q + 2)
                dve.tensor_tensor(gl_l[:, two], gl[:, two], f32(gl_h[:, two]), ALU.subtract).then_inc(gl_ls, 1)

            def result(u):
                dve.wait_ge(fft_ready, u + 1)
                dve.wait_ge(s_out, 16 * (GIVEN + u))
                dve.tensor_tensor(res[:], bank(B7, NT, F), y2_kept[:], ALU.add).then_inc(res_ready, 1)

            def turn(un, ua, ub, uc):
                if ua is not None:
                    nonzero(ua)
                if ub is not None:
                    normalize(ub, 0)
                if uc is not None:
                    gelu_low(uc, 0)
                if ua is not None:
                    features_low(ua)
                    label_biases(ua)
                if uc is not None:
                    gelu_low(uc, 1)
                if ub is not None:
                    scan(ub)
                if uc is not None:
                    gelu_low(uc, 2)
                    gelu_low(uc, 3)
                if ua is not None:
                    shift(ua, 0)
                if ub is not None:
                    gated(ub)
                if ua is not None:
                    shift(ua, 1)
                    sums(ua, 0)
                if ub is not None:
                    s5_residual(ub)
                    statistics(ub, 1)
                    aggregate(ub, 1, lambda: None if ua is None else sums(ua, 1))
                    normalize(ub, 1)
                if un is not None:
                    label_counts(un)
                if ua is not None:
                    residual(ua)
                    statistics(ua, 0)
                if ub is not None:
                    mlp_high(ub)
                    if ua is None:
                        mlp_low(ub)
                    else:
                        aggregate(ua, 0, lambda: mlp_low(ub))
                if uc is not None:
                    result(uc)

            def low_part(name):
                whole, part_h, part_l = parts[name]
                dve.wait_ge(high, at[name])
                dve.tensor_tensor(part_l[:], whole[:], f32(part_h[:]), ALU.subtract).then_inc(low, 1)

            step = stepper(dve, params_step)
            low_part("wself")
            low_part("xkv")
            dve.wait_ge(s_const, 16)
            dve.tensor_copy(ones_r[:], const[:, C_ONE:C_ONE + P]).then_inc(consts_r, 1)
            dve.tensor_copy(ident_r[:], ident).then_inc(consts_r, 1)
            dve.tensor_copy(rep_r[:].rearrange("p d k -> p (d k)"), const[:, C_REP:C_REP + D * HM]).then_inc(consts_r, 1)
            dve.tensor_copy(gsel_r[:].rearrange("p b k -> p (b k)"), const[:, C_GSEL:C_GSEL + GB * CR])\
                .then_inc(consts_r, 1)
            dve.wait_ge(cond_ready, 1)
            dve.tensor_copy(qw[:], bank(B6, F)).then_inc(qw_ready, 1)
            dve.wait_ge(qw_ready, 1)
            for r in (32, 96):
                dve.tensor_tensor(qw[r:r + 32], ps[r:r + 32, B6, 0:F], f32(qw[r:r + 32]), ALU.subtract)\
                    .then_inc(qw_ready, 1)
            bias_rows = const[64:P, C_BIASROW:C_BIASROW + 1]
            dve.tensor_copy(nz[64:P], bias_rows.broadcast_to([64, N])).then_inc(nzkv_ready, 1)
            dve.tensor_copy(nzkv[64:P], bias_rows.broadcast_to([64, KV])).then_inc(nzkv_ready, 1)
            dve.memset(f32(nz[0:64]), 0.0).then_inc(nzkv_ready, 1)
            dve.wait_ge(nzkv_ready, 3)
            dve.wait_ge(kv_sums, 1)
            dve.scalar_tensor_tensor(out=nzkv[0:64], in0=ps[0:64, B7, 0:KV], scalar=0.0,
                                     in1=const[0:64, C_KVSEL:C_KVSEL + KV], op0=ALU.not_equal, op1=ALU.mult)\
                .then_inc(nzkv_ready, 1)
            low_part("wk")
            nonzero(0)
            dve.wait_ge(skv_hs, 1)
            dve.tensor_tensor(skv_l[:], bank(SCORE, KT, KV), f32(skv_h[:]), ALU.subtract).then_inc(skv_ls, 1)
            low_part("wq")
            features_low(0)
            low_part("wout")
            label_counts(0)
            for g in range(B // GB):
                dve.wait_ge(vo_hs, g + 1)
                dve.tensor_tensor(vo_l[0:GR, g], ps[0:GR, (PROB, SCORE)[g], :], f32(vo_h[0:GR, g]), ALU.subtract)\
                    .then_inc(vo_ls, 1)
            dve.wait_ge(s_small, 16 * 6)
            label_biases(0)
            for b in range(B):
                dve.wait_ge(vo_spread, b + 1)
                dve.tensor_tensor(vo_all[0:CR, b].rearrange("p (d f) -> p d f", d=D),
                                  ps[0:CR, (B6, B7)[b % 2], :].rearrange("p (d f) -> p d f", d=D),
                                  const[0:CR, C_VMASK:C_VMASK + F].unsqueeze(1).broadcast_to([CR, D, F]),
                                  ALU.mult).then_inc(vo_masked, 1)
            shift(0, 0)
            sums(0, 0)
            shift(0, 1)
            sums(0, 1)
            residual(0)
            statistics(0, 0)
            aggregate(0, 0, lambda: None)
            dve.wait_ge(mod_ready, 1)
            dve.tensor_tensor(mod[:], bank(B6, NMOD, B), bmod[:].unsqueeze(2).broadcast_to([P, NMOD, B]),
                              ALU.add).then_inc(mod_copied, 1)
            dve.wait_ge(mod_copied, 1)
            shift_a, scale_a, gate_a, shift_f, scale_f, gate_f, scale_c, shift_c = (
                mod[:, KT * j:KT * j + KT] for j in range(8))
            pa = [par_a[:, :, KT * j:KT * j + KT].rearrange("p b k -> p k b") for j in range(4)]
            pf = [par_f[:, :, KT * j:KT * j + KT].rearrange("p b k -> p k b") for j in range(4)]
            per_feature = lambda j: b12[:, j:j + KT].unsqueeze(2).broadcast_to([P, KT, B])
            step(dve.tensor_scalar(pa[0], scale_a, 1.0, None, ALU.add))
            step(dve.tensor_copy(pa[1], shift_a))
            step(dve.tensor_copy(pa[2], gate_a))
            step(dve.tensor_tensor(pa[3], gate_a, per_feature(FT + KT), ALU.mult))
            step(dve.tensor_scalar(pt[:, 0], scale_f, 1.0, None, ALU.add))
            step(dve.tensor_scalar(pt[:, 1], scale_c, 1.0, None, ALU.add))
            step(dve.tensor_tensor(pf[0], pt[:, 0], pt[:, 1], ALU.mult))
            step(dve.tensor_tensor(pt[:, 2], shift_c, pt[:, 0], ALU.mult))
            step(dve.tensor_tensor(pf[1], pt[:, 2], shift_f, ALU.add))
            step(dve.tensor_copy(pf[2], gate_f))
            step(dve.tensor_tensor(pf[3], gate_f, per_feature(FT), ALU.mult))
            label_counts(1)
            all_turns(dve, turn)


def kernel(x, cond_1024, mask_BxSxSx11_ik0, L0_cond_W_self, L0_cond_b_self, L0_cond_w_bias, L0_cond_b_bias,
           L0_cond_Wq, L0_cond_bq, L0_cond_Wk, L0_cond_bk, L0_cond_Wout, L0_cond_bout, L1_cond_Wm, L1_cond_bm,
           L1_cond_Lam_re, L1_cond_Lam_im, L1_cond_B_re, L1_cond_B_im, L1_cond_C_re, L1_cond_C_im,
           L1_cond_D_diag, L1_cond_log_step, L1_cond_Wc, L1_cond_bc, L1_cond_W1, L1_cond_b1, L1_cond_W2,
           L1_cond_b2):
    import concourse.bacc as bacc
    from concourse.bass_utils import run_bass_kernel_spmd

    def on_rows(a):
        a = np.asarray(a)
        return np.ascontiguousarray(a.reshape(a.shape[0] // P, P, -1).transpose(1, 0, 2))

    def columns(*vectors):
        return np.ascontiguousarray(np.concatenate([np.asarray(v).reshape(-1) for v in vectors]).reshape(-1, P).T)

    x = np.asarray(x)
    w_self = np.asarray(L0_cond_W_self)
    adj = np.asarray(mask_BxSxSx11_ik0)
    pairs = np.stack([adj[:, :, :M], adj[:, :M].transpose(0, 2, 1, 3)], axis=2)
    pairs = pairs.reshape(B, NT, P, D * M, L).transpose(0, 2, 1, 3, 4).reshape(B, P, NT * D * M, L)
    arrays = {
        "const": constants(),
        "x": x,
        "xT": np.ascontiguousarray(x.reshape(B, N, KT, P).transpose(0, 3, 2, 1)),
        "xkv": on_rows(x[:, :M].reshape(KV, F).T),
        "adj": np.ascontiguousarray(pairs),
        "wself": on_rows(w_self[:, :F].T),
        "wselfq": on_rows(w_self[:, F:].T),
        "condT": on_rows(np.asarray(cond_1024).T),
        "rows": np.concatenate([np.asarray(L0_cond_b_self), np.asarray(L0_cond_bout).reshape(-1)])[None],
        "wbias": np.asarray(L0_cond_w_bias)[None],
        "bbias": np.asarray(L0_cond_b_bias).reshape(1, 1),
        "wq": on_rows(np.asarray(L0_cond_Wq).reshape(D * F, F).T),
        "wk": on_rows(np.asarray(L0_cond_Wk).reshape(D * F, F).T),
        "bq": columns(L0_cond_bq),
        "bk": columns(L0_cond_bk),
        "wout": on_rows(np.asarray(L0_cond_Wout).reshape(D * F, F).T),
        "wmod": on_rows(np.concatenate([np.asarray(L1_cond_Wm), np.asarray(L1_cond_Wc)], axis=1)),
        "bmod": columns(L1_cond_bm, L1_cond_bc),
        "lam": np.stack([np.asarray(v) for v in (L1_cond_Lam_re, L1_cond_Lam_im, L1_cond_log_step)], axis=1),
        "b_ri": np.stack([np.asarray(L1_cond_B_re), np.asarray(L1_cond_B_im)]),
        "c_ri": np.stack([np.asarray(L1_cond_C_re).T, np.asarray(L1_cond_C_im).T]),
        "w1": on_rows(L1_cond_W1),
        "w2": on_rows(L1_cond_W2),
        "b12": columns(L1_cond_b1, L1_cond_b2, L1_cond_D_diag),
    }
    nc = bacc.Bacc("TRN2", target_bir_lowering=False, num_devices=1, dynamic_dma_scratch_size=1024)
    arrays = {f"in_{n}": np.ascontiguousarray(a) for n, a in arrays.items()}
    dram = {n[3:]: nc.dram_tensor(n, a.shape, mybir.dt.from_np(a.dtype), kind="ExternalInput").ap()
            for n, a in arrays.items()}
    dram["out"] = nc.dram_tensor("out", (B, N, F), F32, kind="ExternalOutput").ap()
    build(nc, dram)
    return run_bass_kernel_spmd(nc, [arrays], core_ids=[0]).results[0]["out"]
```

```python
from contextlib import ExitStack

import numpy as np

import concourse.bass as bass
from concourse import mybir

F32 = mybir.dt.float32
F32R = mybir.dt.float32r
I32 = mybir.dt.int32
ALU = mybir.AluOpType
ACT = mybir.ActivationFunctionType
AX_X = mybir.AxisListType.X

P = 128
B = 8
N = 256
F = 256
KT = F // P
NT = N // P
D = 2
H = 16
G = F // H
M = 20
L = 11
HM = H * M
HB = P // G
CH = 6
CR = CH * M
CHUNK_HEAD = (0, 6, 10)
CHUNK_COLS = ((0, 96), (96, 192), (192, 256))
NC = len(CHUNK_HEAD)
KV = B * M
GB = 4
GR = GB * M
S = 64
FF = 4 * F
FT = FF // P
NEG = -9000000000000000.0
EPS = 1e-5
ROUND = 12582912.0
TWO_PI = 6.283185307179586
LOG2E = 1.4426950408889634
LN2_H = 0.693359375
LN2_L = -2.12194440054690581e-4
PI2_H = 6.28125
PI2_M = 1.93500518798828125e-3
PI2_L = 3.0199159819567e-7
SIN_SCALE = 6.2831845

C_ID = 0
C_KMASK = C_ID + P
C_BSEL = C_KMASK + HB
C_KVSEL = C_BSEL + B
C_TIME = C_KVSEL + KV
C_SIGN = C_TIME + N
C_ROW = C_SIGN + 1
C_ONE = C_ROW + P
C_BIASROW = C_ONE + GR
C_LATE = C_BIASROW + 1
C_REP = C_LATE
C_VMASK = C_REP + D * HM
C_GSEL = C_VMASK + F
C_END = C_GSEL + GB * CR


def constants():
    c = np.zeros((P, C_END), np.float32)
    c[:, C_ID:C_ID + P] = np.eye(P)
    rep = c[:, C_REP:C_REP + D * HM].reshape(P, D, H, M)
    for d in range(D):
        for m in range(M):
            rep[64 * d + m, d, :, m] = 1
            rep[64 * d + M + m, d, :, m] = 1
    for n, (lo, hi) in enumerate(CHUNK_COLS):
        for r in range(CR):
            h = CHUNK_HEAD[n] + r // M
            a, b = max(lo, h * G), min(hi, (h + 1) * G)
            if a < b:
                c[r, C_VMASK + a:C_VMASK + b] = 1
    for p in range(P):
        c[p, C_KMASK + p // G] = 0.25
    for b in range(B):
        for r in (b, 32 + b):
            c[r, C_BSEL + b] = 1
            c[r, C_KVSEL + b * M:C_KVSEL + (b + 1) * M] = 1
    gsel = c[:, C_GSEL:C_GSEL + GB * CR].reshape(P, GB, CH, M)
    for b in range(GB):
        for m in range(M):
            gsel[b * M + m, b, :, m] = 1
    c[:, C_TIME:C_TIME + N] = np.arange(N)
    c[:S, C_SIGN] = -1
    c[S:, C_SIGN] = 1
    c[0, C_ROW + 64] = c[0, C_ROW + 96] = 1
    c[:, C_ONE:C_ONE + GR] = 1
    c[64, C_BIASROW] = c[96, C_BIASROW] = 1
    return c


def build(nc, dram):
    ctx = ExitStack()
    with ctx:
        def sb(name, shape, dt=F32):
            return ctx.enter_context(nc.sbuf_tensor(name, shape, dt))

        def sem(name):
            return ctx.enter_context(nc.semaphore(name))

        def f32(ap):
            return ap.bitcast(F32)

        const = sb("const", [P, C_END])
        ident = const[:, C_ID:C_ID + P]
        ident_r = sb("ident_r", [P, P], F32R)
        rep_r = sb("rep_r", [P, D, HM], F32R)
        gsel_r = sb("gsel_r", [P, GB, CR], F32R)
        ones_r = sb("ones_r", [P, P], F32R)
        stage = sb("stage", [P, 4, KT * D * F])
        wk, wq, wout = (stage[:, k].rearrange("p (k n) -> p k n", k=KT) for k in range(3))
        wself, wselfq = (stage[:, 3, k * KT * F:(k + 1) * KT * F].rearrange("p (k n) -> p k n", k=KT)
                         for k in range(2))
        w1 = stage[:, 0:2].rearrange("p a (b n) -> p (a b) n", n=FF)
        w2 = stage[:, 2:4].rearrange("p a (b n) -> p (a b) n", n=F)
        wself_h, wself_l = sb("wself_h", [P, KT, F], F32R), sb("wself_l", [P, KT, F], F32R)
        wq_h, wq_l = sb("wq_h", [P, KT, D * F], F32R), sb("wq_l", [P, KT, D * F], F32R)
        gl_h, gl_l = sb("gl_h", [P, FT, N], F32R), sb("gl_l", [P, FT, N], F32R)
        wk_h, wk_l, wout_h, wout_l = (g[:, k * FT // 2:(k + 1) * FT // 2].rearrange("p (k a) n -> p k (a n)", k=KT)
                                      for g in (gl_h, gl_l) for k in range(2))
        w1_h, w1_l = sb("w1_h", [P, KT, FF], F32R), sb("w1_l", [P, KT, FF], F32R)
        w2_h, w2_l = sb("w2_h", [P, FT, F], F32R), sb("w2_l", [P, FT, F], F32R)
        NMOD = 8 * KT
        late = sb("late", [P, KT * NMOD * P])
        wmod = late[:, :].rearrange("p (h k n) -> p (h k) n", h=2, k=KT)
        gl = late[:, FT * N:2 * FT * N].rearrange("p (k n) -> p k n", n=N)
        aT, cz, ffT, y2 = (late[:, 2 * k * N:(2 * k + 2) * N].rearrange("p (k n) -> p k n", n=N)
                           for k in range(4))
        condT = sb("condT", [P, KT, P])
        rows = sb("rows", [1, F + D * F])
        small = sb("small", [P, 2 * D * KT + NMOD + FT + 2 * KT])
        bq, bk, bmod, b12 = (small[:, a:b] for a, b in (
            (0, D * KT), (D * KT, 2 * D * KT), (2 * D * KT, 2 * D * KT + NMOD),
            (2 * D * KT + NMOD, 2 * D * KT + NMOD + FT + 2 * KT)))
        lbias = sb("lbias", [P, L + 1])
        wbias, bbias = lbias[:, 0:L], lbias[:, L:L + 1]
        xkv = sb("xkv", [P, KT, KV])
        xkv_h, xkv_l = sb("xkv_h", [P, KT, KV], F32R), sb("xkv_l", [P, KT, KV], F32R)
        nzkv = sb("nzkv", [P, KV], F32R)
        qw = sb("qw", [P, F], F32R)
        skv_h, skv_l = sb("skv_h", [P, KT, KV], F32R), sb("skv_l", [P, KT, KV], F32R)
        kh = sb("kh", [P, D * KT, KV])
        vo_h, vo_l = (gl_h[:, k * FT // 2:(k + 1) * FT // 2].rearrange("p (g a) n -> p g (a n)", g=B // GB)
                      for k in range(2))
        vo_all = sb("vo_all", [P, B, D * F])
        lam = sb("lam", [P, 3])
        sc = sb("sc", [P, 40])
        sci = sb("sci", [P, 1], I32)
        bri = sb("bri", [P, 2, F])
        bw = sb("bw", [P, 2, F])
        bt = sb("bt", [P, 3, F])
        bwT = sb("bwT", [P, KT, 2, P])
        cri = sb("cri", [P, 2, F])
        cw = sb("cw", [P, 2, F])
        rot = sb("rot", [P, 2, N])
        mod = sb("mod", [P, NMOD, B])
        par_a = sb("par_a", [P, B, 8])
        par_f = sb("par_f", [P, B, 8])
        pt = sb("pt", [P, 4, KT, B])
        xT = sb("xT", [P, KT, N])
        x = sb("x", [P, NT, F])
        adj = sb("adj", [P, NT * D * M, L], I32)
        x_h, x_l = sb("x_h", [P, KT, N], F32R), sb("x_l", [P, KT, N], F32R)
        nz = sb("nz", [P, N], F32R)
        sf_h, sf_l = sb("sf_h", [P, KT, N], F32R), sb("sf_l", [P, KT, N], F32R)
        qT = sb("qT", [P, D, KT, N])
        count = sb("count", [P, NT * D * M])
        weighed = sb("weighed", [P, NT * D * M, L])
        vbias = sb("vbias", [P, NT * D * M])
        masked = sb("masked", [P, NT * D * M])
        addv = sb("addv", [P, NT, D, M])
        addn = sb("addn", [P, NT, D, 64])
        addT = sb("addT", [P, NT, P], F32R)
        kbd = sb("kbd", [P, D * KT, HB, M])
        vbd = sb("vbd", [P, D, F])
        smax = sb("smax", [P, NT, D * H])
        soft = sb("soft", [P, NT, D * H, M])
        ssum = sb("ssum", [P, NT, D * H])
        srec = sb("srec", [P, NT, D * H])
        pT = sb("pT", [P, NT, D, NC * P])
        y = sb("y", [P, NT, F])
        cur_a = sb("cur_a", [P, 8])
        cur_f = sb("cur_f", [P, 4])
        cur_g = sb("cur_g", [P, 4])
        st = sb("st", [P, 2, NT, 6])
        mv = sb("mv", [P, 2, NT, 2])
        rstd = sb("rstd", [P, 2, NT])
        veps = sb("veps", [P, 2, NT])
        half, eps = sb("half", [P, NT]), sb("eps", [P, NT])
        mrs = sb("mrs", [P, 2, NT])
        ln = sb("ln", [P, 2, NT, F])
        y2_kept = sb("y2_kept", [P, NT, F])
        uT = sb("uT", [P, KT, N])
        gdu = sb("gdu", [P, KT, N])
        bu = sb("bu", [P, 2, N])
        zin = sb("zin", [P, N])
        z = sb("z", [P, N])
        mt = sb("mt", [P, KT, N])
        m_h, m_l = sb("m_h", [P, KT, N], F32R), sb("m_l", [P, KT, N], F32R)
        table_use = sb("table_use", [P, 1])
        res = sb("res", [P, NT, F])

        v = lambda k: sc[:, k:k + 1]
        sign = const[:, C_SIGN:C_SIGN + 1]
        fh, fl = v(6), v(7)
        kr, ki, kis, krs = v(23), v(24), v(26), v(27)
        tb = [v[:, k] for v in (res, y2_kept, uT) for k in range(2)]
        ps = ctx.enter_context(nc.psum_tensor("ps", [P, 8, 512], F32))
        ROWS, FEAT, SCORE, PROB, B6, B7 = 0, 1, 2, 4, 6, 7
        VO = PROB, B7

        def bank(n, *dims):
            size = int(np.prod(dims))
            return ps[:, n, 0:size] if len(dims) == 1 else ps[:, n, 0:size].rearrange(
                "p (a b) -> p a b", a=dims[0])

        s_const, s_wselfq, s_rows, s_small, s_lam, s_bri, s_cri, s_wmod = (sem(n) for n in (
            "const_loaded", "wselfq_loaded", "rows_loaded", "small_loaded", "lam_loaded", "b_loaded",
            "c_loaded", "wmod_loaded"))
        s_cond, s_const_late = sem("cond_loaded"), sem("const_late_loaded")
        split_order = ("wself", "xkv", "wk", "wq", "wout", "w1", "w2")
        loaded = {n: sem(n + "_loaded") for n in split_order}
        high = sem("high_parts")
        low, low_mlp = sem("low_parts"), sem("low_parts_mlp")
        at = {n: k + 1 for k, n in enumerate(split_order)}
        parts = {"wself": (wself, wself_h, wself_l), "xkv": (xkv, xkv_h, xkv_l), "wk": (wk, wk_h, wk_l),
                 "wq": (wq, wq_h, wq_l), "wout": (wout, wout_h, wout_l), "w1": (w1, w1_h, w1_l),
                 "w2": (w2, w2_h, w2_l)}
        cleared, consts_r, cond_ready, qw_ready, kv_sums, nzkv_ready = (sem(n) for n in (
            "cleared", "consts_rounded", "cond_part_ready", "qw_ready", "kv_sums", "nzkv_ready"))
        skv_ready, skv_hs, skv_ls, kh_ready, kh_copied = (sem(n) for n in (
            "skv_ready", "skv_h_ready", "skv_l_ready", "kh_ready", "kh_copied"))
        vo_ready, vo_hs, vo_ls, vo_spread, vo_copied = (sem(n) for n in (
            "vo_ready", "vo_h_ready", "vo_l_ready", "vo_spread", "vo_copied"))
        mod_ready, mod_copied, params_step = sem("mod_ready"), sem("mod_copied"), sem("params_ready")
        s5_step, turns, rot_ready, bw_ready, cw_ready, bwt_ready, bwt_copied = (sem(n) for n in (
            "s5_step", "turns_ready", "rot_ready", "bw_ready", "cw_ready", "bwt_ready", "bwt_copied"))
        tables_step, weights_step = sem("tables_step"), sem("weights_step")
        gelu_table = sem("gelu_table_loaded")
        turn_parts, b_scales = sem("turn_parts_ready"), sem("b_scales_ready")

        s_xT, s_x, s_adj, s_out = (sem(n) for n in ("xT_loaded", "x_loaded", "adj_loaded", "out_stored"))
        x_high, x_low = sem("x_high"), sem("x_low")
        row_sums, nz_ready, feat_ready, feat_h, feat_l = (sem(n) for n in (
            "row_sums", "nz_ready", "feat_ready", "feat_h_ready", "feat_l_ready"))
        q_ready, q_copied = sem("q_ready"), sem("q_copied")
        label_floats = sem("label_floats")
        counted, label_weighed, label_sums, label_add, add_ready, addt_ready, addt_copied = (sem(n) for n in (
            "counted", "label_weighed", "label_sums", "label_add", "add_ready", "addt_ready", "addt_copied"))
        kbd_ready, vbd_ready = sem("kbd_ready"), sem("vbd_ready")
        scored, maxed, shifted_s, exped, summed, inverted, probs_ready = (sem(n) for n in (
            "scored", "maxed", "shifted_ready", "exped", "summed", "inverted", "probs_ready"))
        pt_ready, pt_copied, attended, y_ready = (sem(n) for n in (
            "pt_ready", "pt_copied", "attended", "y_ready"))
        cur_a_s, cur_f_s, cur_g_s = sem("cur_a_ready"), sem("cur_f_ready"), sem("cur_g_ready")
        stats_s, mv_s, veps_s, rstd_s, mrs_s, ln_s, lnt_ready = ([sem(f"{n}_{k}") for k in range(2)] for n in (
            "stats_ready", "mean_var_ready", "var_eps_ready", "rstd_ready", "mean_rstd_ready", "ln_ready",
            "lnt_ready"))
        u_ready, gdu_ready, bu_ready, bu_turned, zin_s, z_s, cz_s, c_ready, a_ready, at_ready = (sem(n) for n in (
            "u_ready", "gdu_ready", "bu_ready", "bu_turned", "scan_input", "scanned", "z_turned",
            "c_ready", "a_ready", "at_ready"))
        y2_ready, y2_copied, m_ready, m_hs, m_ls, h_ready, gelu_s, gl_hs, gl_ls = (sem(n) for n in (
            "y2_ready", "y2_copied", "m_ready", "m_h_ready", "m_l_ready", "h_ready", "gelu_done", "gelu_h_ready",
            "gelu_l_ready"))
        ff_ready, ff_copied, fft_ready, res_ready = (sem(n) for n in (
            "ff_ready", "ff_copied", "fft_ready", "res_ready"))

        block = ctx.enter_context(nc.Block())

        GIVEN = 1

        def waited(eng, signal, value):
            if not (isinstance(value, int) and value <= 0):
                eng.wait_ge(signal, value)

        def stepper(eng, chain):
            count = {}

            def step(ins, signal=chain):
                count[signal.name] = count.get(signal.name, 0) + 1
                ins.then_inc(signal, 1)
                eng.wait_ge(signal, count[signal.name])
            return step

        def all_turns(eng, turn, turn_bc, turn_c):
            with eng.Fori(0, B - 3) as i:
                turn(i + 3, i + 2, i + 1, i)
            turn(None, B - 1, B - 2, B - 3)
            turn_bc(B - 1, B - 2)
            turn_c(B - 1)

        @block.sync
        def _(sp):
            def load_xT(u):
                waited(sp, x_low, u)
                sp.dma_start(xT[:], dram["xT"][bass.ds(u, 1)].rearrange("b p k n -> (b p) k n")).then_inc(s_xT, 16)

            def load_adj(u):
                waited(sp, counted, u)
                waited(sp, label_floats, u)
                sp.dma_start(adj[:], dram["adj"][bass.ds(u, 1)].rearrange("b p t l -> (b p) t l")).then_inc(s_adj, 16)

            def load_x(u):
                waited(sp, y_ready, u)
                sp.dma_start(x[:], dram["x"][bass.ds(u, 1)].rearrange("b (t p) f -> p (b t) f", p=P)).then_inc(s_x, 16)

            def store(u):
                sp.wait_ge(res_ready, GIVEN + u + 1)
                sp.dma_start(dram["out"][bass.ds(u, 1)].rearrange("b (t p) f -> p (b t) f", p=P), res[:])\
                    .then_inc(s_out, 16)

            for signal, count in ((ff_copied, KT), (ff_ready, KT), (res_ready, 1), (s_out, 16)):
                sp.sem_inc(signal, GIVEN * count)
            sp.dma_start(lam[:], dram["lam"]).then_inc(s_lam, 16)
            sp.dma_start(wself[:], dram["wself"]).then_inc(loaded["wself"], 16)
            sp.dma_start(xkv[:], dram["xkv"]).then_inc(loaded["xkv"], 16)
            load_xT(0)
            sp.dma_start(const[:, 0:C_LATE], dram["const"][:, 0:C_LATE]).then_inc(s_const, 16)
            sp.dma_start(wk[:], dram["wk"]).then_inc(loaded["wk"], 16)
            load_adj(0)
            sp.dma_start(wq[:], dram["wq"]).then_inc(loaded["wq"], 16)
            sp.dma_start(wout[:], dram["wout"]).then_inc(loaded["wout"], 16)
            sp.dma_start(const[:, C_LATE:C_END], dram["const"][:, C_LATE:C_END]).then_inc(s_const_late, 16)
            sp.dma_start(late[:], dram["wmod"]).then_inc(s_wmod, 16)
            load_x(0)
            for name, before in (("w1", "wq"), ("w2", "wout")):
                sp.wait_ge(low, at[before])
                if name == "w2":
                    sp.wait_ge(cond_ready, 1)
                sp.dma_start(parts[name][0][:], dram[name]).then_inc(loaded[name], 16)
            load_xT(1)
            load_adj(1)
            for u in (1, 2):
                load_xT(u + 1)
                load_adj(u + 1)
                load_x(u)
            with sp.Fori(0, B - 4) as i:
                load_xT(i + 4)
                load_adj(i + 4)
                load_x(i + 3)
                store(i)
            load_x(B - 1)
            for u in range(B - 4, B):
                store(u)
            sp.wait_ge(s_out, 16 * (GIVEN + B))

        @block.gpsimd
        def _(pool):
            step = stepper(pool, s5_step)

            def exp_steps(out, v, t):
                n, r, q, w = (sc[:, t + k:t + k + 1] for k in range(4))
                step(pool.tensor_scalar(q, v, -87.0, 88.0, ALU.max, ALU.min))
                step(pool.tensor_scalar(n, q, LOG2E, ROUND, ALU.mult, ALU.add))
                step(pool.tensor_scalar(n, n, ROUND, None, ALU.subtract))
                step(pool.tensor_scalar(w, n, LN2_H, None, ALU.mult))
                step(pool.tensor_tensor(r, q, w, ALU.subtract))
                step(pool.tensor_scalar(w, n, LN2_L, None, ALU.mult))
                step(pool.tensor_tensor(r, r, w, ALU.subtract))
                step(pool.tensor_scalar(q, r, 1.0 / 5040, 1.0 / 720, ALU.mult, ALU.add))
                for c in (1.0 / 120, 1.0 / 24, 1.0 / 6, 0.5, 1.0, 1.0):
                    step(pool.tensor_scalar(q, q, r, c, ALU.mult, ALU.add))
                step(pool.tensor_scalar(sci[:], n, 127.0, 8388608.0, ALU.add, ALU.mult))
                step(pool.tensor_tensor(out, q, sci[:].bitcast(F32), ALU.mult))

            def x_parts(u):
                pool.wait_ge(x_high, u + 1)
                pool.tensor_tensor(x_l[:], xT[:], f32(x_h[:]), ALU.subtract).then_inc(x_low, 1)

            def label_weights(u):
                pool.wait_ge(label_floats, u + 1)
                pool.tensor_tensor(weighed[:], weighed[:], wbias[:].unsqueeze(1).broadcast_to([P, NT * D * M, L]),
                                   ALU.mult).then_inc(label_weighed, 1)

            def key_blocks(u):
                waited(pool, scored, NT * u)
                keys = kh[:, :, bass.ds(u * M, M)]
                pool.tensor_tensor(kbd[:], keys.unsqueeze(2).broadcast_to([P, D * KT, HB, M]),
                                   const[:, C_KMASK:C_KMASK + HB].unsqueeze(1).unsqueeze(3)
                                   .broadcast_to([P, D * KT, HB, M]), ALU.mult).then_inc(kbd_ready, 1)

            def value_blocks(u):
                waited(pool, attended, u)
                pool.wait_ge(vo_copied, u + 1)
                pool.tensor_tensor(vbd[0:CR, :, :], vo_all[0:CR, bass.ds(u, 1), :]
                                   .rearrange("p b (d f) -> p (b d) f", d=D),
                                   const[0:CR, C_VMASK:C_VMASK + F].unsqueeze(1).broadcast_to([CR, D, F]),
                                   ALU.mult).then_inc(vbd_ready, 1)

            def probabilities(u, t):
                pool.wait_ge(inverted, NT * u + t + 1)
                pool.tensor_tensor(soft[:, t], soft[:, t], srec[:, t].unsqueeze(2).broadcast_to([P, D * H, M]),
                                   ALU.mult).then_inc(probs_ready, 1)

            def rstd_of(u, k):
                pool.wait_ge(mv_s[k], NT * u + NT)
                pool.tensor_tensor(veps[:, k], mv[:, k, :, 1], eps[:], ALU.add).then_inc(veps_s[k], 1)
                pool.wait_ge(veps_s[k], u + 1)
                pool.tensor_tensor(rstd[:, k], veps[:, k], half[:], ALU.pow).then_inc(rstd_s[k], 1)
                pool.wait_ge(rstd_s[k], u + 1)
                pool.tensor_tensor(mrs[:, k], mv[:, k, :, 0], rstd[:, k], ALU.mult).then_inc(mrs_s[k], 1)

            def take_s5_params(u):
                waited(pool, a_ready, KT * u)
                pool.tensor_copy(cur_a[:], par_a[:, bass.ds(u, 1), :].rearrange("p b k -> p (b k)"))\
                    .then_inc(cur_a_s, 1)

            def take_mlp_params(u):
                waited(pool, m_ready, KT * u)
                pool.tensor_copy(cur_f[:], par_f[:, bass.ds(u, 1), 0:4].rearrange("p b k -> p (b k)"))\
                    .then_inc(cur_f_s, 1)

            def take_gate(u):
                pool.wait_ge(ff_copied, KT * (GIVEN + u))
                pool.tensor_copy(cur_g[:], par_f[:, bass.ds(u, 1), 4:8].rearrange("p b k -> p (b k)"))\
                    .then_inc(cur_g_s, 1)

            def skip_term(u):
                pool.wait_ge(u_ready, KT * u + KT)
                pool.tensor_tensor(gdu[:], uT[:], cur_a[:, 6:6 + KT].unsqueeze(2).broadcast_to([P, KT, N]), ALU.mult)\
                    .then_inc(gdu_ready, 1)

            def turn(un, ua, ub, uc):
                take_s5_params(ub)
                take_mlp_params(ub)
                take_gate(uc)
                label_weights(ua)
                key_blocks(ua)
                rstd_of(ub, 0)
                skip_term(ub)
                value_blocks(ua)
                probabilities(ua, 0)
                probabilities(ua, 1)
                rstd_of(ub, 1)
                if un is not None:
                    x_parts(un)

            def turn_bc(ub, uc):
                rstd_of(ub, 0)
                take_s5_params(ub)
                take_mlp_params(ub)
                take_gate(uc)
                skip_term(ub)
                rstd_of(ub, 1)

            def turn_c(uc):
                take_gate(uc)

            step(pool.memset(addn[:], 0.0), cleared)
            step(pool.memset(half[:], -0.5), cleared)
            step(pool.memset(eps[:], EPS), cleared)
            step(pool.memset(f32(ones_r[:]), 1.0), cleared)

            lr, li, ls = lam[:, 0:1], lam[:, 1:2], lam[:, 2:3]
            dt, a, th, n, r, w = v(0), v(1), v(2), v(3), v(4), v(5)
            pool.wait_ge(s_lam, 16)
            exp_steps(dt, ls, 10)
            step(pool.tensor_tensor(a, lr, dt, ALU.mult))
            exp_steps(a, a, 10)
            step(pool.tensor_tensor(th, li, dt, ALU.mult))
            step(pool.tensor_scalar(n, th, 1.0 / TWO_PI, ROUND, ALU.mult, ALU.add))
            step(pool.tensor_scalar(n, n, ROUND, None, ALU.subtract))
            for part in (PI2_H, PI2_M, PI2_L):
                step(pool.tensor_scalar(w, n, part, None, ALU.mult))
                step(pool.tensor_tensor(th, th, w, ALU.subtract))
            step(pool.tensor_scalar(r, th, 1.0 / TWO_PI, None, ALU.mult))
            step(pool.tensor_scalar(fh, r, 4096.0, ROUND, ALU.mult, ALU.add))
            step(pool.tensor_scalar(fh, fh, ROUND, 1.0 / 4096, ALU.subtract, ALU.mult))
            step(pool.tensor_tensor(fl, r, fh, ALU.subtract), turn_parts)
            pool.wait_ge(s_small, 16 * 2)
            label_weights(0)
            pool.wait_ge(kh_copied, D * KT)
            pool.wait_ge(s_const, 16)
            key_blocks(0)
            probabilities(0, 0)
            probabilities(0, 1)
            pool.wait_ge(s_const_late, 16)
            value_blocks(0)
            label_weights(1)
            pool.wait_ge(rot_ready, 2)
            cs, sn = rot[:, 0, 1:2], rot[:, 1, 1:2]
            nr, ni, den, e, c2 = v(20), v(21), v(22), v(25), v(28)
            step(pool.tensor_tensor(nr, a, cs, ALU.mult))
            step(pool.tensor_scalar(nr, nr, 1.0, None, ALU.subtract))
            step(pool.tensor_tensor(ni, a, sn, ALU.mult))
            step(pool.tensor_tensor(den, lr, lr, ALU.mult))
            step(pool.tensor_tensor(e, li, li, ALU.mult))
            step(pool.tensor_tensor(den, den, e, ALU.add))
            step(pool.tensor_tensor(kr, nr, lr, ALU.mult))
            step(pool.tensor_tensor(e, ni, li, ALU.mult))
            step(pool.tensor_tensor(kr, kr, e, ALU.add))
            step(pool.tensor_tensor(ki, ni, lr, ALU.mult))
            step(pool.tensor_tensor(e, nr, li, ALU.mult))
            step(pool.tensor_tensor(ki, ki, e, ALU.subtract))
            step(pool.memset(c2, -1.0))
            step(pool.tensor_tensor(den, den, c2, ALU.pow))
            step(pool.tensor_tensor(kr, kr, den, ALU.mult))
            step(pool.tensor_tensor(ki, ki, den, ALU.mult))
            step(pool.tensor_tensor(kis, ki, sign, ALU.mult))
            step(pool.tensor_tensor(krs, kr, sign, ALU.mult))
            step(pool.tensor_scalar(krs, krs, -1.0, None, ALU.mult), b_scales)
            rstd_of(0, 0)
            key_blocks(1)
            value_blocks(1)
            pool.wait_ge(params_step, 4)
            take_s5_params(0)
            skip_term(0)
            pool.wait_ge(high, at["w2"])
            pool.tensor_tensor(w2_l[:], w2[:], f32(w2_h[:]), ALU.subtract).then_inc(low_mlp, 1)
            probabilities(1, 0)
            probabilities(1, 1)
            x_parts(2)
            rstd_of(0, 1)
            pool.wait_ge(params_step, 11)
            take_mlp_params(0)
            all_turns(pool, turn, turn_bc, turn_c)

        @block.scalar
        def _(act):
            def tokens_high(u):
                act.wait_ge(s_xT, 16 * u + 16)
                waited(act, feat_ready, u)
                act.activation(x_h[:], xT[:], ACT.Copy).then_inc(x_high, 1)

            def label_float(u):
                act.wait_ge(s_adj, 16 * u + 16)
                waited(act, label_sums, u)
                act.activation(weighed[:], adj[:], ACT.Copy).then_inc(label_floats, 1)

            def features_high(u):
                act.wait_ge(feat_ready, u + 1)
                act.activation(sf_h[:], bank(FEAT, KT, N), ACT.Copy).then_inc(feat_h, 1)

            def queries(u, d):
                act.wait_ge(q_ready, D * u + d + 1)
                for k in range(KT):
                    act.activation(qT[:, d, k], bank(ROWS + d, KT, N)[:, k], ACT.Identity,
                                   bias=bq[:, d * KT + k:d * KT + k + 1]).then_inc(q_copied, 1)

            def additive(u):
                act.wait_ge(addt_ready, u + 1)
                act.activation(addT[:], bank(PROB + 1, NT, P), ACT.Copy).then_inc(addt_copied, 1)

            def exponentials(u, t):
                act.wait_ge(shifted_s, NT * u + t + 1)
                act.activation(soft[:, t], soft[:, t], ACT.Exp).then_inc(exped, 1)

            def transposed(u, t):
                act.wait_ge(pt_ready, NT * u + t + 1)
                act.activation(pT[0:CR, t], ps[0:CR, PROB:PROB + D, 0:NC * P], ACT.Copy).then_inc(pt_copied, 1)

            def s5_input(u):
                act.wait_ge(lnt_ready[0], u + 1)
                act.wait_ge(cur_a_s, u + 1)
                for k in range(KT):
                    act.activation(uT[:, k], bank(B6, KT, N)[:, k], ACT.Identity, bias=cur_a[:, 2 + k:3 + k],
                                   scale=cur_a[:, k:k + 1]).then_inc(u_ready, 1)

            def mlp_input(u):
                act.wait_ge(lnt_ready[1], u + 1)
                act.wait_ge(cur_f_s, u + 1)
                waited(act, m_ls, KT * u)
                for k in range(KT):
                    act.activation(mt[:, k], bank(B6, KT, N)[:, k], ACT.Identity, bias=cur_f[:, 2 + k:3 + k],
                                   scale=cur_f[:, k:k + 1]).then_inc(m_ready, 1)

            def load_gelu_table(u):
                waited(act, gelu_table, u)
                act.activation(table_use[:], const[:, 0:1], ACT.Gelu_apprx_tanh).then_inc(gelu_table, 1)

            def gelus(u, q):
                if q == 0:
                    act.wait_ge(ff_ready, KT * (GIVEN + u))
                act.wait_ge(h_ready, FT // 2 * u + q + 1)
                for k in (2 * q, 2 * q + 1):
                    act.activation(gl[:, k], bank((PROB, B7)[q % 2], 2, N)[:, k % 2], ACT.Gelu_apprx_tanh,
                                   bias=b12[:, k:k + 1]).then_inc(gelu_s, 1)
                act.wait_ge(gelu_s, FT * u + 2 * q + 2)
                act.activation(gl_h[:, 2 * q:2 * q + 2], gl[:, 2 * q:2 * q + 2], ACT.Copy).then_inc(gl_hs, 1)

            def mlp_output(u):
                act.wait_ge(cur_g_s, u + 1)
                for k in range(KT):
                    act.wait_ge(ff_ready, KT * (GIVEN + u) + k + 1)
                    act.activation(ffT[:, k], ps[:, SCORE + k, 0:N], ACT.Identity, bias=cur_g[:, 2 + k:3 + k],
                                   scale=cur_g[:, k:k + 1]).then_inc(ff_copied, 1)

            def copy_values(b):
                act.wait_ge(vo_spread, b + 1)
                act.activation(vo_all[0:CR, b], ps[0:CR, B7, :], ACT.Copy).then_inc(vo_copied, 1)

            def keep_y2(u):
                act.wait_ge(y2_ready, u + 1)
                act.wait_ge(res_ready, GIVEN + u)
                act.activation(y2_kept[:], y2[:], ACT.Copy).then_inc(y2_copied, 1)

            def turn(un, ua, ub, uc):
                features_high(ua)
                gelus(uc, 0)
                gelus(uc, 1)
                queries(ua, 0)
                s5_input(ub)
                queries(ua, 1)
                gelus(uc, 2)
                additive(ua)
                keep_y2(uc)
                gelus(uc, 3)
                exponentials(ua, 0)
                if un is not None:
                    label_float(un)
                    tokens_high(un)
                exponentials(ua, 1)
                transposed(ua, 0)
                mlp_output(uc)
                transposed(ua, 1)
                mlp_input(ub)
                load_gelu_table(ub)

            def turn_bc(ub, uc):
                s5_input(ub)
                gelus(uc, 0)
                gelus(uc, 1)
                keep_y2(uc)
                gelus(uc, 2)
                gelus(uc, 3)
                mlp_input(ub)
                mlp_output(uc)

            def turn_c(uc):
                for q in range(FT // 2):
                    gelus(uc, q)
                keep_y2(uc)
                mlp_output(uc)

            def high_part(name):
                whole, part_h, _ = parts[name]
                act.wait_ge(loaded[name], 16)
                act.activation(part_h[:], whole[:], ACT.Copy).then_inc(high, 1)

            act.dma_start(wselfq[:], dram["wselfq"]).then_inc(s_wselfq, 16)
            act.dma_start(condT[:], dram["condT"]).then_inc(s_cond, 16)
            act.dma_start(rows[:], dram["rows"]).then_inc(s_rows, 16)
            act.dma_start(small[:], dram["small"]).then_inc(s_small, 16)
            act.dma_start(lbias[:], dram["lbias"].broadcast_to([P, L + 1])).then_inc(s_small, 16)
            high_part("wself")
            high_part("xkv")
            tokens_high(0)
            high_part("wk")
            act.dma_start(bri[:], dram["b_ri"]).then_inc(s_bri, 16)
            act.dma_start(cri[:], dram["c_ri"]).then_inc(s_cri, 16)
            act.wait_ge(skv_ready, 1)
            act.activation(skv_h[:], bank(SCORE, KT, KV), ACT.Copy).then_inc(skv_hs, 1)
            high_part("wq")
            label_float(0)
            features_high(0)
            act.wait_ge(s_small, 16 * 2)
            for d in range(D):
                act.wait_ge(kh_ready, d + 1)
                for k in range(KT):
                    act.activation(kh[:, d * KT + k], bank(SCORE + 1 + d, KT, KV)[:, k], ACT.Identity,
                                   bias=bk[:, d * KT + k:d * KT + k + 1]).then_inc(kh_copied, 1)
            high_part("wout")
            queries(0, 0)
            queries(0, 1)
            additive(0)
            exponentials(0, 0)
            exponentials(0, 1)
            for g in range(B // GB):
                act.wait_ge(vo_ready, g + 1)
                act.activation(vo_h[0:GR, g], ps[0:GR, VO[g], :], ACT.Copy).then_inc(vo_hs, 1)
            transposed(0, 0)
            copy_values(0)
            tokens_high(1)
            label_float(1)
            transposed(0, 1)
            act.wait_ge(turns, 2)
            for k in range(2):
                act.activation(rot[:, k], tb[4 + k], ACT.Sin, scale=SIN_SCALE).then_inc(rot_ready, 1)
            copy_values(1)
            features_high(1)
            high_part("w1")
            copy_values(2)
            queries(1, 0)
            queries(1, 1)
            additive(1)
            high_part("w2")
            copy_values(3)
            s5_input(0)
            act.wait_ge(bwt_ready, 1)
            act.activation(bwT[:].rearrange("p k s q -> p (k s q)"), ps[:, PROB, :], ACT.Copy).then_inc(bwt_copied, 1)
            exponentials(1, 0)
            copy_values(4)
            exponentials(1, 1)
            copy_values(5)
            label_float(2)
            tokens_high(2)
            transposed(1, 0)
            copy_values(6)
            transposed(1, 1)
            copy_values(7)
            mlp_input(0)
            load_gelu_table(0)
            all_turns(act, turn, turn_bc, turn_c)

        @block.tensor
        def _(pe):
            def three(out, wh, wl, xh, xl, first, last):
                pe.matmul(out, wh, xh, start=first, stop=False, skip_group_check=True)
                pe.matmul(out, wh, xl, start=False, stop=False, skip_group_check=True)
                return pe.matmul(out, wl, xh, start=False, stop=last, skip_group_check=True)

            def rowsums(u):
                pe.wait_ge(x_high, u + 1)
                pe.wait_ge(x_low, u + 1)
                waited(pe, q_copied, D * KT * u)
                for k in range(KT):
                    for part in (x_h, x_l):
                        last = pe.matmul(bank(ROWS, N), ones_r[:], part[:, k], start=k == 0 and part is x_h,
                                         stop=k == KT - 1 and part is x_l)
                last.then_inc(row_sums, 1)

            def features(u):
                waited(pe, y_ready, u)
                for f in range(KT):
                    for k in range(KT):
                        cols = slice(f * P, (f + 1) * P)
                        three(bank(FEAT, KT, N)[:, f], wself_h[:, k, cols], wself_l[:, k, cols], x_h[:, k], x_l[:, k],
                              f == 0 and k == 0, False)

            def condition_part(u):
                pe.wait_ge(nz_ready, u + 1)
                for f in range(KT):
                    last = pe.matmul(bank(FEAT, KT, N)[:, f], qw[:, f * P:(f + 1) * P], nz[:], start=False,
                                     stop=f == KT - 1, skip_group_check=True)
                last.then_inc(feat_ready, 1)

            def queries(u, d):
                if d == 0:
                    pe.wait_ge(feat_h, u + 1)
                    pe.wait_ge(feat_l, u + 1)
                for f in range(KT):
                    cols = slice(d * F + f * P, d * F + (f + 1) * P)
                    for k in range(KT):
                        last = three(bank(ROWS + d, KT, N)[:, f], wq_h[:, k, cols], wq_l[:, k, cols],
                                     sf_h[:, k], sf_l[:, k], k == 0, k == KT - 1)
                last.then_inc(q_ready, 1)

            def additive(u):
                pe.wait_ge(add_ready, 2 * u + 2)
                waited(pe, pt_copied, NT * u)
                for t in range(NT):
                    last = pe.transpose(bank(PROB + 1, NT, P)[:, t], addn[:, t].rearrange("p d m -> p (d m)"), ident)
                last.then_inc(addt_ready, 1)

            def scores(u, t):
                if t == 0:
                    pe.wait_ge(kbd_ready, u + 1)
                    pe.wait_ge(q_copied, D * KT * (u + 1))
                    pe.wait_ge(addt_copied, u + 1)
                rows_t = slice(t * P, (t + 1) * P)
                for d in range(D):
                    out = ps[:, (SCORE, ROWS)[t] + d, 0:HM]
                    pe.matmul(out, addT[:, t], rep_r[:, d], start=True, stop=False, skip_group_check=True)
                    for k in range(KT):
                        last = pe.matmul(out[:, k * HB * M:(k + 1) * HB * M], qT[:, d, k, rows_t],
                                         kbd[:, d * KT + k].rearrange("p h m -> p (h m)"), start=False,
                                         stop=k == KT - 1, skip_group_check=True)
                last.then_inc(scored, 1)

            def prob_transposes(u, t):
                pe.wait_ge(probs_ready, NT * u + t + 1)
                waited(pe, pt_copied, NT * u + t)
                if t == 0:
                    waited(pe, gelu_s, FT * (u - 1) - 2)
                for d in range(D):
                    rows_of = soft[:, t, d * H:(d + 1) * H].rearrange("p h m -> p (h m)")
                    for c, h in enumerate(CHUNK_HEAD):
                        last = pe.transpose(ps[0:CR, PROB + d, c * P:(c + 1) * P],
                                            rows_of[:, h * M:h * M + CR], ident)
                last.then_inc(pt_ready, 1)

            def own_features(u):
                pe.wait_ge(shifted_s, NT * u + NT)
                for t in range(NT):
                    rows_t = slice(t * P, (t + 1) * P)
                    for k in range(KT):
                        out = ps[:, FEAT, t * F + k * P:t * F + (k + 1) * P]
                        pe.matmul(out, sf_h[:, k, rows_t], ident_r[:], start=t == 0 and k == 0, stop=False,
                                  skip_group_check=True)
                        pe.matmul(out, sf_l[:, k, rows_t], ident_r[:], start=False, stop=False,
                                  skip_group_check=True)

            def attend(u, t):
                if t == 0:
                    pe.wait_ge(vbd_ready, u + 1)
                pe.wait_ge(pt_copied, NT * u + t + 1)
                for d in range(D):
                    for c, (lo, hi) in enumerate(CHUNK_COLS):
                        last = pe.matmul(ps[:, FEAT, t * F + lo:t * F + hi], pT[0:CR, t, d, c * P:(c + 1) * P],
                                         vbd[0:CR, d, lo:hi], start=False,
                                         stop=t == NT - 1 and d == D - 1 and c == NC - 1, skip_group_check=True)
                if t == NT - 1:
                    last.then_inc(attended, 1)

            def ln_transposes(u, n):
                if n == 0:
                    waited(pe, m_ready, KT * u)
                for t in range(NT):
                    pe.wait_ge(ln_s[n], NT * u + t + 1)
                    for k in range(KT):
                        last = pe.transpose(bank(B6, KT, N)[:, k, t * P:(t + 1) * P],
                                            ln[:, n, t, k * P:(k + 1) * P], ident)
                last.then_inc(lnt_ready[n], 1)

            def s5_in(u):
                pe.wait_ge(u_ready, KT * u + KT)
                for s in range(2):
                    for k in range(KT):
                        last = pe.matmul(bank(B6, 2, N)[:, s], bwT[:, k, s], uT[:, k], start=k == 0,
                                         stop=k == KT - 1)
                last.then_inc(bu_ready, 1)

            def s5_out(u):
                pe.wait_ge(cz_s, u + 1)
                for f in range(KT):
                    for s in range(2):
                        last = pe.matmul(bank(B6, KT, N)[:, f], cw[:, s, f * P:(f + 1) * P], cz[:, s],
                                         start=s == 0, stop=s == 1)
                last.then_inc(c_ready, 1)

            def s5_transposes(u):
                pe.wait_ge(a_ready, KT * (u + 1))
                for t in range(NT):
                    for k in range(KT):
                        last = pe.transpose(bank(B6, NT, F)[:, t, k * P:(k + 1) * P],
                                            aT[:, k, t * P:(t + 1) * P], ident)
                last.then_inc(at_ready, 1)

            def mlp_up(u, q):
                if q == 0:
                    pe.wait_ge(m_hs, KT * u + KT)
                    pe.wait_ge(m_ls, KT * u + KT)
                if q == 1:
                    pe.wait_ge(res_ready, GIVEN + u)
                if q >= 2:
                    pe.wait_ge(gelu_s, FT * u + 2 * q - 2)
                for j in range(2):
                    cols = slice((2 * q + j) * P, (2 * q + j + 1) * P)
                    for k in range(KT):
                        last = three(bank((PROB, B7)[q % 2], 2, N)[:, j], w1_h[:, k, cols],
                                     w1_l[:, k, cols], m_h[:, k], m_l[:, k], k == 0, k == KT - 1)
                last.then_inc(h_ready, 1)

            def mlp_down(u, q, ua):
                if q == 0 and ua is not None:
                    pe.wait_ge(shifted_s, NT * ua + 1)
                pe.wait_ge(gl_hs, FT // 2 * u + q + 1)
                pe.wait_ge(gl_ls, FT // 2 * u + q + 1)
                for f in range(KT):
                    cols = slice(f * P, (f + 1) * P)
                    for k in (2 * q, 2 * q + 1):
                        last = three(ps[:, SCORE + f, 0:N], w2_h[:, k, cols], w2_l[:, k, cols], gl_h[:, k],
                                     gl_l[:, k], k == 0, k == FT - 1)
                    if q == FT // 2 - 1:
                        last.then_inc(ff_ready, 1)

            def mlp_transposes(u):
                for k in range(KT):
                    pe.wait_ge(ff_copied, KT * (GIVEN + u) + k + 1)
                    for t in range(NT):
                        last = pe.transpose(bank(B7, NT, F)[:, t, k * P:(k + 1) * P],
                                            ffT[:, k, t * P:(t + 1) * P], ident)
                last.then_inc(fft_ready, 1)

            def spread(b):
                if b == 0:
                    pe.wait_ge(consts_r, 3)
                    pe.wait_ge(vo_hs, B // GB)
                    pe.wait_ge(vo_ls, B // GB)
                waited(pe, vo_copied, b)
                out = ps[0:CR, B7, :]
                pe.matmul(out, gsel_r[0:GR, b % GB], vo_h[0:GR, b // GB], start=True, stop=False)
                pe.matmul(out, gsel_r[0:GR, b % GB], vo_l[0:GR, b // GB], start=False, stop=True)\
                    .then_inc(vo_spread, 1)

            def turn(un, ua, ub, uc):
                rowsums(ua)
                features(ua)
                mlp_up(uc, 0)
                condition_part(ua)
                mlp_up(uc, 1)
                queries(ua, 0)
                queries(ua, 1)
                ln_transposes(ub, 0)
                mlp_up(uc, 2)
                additive(ua)
                s5_in(ub)
                mlp_up(uc, 3)
                scores(ua, 0)
                s5_out(ub)
                scores(ua, 1)
                s5_transposes(ub)
                mlp_down(uc, 0, ua)
                mlp_down(uc, 1, ua)
                own_features(ua)
                prob_transposes(ua, 0)
                mlp_down(uc, 2, ua)
                mlp_down(uc, 3, ua)
                prob_transposes(ua, 1)
                attend(ua, 0)
                ln_transposes(ub, 1)
                attend(ua, 1)
                mlp_transposes(uc)

            def turn_bc(ub, uc):
                mlp_up(uc, 0)
                ln_transposes(ub, 0)
                mlp_up(uc, 1)
                s5_in(ub)
                mlp_up(uc, 2)
                mlp_up(uc, 3)
                s5_out(ub)
                mlp_down(uc, 0, None)
                s5_transposes(ub)
                mlp_down(uc, 1, None)
                mlp_down(uc, 2, None)
                ln_transposes(ub, 1)
                mlp_down(uc, 3, None)
                mlp_transposes(uc)

            def turn_c(uc):
                for q in range(FT // 2):
                    mlp_up(uc, q)
                for q in range(FT // 2):
                    mlp_down(uc, q, None)
                mlp_transposes(uc)

            def modulations(tiles):
                for j in tiles:
                    h, col = divmod(j * P, NMOD // 2 * P)
                    for k in range(KT):
                        last = pe.matmul(bank((B6, SCORE + 1)[h], NMOD, B)[:, j], wmod[:, h * KT + k, col:col + P],
                                         condT[:, k, 0:B], start=k == 0, stop=k == KT - 1, skip_group_check=True)
                if j % (NMOD // 2) == NMOD // 2 - 1:
                    last.then_inc(mod_ready, 1)

            pe.wait_ge(cleared, 4)
            pe.wait_ge(s_cond, 16)
            pe.wait_ge(s_wselfq, 16)
            for k in range(KT):
                pe.matmul(bank(B6, F), condT[:, k], wselfq[:, k], start=k == 0, stop=False)
            pe.wait_ge(s_rows, 16)
            pe.wait_ge(s_const, 16)
            pe.matmul(bank(B6, F), const[0:1, C_ROW:C_ROW + P], rows[:, 0:F], start=False, stop=True)\
                .then_inc(cond_ready, 1)
            pe.wait_ge(high, at["xkv"])
            pe.wait_ge(low, at["xkv"])
            for k in range(KT):
                for part in (xkv_h, xkv_l):
                    last = pe.matmul(bank(B7, KV), ones_r[:], part[:, k], start=k == 0 and part is xkv_h,
                                     stop=k == KT - 1 and part is xkv_l)
            last.then_inc(kv_sums, 1)
            rowsums(0)
            for f in range(KT):
                out, cols = bank(SCORE, KT, KV)[:, f], slice(f * P, (f + 1) * P)
                for k in range(KT):
                    three(out, wself_h[:, k, cols], wself_l[:, k, cols], xkv_h[:, k], xkv_l[:, k], k == 0, False)
                if f == 0:
                    pe.wait_ge(qw_ready, 3)
                    pe.wait_ge(nzkv_ready, 4)
                last = pe.matmul(out, qw[:, cols], nzkv[:], start=False, stop=True, skip_group_check=True)
            last.then_inc(skv_ready, 1)
            features(0)
            condition_part(0)
            pe.wait_ge(high, at["wk"])
            pe.wait_ge(low, at["wk"])
            pe.wait_ge(skv_hs, 1)
            pe.wait_ge(skv_ls, 1)
            for d in range(D):
                for f in range(KT):
                    cols = slice(d * F + f * P, d * F + (f + 1) * P)
                    for k in range(KT):
                        last = three(bank(SCORE + 1 + d, KT, KV)[:, f], wk_h[:, k, cols], wk_l[:, k, cols],
                                     skv_h[:, k], skv_l[:, k], k == 0, k == KT - 1)
                last.then_inc(kh_ready, 1)
            pe.wait_ge(high, at["wq"])
            pe.wait_ge(low, at["wq"])
            queries(0, 0)
            queries(0, 1)
            additive(0)
            pe.wait_ge(s_wmod, 16)
            pe.wait_ge(qw_ready, 3)
            modulations(range(0, 2))
            pe.wait_ge(consts_r, 2)
            scores(0, 0)
            scores(0, 1)
            pe.wait_ge(high, at["wout"])
            pe.wait_ge(low, at["wout"])
            pe.wait_ge(kh_copied, D * KT)
            for g in range(B // GB):
                out, keys = ps[0:GR, VO[g], :], slice(g * GR, (g + 1) * GR)
                for k in range(KT):
                    three(out, skv_h[:, k, keys], skv_l[:, k, keys], wout_h[:, k], wout_l[:, k], k == 0, False)
                pe.matmul(out, const[0:1, C_ONE:C_ONE + GR], rows[:, F:F + D * F], start=False, stop=True,
                          skip_group_check=True).then_inc(vo_ready, 1)

            own_features(0)
            pe.wait_ge(vo_hs, 1)
            pe.wait_ge(vo_ls, 1)
            prob_transposes(0, 0)
            spread(0)
            modulations(range(2, NMOD // 2))
            prob_transposes(0, 1)
            attend(0, 0)
            attend(0, 1)
            spread(1)
            rowsums(1)
            features(1)
            condition_part(1)
            spread(2)
            queries(1, 0)
            queries(1, 1)
            additive(1)
            pe.wait_ge(mod_copied, 1)
            ln_transposes(0, 0)
            spread(3)
            scores(1, 0)
            pe.wait_ge(bw_ready, 2)
            pe.wait_ge(pt_copied, NT)
            for k in range(KT):
                for s in range(2):
                    last = pe.transpose(ps[:, PROB, (2 * k + s) * P:(2 * k + s + 1) * P], bw[:, s, k * P:(k + 1) * P],
                                        ident)
            last.then_inc(bwt_ready, 1)
            scores(1, 1)
            pe.wait_ge(bwt_copied, 1)
            s5_in(0)
            spread(4)
            pe.wait_ge(shifted_s, NT + 1)
            modulations(range(NMOD // 2, NMOD - 3))
            pe.wait_ge(cw_ready, 2)
            s5_out(0)
            spread(5)
            own_features(1)
            prob_transposes(1, 0)
            s5_transposes(0)
            modulations(range(NMOD - 3, NMOD))
            spread(6)
            prob_transposes(1, 1)
            attend(1, 0)
            spread(7)
            ln_transposes(0, 1)
            attend(1, 1)
            pe.wait_ge(vo_copied, B)
            pe.wait_ge(mod_copied, 2)
            pe.wait_ge(high, at["w2"])
            pe.wait_ge(low_mlp, 2)
            all_turns(pe, turn, turn_bc, turn_c)

        @block.vector
        def _(dve):
            def nonzero(u):
                dve.wait_ge(row_sums, u + 1)
                dve.tensor_scalar(nz[0:64], ps[0:64, ROWS, 0:N], 0.0, const[0:64, bass.ds(u + C_BSEL, 1)],
                                  ALU.not_equal, ALU.mult).then_inc(nz_ready, 1)

            def features_low(u):
                dve.wait_ge(feat_h, u + 1)
                dve.tensor_tensor(sf_l[:], bank(FEAT, KT, N), f32(sf_h[:]), ALU.subtract).then_inc(feat_l, 1)

            def label_counts(u):
                dve.wait_ge(s_adj, 16 * u + 16)
                dve.tensor_reduce(count[:], adj[:], AX_X, ALU.add).then_inc(counted, 1)

            def label_biases(u):
                dve.wait_ge(counted, u + 1)
                dve.tensor_scalar(masked[:], count[:], 0.0, NEG, ALU.is_le, ALU.mult).then_inc(label_add, 1)
                dve.wait_ge(label_weighed, u + 1)
                dve.tensor_reduce(vbias[:], weighed[:], AX_X, ALU.add).then_inc(label_sums, 1)
                dve.wait_ge(label_sums, u + 1)
                dve.wait_ge(label_add, 2 * u + 1)
                dve.scalar_tensor_tensor(out=addv[:].rearrange("p t d m -> p (t d m)"), in0=vbias[:],
                                         scalar=bbias[:], in1=masked[:], op0=ALU.add, op1=ALU.add)\
                    .then_inc(label_add, 1)
                dve.wait_ge(label_add, 2 * u + 2)
                waited(dve, addt_ready, u)
                dve.tensor_copy(addn[:, :, :, 0:M].bitcast(F32R), addv[:]).then_inc(add_ready, 1)
                dve.wait_ge(add_ready, 2 * u + 1)
                dve.tensor_tensor(addn[:, :, :, M:2 * M].bitcast(F32R), addv[:], addn[:, :, :, 0:M],
                                  ALU.subtract).then_inc(add_ready, 1)

            def shift(u, t):
                dve.wait_ge(scored, NT * u + t + 1)
                first = (SCORE, ROWS)[t]
                s = ps[:, first:first + D, 0:HM].rearrange("p d (h m) -> p d h m", m=M)
                dve.tensor_reduce(smax[:, t].rearrange("p (d h) -> p d h", d=D), s, AX_X, ALU.max).then_inc(maxed, 1)
                dve.wait_ge(maxed, NT * u + t + 1)
                dve.tensor_tensor(soft[:, t].rearrange("p (d h) m -> p d h m", d=D), s,
                                  smax[:, t].rearrange("p (d h) -> p d h", d=D).unsqueeze(3)
                                  .broadcast_to([P, D, H, M]), ALU.subtract).then_inc(shifted_s, 1)

            def sums(u, t):
                dve.wait_ge(exped, NT * u + t + 1)
                dve.tensor_reduce(ssum[:, t], soft[:, t], AX_X, ALU.add).then_inc(summed, 1)
                dve.wait_ge(summed, NT * u + t + 1)
                dve.reciprocal(srec[:, t], ssum[:, t]).then_inc(inverted, 1)

            def residual(u):
                dve.wait_ge(attended, u + 1)
                dve.wait_ge(s_x, 16 * u + 16)
                dve.scalar_tensor_tensor(out=y[:], in0=bank(FEAT, NT, F), scalar=0.0, in1=x[:], op0=ALU.max,
                                         op1=ALU.add).then_inc(y_ready, 1)

            def statistics(u, n):
                v = (y, y2)[n]
                dve.wait_ge((y_ready, y2_ready)[n], u + 1)
                for t in range(NT):
                    dve.bn_stats(st[:, n, t], v[:, t]).then_inc(stats_s[n], 1)

            def aggregate(u, n, op):
                dve.wait_ge(stats_s[n], NT * u + NT)
                op()
                for t in range(NT):
                    dve.bn_aggr(mv[:, n, t], st[:, n, t]).then_inc(mv_s[n], 1)

            def normalize(u, n):
                v = (y, y2)[n]
                dve.wait_ge(mrs_s[n], u + 1)
                for t in range(NT):
                    dve.tensor_scalar(ln[:, n, t], v[:, t], rstd[:, n, t:t + 1], mrs[:, n, t:t + 1],
                                      ALU.mult, ALU.subtract).then_inc(ln_s[n], 1)

            def scan(u):
                dve.wait_ge(bu_ready, u + 1)
                dve.tensor_tensor(bu[:], bank(B6, 2, N), rot[:], ALU.mult).then_inc(bu_turned, 1)
                dve.wait_ge(bu_turned, u + 1)
                dve.tensor_tensor(zin[:], bu[:, 0], bu[:, 1], ALU.add).then_inc(zin_s, 1)
                dve.wait_ge(zin_s, u + 1)
                dve.tensor_tensor_scan(z[:], sc[:, 1:2].broadcast_to([P, N]), zin[:], 0.0, ALU.mult, ALU.add)\
                    .then_inc(z_s, 1)
                dve.wait_ge(z_s, u + 1)
                dve.tensor_tensor(cz[:], z[:].unsqueeze(1).broadcast_to([P, 2, N]), rot[:], ALU.mult)\
                    .then_inc(cz_s, 1)

            def gated(u):
                dve.wait_ge(c_ready, u + 1)
                dve.wait_ge(gdu_ready, u + 1)
                for k in range(KT):
                    dve.scalar_tensor_tensor(out=aT[:, k], in0=bank(B6, KT, N)[:, k], scalar=cur_a[:, 4 + k:5 + k],
                                             in1=gdu[:, k], op0=ALU.mult, op1=ALU.add).then_inc(a_ready, 1)

            def s5_residual(u):
                dve.wait_ge(at_ready, u + 1)
                waited(dve, y2_copied, u)
                dve.tensor_tensor(y2[:], bank(B6, NT, F), y[:], ALU.add).then_inc(y2_ready, 1)

            def mlp_high(u):
                waited(dve, h_ready, FT // 2 * u)
                for k in range(KT):
                    dve.wait_ge(m_ready, KT * u + k + 1)
                    dve.tensor_copy(m_h[:, k], mt[:, k]).then_inc(m_hs, 1)

            def mlp_low(u):
                for k in range(KT):
                    dve.wait_ge(m_hs, KT * u + k + 1)
                    dve.tensor_tensor(m_l[:, k], mt[:, k], f32(m_h[:, k]), ALU.subtract).then_inc(m_ls, 1)

            def gelu_low(u, q):
                dve.wait_ge(gl_hs, FT // 2 * u + q + 1)
                two = slice(2 * q, 2 * q + 2)
                dve.tensor_tensor(gl_l[:, two], gl[:, two], f32(gl_h[:, two]), ALU.subtract).then_inc(gl_ls, 1)

            def result(u):
                dve.wait_ge(fft_ready, u + 1)
                dve.wait_ge(s_out, 16 * (GIVEN + u))
                dve.tensor_tensor(res[:], bank(B7, NT, F), y2_kept[:], ALU.add).then_inc(res_ready, 1)

            def turn(un, ua, ub, uc):
                nonzero(ua)
                statistics(ub, 0)
                aggregate(ub, 0, lambda: features_low(ua))
                gelu_low(uc, 0)
                normalize(ub, 0)
                label_biases(ua)
                gelu_low(uc, 1)
                scan(ub)
                gelu_low(uc, 2)
                shift(ua, 0)
                gated(ub)
                sums(ua, 0)
                shift(ua, 1)
                gelu_low(uc, 3)
                s5_residual(ub)
                statistics(ub, 1)
                aggregate(ub, 1, lambda: sums(ua, 1))
                normalize(ub, 1)
                if un is not None:
                    label_counts(un)
                if un is None:
                    mlp_high(ub)
                    mlp_low(ub)
                    residual(ua)
                    statistics(ua, 0)
                    aggregate(ua, 0, lambda: None)
                else:
                    residual(ua)
                    mlp_high(ub)
                    mlp_low(ub)
                result(uc)

            def turn_bc(ub, uc):
                normalize(ub, 0)
                gelu_low(uc, 0)
                scan(ub)
                gelu_low(uc, 1)
                gelu_low(uc, 2)
                gated(ub)
                gelu_low(uc, 3)
                s5_residual(ub)
                statistics(ub, 1)
                aggregate(ub, 1, lambda: None)
                normalize(ub, 1)
                mlp_high(ub)
                mlp_low(ub)
                result(uc)

            def turn_c(uc):
                for q in range(FT // 2):
                    gelu_low(uc, q)
                result(uc)

            def low_part(name):
                whole, part_h, part_l = parts[name]
                dve.wait_ge(high, at[name])
                dve.tensor_tensor(part_l[:], whole[:], f32(part_h[:]), ALU.subtract).then_inc(low, 1)

            low_part("wself")
            low_part("xkv")
            dve.wait_ge(x_high, 1)
            dve.tensor_tensor(x_l[:], xT[:], f32(x_h[:]), ALU.subtract).then_inc(x_low, 1)
            dve.wait_ge(cond_ready, 1)
            dve.tensor_copy(qw[:], bank(B6, F)).then_inc(qw_ready, 1)
            dve.wait_ge(qw_ready, 1)
            for r in (32, 96):
                dve.tensor_tensor(qw[r:r + 32], ps[r:r + 32, B6, 0:F], f32(qw[r:r + 32]), ALU.subtract)\
                    .then_inc(qw_ready, 1)
            bias_rows = const[64:P, C_BIASROW:C_BIASROW + 1]
            dve.wait_ge(s_const, 16)
            dve.tensor_copy(nz[64:P], bias_rows.broadcast_to([64, N])).then_inc(nzkv_ready, 1)
            dve.tensor_copy(nzkv[64:P], bias_rows.broadcast_to([64, KV])).then_inc(nzkv_ready, 1)
            dve.memset(f32(nz[0:64]), 0.0).then_inc(nzkv_ready, 1)
            dve.wait_ge(nzkv_ready, 3)
            dve.wait_ge(kv_sums, 1)
            dve.scalar_tensor_tensor(out=nzkv[0:64], in0=ps[0:64, B7, 0:KV], scalar=0.0,
                                     in1=const[0:64, C_KVSEL:C_KVSEL + KV], op0=ALU.not_equal, op1=ALU.mult)\
                .then_inc(nzkv_ready, 1)
            nonzero(0)
            low_part("wk")
            dve.wait_ge(skv_hs, 1)
            dve.tensor_tensor(skv_l[:], bank(SCORE, KT, KV), f32(skv_h[:]), ALU.subtract).then_inc(skv_ls, 1)
            low_part("wq")
            features_low(0)
            dve.tensor_copy(ident_r[:], ident).then_inc(consts_r, 1)
            label_counts(0)
            dve.wait_ge(s_const_late, 16)
            dve.tensor_copy(rep_r[:].rearrange("p d k -> p (d k)"), const[:, C_REP:C_REP + D * HM])\
                .then_inc(consts_r, 1)
            dve.wait_ge(s_small, 16 * 2)
            label_biases(0)
            low_part("wout")
            dve.tensor_copy(gsel_r[:].rearrange("p b k -> p (b k)"), const[:, C_GSEL:C_GSEL + GB * CR])\
                .then_inc(consts_r, 1)
            shift(0, 0)
            shift(0, 1)
            for g in range(B // GB):
                sums(0, g)
                dve.wait_ge(vo_hs, g + 1)
                dve.tensor_tensor(vo_l[0:GR, g], ps[0:GR, VO[g], :], f32(vo_h[0:GR, g]), ALU.subtract)\
                    .then_inc(vo_ls, 1)
            label_counts(1)
            step = stepper(dve, tables_step)
            dve.wait_ge(turn_parts, 1)
            time = const[:, C_TIME:C_TIME + N]
            T = lambda k: tb[k]
            step(dve.tensor_scalar(T(0), time, fh, None, ALU.mult))
            step(dve.tensor_scalar(T(1), T(0), ROUND, ROUND, ALU.add, ALU.subtract))
            step(dve.tensor_tensor(T(0), T(0), T(1), ALU.subtract))
            step(dve.tensor_scalar(T(2), time, fl, None, ALU.mult))
            step(dve.tensor_tensor(T(0), T(0), T(2), ALU.add))
            step(dve.tensor_scalar(T(3), T(0), 0.25, None, ALU.add))
            step(dve.tensor_scalar(T(1), T(0), ROUND, ROUND, ALU.add, ALU.subtract))
            step(dve.tensor_scalar(T(2), T(3), ROUND, ROUND, ALU.add, ALU.subtract))
            step(dve.tensor_tensor(T(4), T(3), T(2), ALU.subtract), turns)
            step(dve.tensor_tensor(T(5), T(0), T(1), ALU.subtract), turns)
            step = stepper(dve, params_step)

            def half_mod(k):
                dve.wait_ge(mod_ready, k + 1)
                half = slice(k * NMOD // 2, (k + 1) * NMOD // 2)
                dve.tensor_tensor(mod[:, half], bank((B6, SCORE + 1)[k], NMOD, B)[:, half],
                                  bmod[:, half].unsqueeze(2).broadcast_to([P, NMOD // 2, B]), ALU.add)\
                    .then_inc(mod_copied, 1)
                dve.wait_ge(mod_copied, k + 1)

            shift_a, scale_a, gate_a, shift_f, scale_f, gate_f, scale_c, shift_c = (
                mod[:, KT * j:KT * j + KT] for j in range(8))
            pa = [par_a[:, :, KT * j:KT * j + KT].rearrange("p b k -> p k b") for j in range(4)]
            pf = [par_f[:, :, KT * j:KT * j + KT].rearrange("p b k -> p k b") for j in range(4)]
            per_feature = lambda j: b12[:, j:j + KT].unsqueeze(2).broadcast_to([P, KT, B])
            half_mod(0)
            step(dve.tensor_scalar(pa[0], scale_a, 1.0, None, ALU.add))
            step(dve.tensor_copy(pa[1], shift_a))
            step(dve.tensor_copy(pa[2], gate_a))
            step(dve.tensor_tensor(pa[3], gate_a, per_feature(FT + KT), ALU.mult))
            dve.wait_ge(x_high, 2)
            dve.tensor_tensor(x_l[:], xT[:], f32(x_h[:]), ALU.subtract).then_inc(x_low, 1)
            residual(0)
            statistics(0, 0)
            aggregate(0, 0, lambda: None)
            nonzero(1)
            features_low(1)
            label_biases(1)
            normalize(0, 0)
            weight_step = stepper(dve, weights_step)
            dve.wait_ge(b_scales, 1)
            dve.wait_ge(s_bri, 16)
            weight_step(dve.tensor_scalar(bt[:, 0], bri[:, 0], kr, None, ALU.mult))
            weight_step(dve.tensor_scalar(bt[:, 1], bri[:, 1], kis, None, ALU.mult))
            weight_step(dve.tensor_tensor(bw[:, 0], bt[:, 0], bt[:, 1], ALU.add), bw_ready)
            weight_step(dve.tensor_scalar(bt[:, 2], bri[:, 0], ki, None, ALU.mult))
            weight_step(dve.tensor_scalar(bt[:, 1], bri[:, 1], krs, None, ALU.mult))
            weight_step(dve.tensor_tensor(bw[:, 1], bt[:, 2], bt[:, 1], ALU.add), bw_ready)
            dve.wait_ge(s_cri, 16)
            weight_step(dve.tensor_scalar(cw[:, 0], cri[:, 0], sign, -2.0, ALU.mult, ALU.mult), cw_ready)
            weight_step(dve.tensor_scalar(cw[:, 1], cri[:, 1], -2.0, None, ALU.mult), cw_ready)
            shift(1, 0)
            shift(1, 1)
            scan(0)
            sums(1, 0)
            sums(1, 1)
            gated(0)
            label_counts(2)
            s5_residual(0)
            statistics(0, 1)
            aggregate(0, 1, lambda: None)
            half_mod(1)
            step(dve.tensor_scalar(pt[:, 0], scale_f, 1.0, None, ALU.add))
            step(dve.tensor_scalar(pt[:, 1], scale_c, 1.0, None, ALU.add))
            step(dve.tensor_tensor(pf[0], pt[:, 0], pt[:, 1], ALU.mult))
            step(dve.tensor_tensor(pt[:, 2], shift_c, pt[:, 0], ALU.mult))
            step(dve.tensor_tensor(pf[1], pt[:, 2], shift_f, ALU.add))
            step(dve.tensor_copy(pf[2], gate_f))
            step(dve.tensor_tensor(pf[3], gate_f, per_feature(FT), ALU.mult))
            normalize(0, 1)
            dve.wait_ge(high, at["w1"])
            dve.tensor_tensor(w1_l[:], w1[:], f32(w1_h[:]), ALU.subtract).then_inc(low_mlp, 1)
            residual(1)
            mlp_high(0)
            mlp_low(0)
            all_turns(dve, turn, turn_bc, turn_c)


def kernel(x, cond_1024, mask_BxSxSx11_ik0, L0_cond_W_self, L0_cond_b_self, L0_cond_w_bias, L0_cond_b_bias,
           L0_cond_Wq, L0_cond_bq, L0_cond_Wk, L0_cond_bk, L0_cond_Wout, L0_cond_bout, L1_cond_Wm, L1_cond_bm,
           L1_cond_Lam_re, L1_cond_Lam_im, L1_cond_B_re, L1_cond_B_im, L1_cond_C_re, L1_cond_C_im,
           L1_cond_D_diag, L1_cond_log_step, L1_cond_Wc, L1_cond_bc, L1_cond_W1, L1_cond_b1, L1_cond_W2,
           L1_cond_b2):
    import concourse.bacc as bacc
    from concourse.bass_utils import run_bass_kernel_spmd

    def on_rows(a):
        a = np.asarray(a)
        return np.ascontiguousarray(a.reshape(a.shape[0] // P, P, -1).transpose(1, 0, 2))

    def columns(*vectors):
        return np.ascontiguousarray(np.concatenate([np.asarray(v).reshape(-1) for v in vectors]).reshape(-1, P).T)

    x = np.asarray(x)
    w_self = np.asarray(L0_cond_W_self)
    w_mod = np.concatenate([np.asarray(L1_cond_Wm), np.asarray(L1_cond_Wc)], axis=1)
    adj = np.asarray(mask_BxSxSx11_ik0)
    pairs = np.stack([adj[:, :, :M], adj[:, :M].transpose(0, 2, 1, 3)], axis=2)
    pairs = pairs.reshape(B, NT, P, D * M, L).transpose(0, 2, 1, 3, 4).reshape(B, P, NT * D * M, L)
    cond = np.zeros((P, KT, P), np.float32)
    cond[:, :, 0:B] = cond[:, :, 32:32 + B] = on_rows(np.asarray(cond_1024).T)

    def both_halves(re, im):
        return np.stack([np.concatenate([re, im]), np.concatenate([im, re])], axis=1)

    lam = np.stack([np.asarray(v) for v in (L1_cond_Lam_re, L1_cond_Lam_im, L1_cond_log_step)], axis=1)
    arrays = {
        "const": constants(),
        "x": x,
        "xT": np.ascontiguousarray(x.reshape(B, N, KT, P).transpose(0, 3, 2, 1)),
        "xkv": on_rows(x[:, :M].reshape(KV, F).T),
        "adj": np.ascontiguousarray(pairs),
        "wself": on_rows(w_self[:, :F].T),
        "wselfq": on_rows(w_self[:, F:].T),
        "condT": cond,
        "rows": np.concatenate([np.asarray(L0_cond_b_self), np.asarray(L0_cond_bout).reshape(-1)])[None],
        "lbias": np.concatenate([np.asarray(L0_cond_w_bias), np.asarray(L0_cond_b_bias).reshape(1)])[None],
        "wq": on_rows(np.asarray(L0_cond_Wq).reshape(D * F, F).T),
        "wk": on_rows(np.asarray(L0_cond_Wk).reshape(D * F, F).T),
        "wout": on_rows(np.asarray(L0_cond_Wout).reshape(D * F, F).T),
        "wmod": np.concatenate([on_rows(h) for h in np.split(w_mod, 2, axis=1)], axis=1).reshape(P, -1),
        "lam": np.concatenate([lam, lam]),
        "b_ri": both_halves(np.asarray(L1_cond_B_re), np.asarray(L1_cond_B_im)),
        "c_ri": both_halves(np.asarray(L1_cond_C_re).T, np.asarray(L1_cond_C_im).T),
        "w1": on_rows(L1_cond_W1),
        "w2": on_rows(L1_cond_W2),
        "small": columns(L0_cond_bq, L0_cond_bk, L1_cond_bm, L1_cond_bc, L1_cond_b1, L1_cond_b2, L1_cond_D_diag),
    }
    nc = bacc.Bacc("TRN2", target_bir_lowering=False, num_devices=1, dynamic_dma_scratch_size=1024)
    arrays = {f"in_{n}": np.ascontiguousarray(a) for n, a in arrays.items()}
    dram = {n[3:]: nc.dram_tensor(n, a.shape, mybir.dt.from_np(a.dtype), kind="ExternalInput").ap()
            for n, a in arrays.items()}
    dram["out"] = nc.dram_tensor("out", (B, N, F), F32, kind="ExternalOutput").ap()
    build(nc, dram)
    return run_bass_kernel_spmd(nc, [arrays], core_ids=[0]).results[0]["out"]
```
